# Optimizing a Trainium2 kernel written in Bass

```python
import numpy as np
import jax
import jax.numpy as jnp

def _softmax(x, axis=-1):
    return jax.nn.softmax(x, axis=axis)

def _gelu(x):
    return jax.nn.gelu(x, approximate=True)

def _silu(x):
    return jax.nn.silu(x)

def _sigmoid(x):
    return jax.nn.sigmoid(x)

def _layernorm(x, axis=-1, eps=1e-05):
    m = jnp.mean(x, axis=axis, keepdims=True)
    v = jnp.var(x, axis=axis, keepdims=True)
    return (x - m) / jnp.sqrt(v + eps)

def _scatter_add(tgt, idx, src, axis=0):
    return tgt.at[idx].add(src)

def _segment_sum(src, seg, n):
    return jax.ops.segment_sum(src, seg, n)
kernel_name = 'mk_recurrent_d2_jaxref_r8_777ed4'

def setup_inputs(seed: int=0):
    np.random.seed(seed)
    _w = jnp.asarray

    def _L0_attn_setup():
        import jax, jax.numpy as jnp
        import numpy as np
        B, S, H = (2, 512, 128)
        NKH, NVH, DK, DV = (8, 16, 64, 64)
        KEY_DIM = NKH * DK
        VAL_DIM = NVH * DV
        CONV_DIM = 2 * KEY_DIM + VAL_DIM
        KSZ = 4
        EPS = 1e-06

        def _forward(hidden_states, W_qkv, conv_w, W_z, W_b, W_a, dt_bias, A_log, norm_weight, W_out):
            b, s, _ = hidden_states.shape
            mixed = hidden_states @ W_qkv.T
            x = mixed.transpose(0, 2, 1)
            y = jax.lax.conv_general_dilated(x, conv_w, (1,), [(KSZ - 1, 0)], dimension_numbers=('NCH', 'OIH', 'NCH'), feature_group_count=CONV_DIM)
            mixed = jax.nn.silu(y).transpose(0, 2, 1)
            z = (hidden_states @ W_z.T).reshape(b, s, NVH, DV)
            beta = jax.nn.sigmoid(hidden_states @ W_b.T)
            a = hidden_states @ W_a.T
            g = -jnp.exp(A_log) * jax.nn.softplus(a + dt_bias)
            q, k, v = jnp.split(mixed, [KEY_DIM, 2 * KEY_DIM], axis=-1)
            q = q.reshape(b, s, NKH, DK)
            k = k.reshape(b, s, NKH, DK)
            v = v.reshape(b, s, NVH, DV)
            rep = NVH // NKH
            if rep > 1:
                q = jnp.repeat(q, rep, axis=2)
                k = jnp.repeat(k, rep, axis=2)
            q = q * DK ** (-0.5)

            def step(Sst, inp):
                q_t, k_t, v_t, g_t, b_t = inp
                Sst = Sst * jnp.exp(g_t)[..., None, None]
                kv = jnp.einsum('bhkv,bhk->bhv', Sst, k_t)
                delta = (v_t - kv) * b_t[..., None]
                Sst = Sst + k_t[..., None] * delta[..., None, :]
                o = jnp.einsum('bhkv,bhk->bhv', Sst, q_t)
                return (Sst, o)
            S0 = jnp.zeros((b, NVH, DK, DV), jnp.float32)
            xs = (q.transpose(1, 0, 2, 3), k.transpose(1, 0, 2, 3), v.transpose(1, 0, 2, 3), g.transpose(1, 0, 2), beta.transpose(1, 0, 2))
            _, o = jax.lax.scan(step, S0, xs)
            o = o.transpose(1, 0, 2, 3)
            h_ = o * jax.nn.silu(z)
            var = jnp.mean(h_ * h_, axis=-1, keepdims=True)
            h_ = h_ * jax.lax.rsqrt(var + EPS) * norm_weight
            return h_.reshape(b, s, VAL_DIM) @ W_out.T
        key = jax.random.key(seed)
        ks = jax.random.split(key, 8)
        s = 0.02
        return {'hidden_states': jax.random.normal(ks[0], (B, S, H), jnp.float32), 'W_qkv': jax.random.normal(ks[1], (CONV_DIM, H), jnp.float32) * s, 'conv_w': jax.random.normal(ks[2], (CONV_DIM, 1, KSZ), jnp.float32) * 0.1, 'W_z': jax.random.normal(ks[3], (VAL_DIM, H), jnp.float32) * s, 'W_b': jax.random.normal(ks[4], (NVH, H), jnp.float32) * s, 'W_a': jax.random.normal(ks[5], (NVH, H), jnp.float32) * s, 'dt_bias': jnp.ones((NVH,), jnp.float32), 'A_log': jnp.log(jax.random.uniform(ks[6], (NVH,), jnp.float32, 0.1, 16.0)), 'norm_weight': jnp.ones((DV,), jnp.float32), 'W_out': jax.random.normal(ks[7], (H, VAL_DIM), jnp.float32) * s}
    _L0_attn_in = _L0_attn_setup()

    def _L0_ffn_setup():
        import jax, jax.numpy as jnp
        import numpy as np
        B, S, H, F, E, K = (2, 256, 128, 512, 8, 2)

        def _ln(x, g, b, eps=1e-05):
            m = jnp.mean(x, axis=-1, keepdims=True)
            v = jnp.var(x, axis=-1, keepdims=True)
            return (x - m) / jnp.sqrt(v + eps) * g + b

        def _gelu(x):
            return jax.nn.gelu(x, approximate=False)
        key = jax.random.key(seed)
        ks = jax.random.split(key, 12)
        F2 = F // 2
        return {'hidden_states': jax.random.normal(ks[0], (B, S, H), jnp.float32), 'ln_g': jnp.ones((H,), jnp.float32), 'ln_b': jnp.zeros((H,), jnp.float32), 'router_w': jax.random.normal(ks[1], (H, E), jnp.float32) * 0.01, 'up_W': jax.random.normal(ks[2], (E, H, F), jnp.float32) * 0.02, 'up_b': jnp.zeros((E, F), jnp.float32), 'down_W': jax.random.normal(ks[3], (E, F, H), jnp.float32) * 0.02, 'down_b': jnp.zeros((E, H), jnp.float32), 'spec0_W': jax.random.normal(ks[4], (2, F, F), jnp.float32) * 0.02, 'spec0_b': jnp.zeros((2, F), jnp.float32), 'ln0_g': jnp.ones((2, F), jnp.float32), 'ln0_b': jnp.zeros((2, F), jnp.float32), 'spec1a_W': jax.random.normal(ks[5], (2, F, F2), jnp.float32) * 0.02, 'spec1a_b': jnp.zeros((2, F2), jnp.float32), 'spec1b_W': jax.random.normal(ks[6], (2, F2, F), jnp.float32) * 0.02, 'spec1b_b': jnp.zeros((2, F), jnp.float32), 'ln1_g': jnp.ones((2, F), jnp.float32), 'ln1_b': jnp.zeros((2, F), jnp.float32), 'spec2_W': jax.random.normal(ks[7], (2, F, F), jnp.float32) * 0.02, 'spec2_b': jnp.zeros((2, F), jnp.float32)}
    _L0_ffn_in = _L0_ffn_setup()

    def _L1_attn_setup():
        import jax, jax.numpy as jnp
        import numpy as np
        D_MODEL = 128
        N_HEADS = 16
        D_FF = 512
        D_STATE = 16
        D_CONV = 4
        EXPAND = 2
        D_INNER = D_MODEL * EXPAND
        DT_RANK = D_MODEL // 16
        BATCH = 4
        SEQ = 128

        def _ln(x, w, b):
            m = jnp.mean(x, axis=-1, keepdims=True)
            v = jnp.var(x, axis=-1, keepdims=True)
            return (x - m) / jnp.sqrt(v + 1e-05) * w + b
        key = jax.random.key(seed)
        ks = jax.random.split(key, 32)
        s = 0.02
        inp = {}
        inp['x'] = jax.random.normal(ks[0], (BATCH, SEQ, D_MODEL), jnp.float32)
        inp['ln1_w'] = jnp.ones((D_MODEL,), jnp.float32)
        inp['ln1_b'] = jnp.zeros((D_MODEL,), jnp.float32)
        inp['ln2_w'] = jnp.ones((D_MODEL,), jnp.float32)
        inp['ln2_b'] = jnp.zeros((D_MODEL,), jnp.float32)
        inp['q_w'] = jax.random.normal(ks[1], (D_MODEL, D_MODEL), jnp.float32) * s
        inp['q_b'] = jnp.zeros((D_MODEL,), jnp.float32)
        inp['k_w'] = jax.random.normal(ks[2], (D_MODEL, D_MODEL), jnp.float32) * s
        inp['k_b'] = jnp.zeros((D_MODEL,), jnp.float32)
        inp['v_w'] = jax.random.normal(ks[3], (D_MODEL, D_MODEL), jnp.float32) * s
        inp['v_b'] = jnp.zeros((D_MODEL,), jnp.float32)
        inp['o_w'] = jax.random.normal(ks[4], (D_MODEL, D_MODEL), jnp.float32) * s
        inp['o_b'] = jnp.zeros((D_MODEL,), jnp.float32)
        inp['in_proj_w'] = jax.random.normal(ks[5], (D_MODEL, 2 * D_INNER), jnp.float32) * s
        inp['conv_w'] = jax.random.normal(ks[6], (D_INNER, D_CONV), jnp.float32) * 0.2
        inp['conv_b'] = jnp.zeros((D_INNER,), jnp.float32)
        inp['x_proj_w'] = jax.random.normal(ks[7], (D_INNER, DT_RANK + 2 * D_STATE), jnp.float32) * s
        dt_std = DT_RANK ** (-0.5)
        inp['dt_w'] = jax.random.uniform(ks[8], (DT_RANK, D_INNER), jnp.float32, -dt_std, dt_std)
        dt = jnp.exp(jax.random.uniform(ks[9], (D_INNER,), jnp.float32) * (np.log(0.1) - np.log(0.001)) + np.log(0.001))
        inp['dt_b'] = dt + jnp.log(-jnp.expm1(-dt))
        A = jnp.tile(jnp.arange(1, D_STATE + 1, dtype=jnp.float32), (D_INNER, 1))
        inp['A_log'] = jnp.log(A)
        inp['D_param'] = jnp.ones((D_INNER,), jnp.float32)
        inp['ssm_out_w'] = jax.random.normal(ks[10], (D_INNER, D_MODEL), jnp.float32) * s
        inp['mix_weight'] = jnp.full((D_MODEL,), 0.5, jnp.float32)
        inp['ffn_w1'] = jax.random.normal(ks[11], (D_MODEL, D_FF), jnp.float32) * s
        inp['ffn_b1'] = jnp.zeros((D_FF,), jnp.float32)
        inp['ffn_w2'] = jax.random.normal(ks[12], (D_FF, D_MODEL), jnp.float32) * s
        inp['ffn_b2'] = jnp.zeros((D_MODEL,), jnp.float32)
        return inp
    _L1_attn_in = _L1_attn_setup()

    def _L1_ffn_setup():
        import jax, jax.numpy as jnp
        import numpy as np
        LN_EPS = 1e-05

        def layer_norm(x, g, b):
            mu = jnp.mean(x, axis=-1, keepdims=True)
            var = jnp.var(x, axis=-1, keepdims=True)
            return (x - mu) / jnp.sqrt(var + LN_EPS) * g + b

        def balanced_assignment(scores):
            T, E = scores.shape
            C = T // E
            taken = jnp.zeros((T,), dtype=bool)
            parts = []
            for e in range(E):
                s = jnp.where(taken, -jnp.inf, scores[:, e])
                _, idx = jax.lax.top_k(s, C)
                parts.append(idx)
                taken = taken.at[idx].set(True)
            return jnp.concatenate(parts)
        key = jax.random.key(seed)
        ks = jax.random.split(key, 4)
        B, S, D, F, E = (4, 256, 128, 512, 8)
        return {'x': jax.random.normal(ks[0], (B, S, D), dtype=jnp.float32), 'centroids': jax.random.normal(ks[1], (E, D), dtype=jnp.float32) * 0.1, 'ln_g': jnp.ones((D,), dtype=jnp.float32), 'ln_b': jnp.zeros((D,), dtype=jnp.float32), 'w1': jax.random.normal(ks[2], (E, D, F), dtype=jnp.float32) * 0.02, 'b1': jnp.zeros((E, F), dtype=jnp.float32), 'w2': jax.random.normal(ks[3], (E, F, D), dtype=jnp.float32) * 0.02, 'b2': jnp.zeros((E, D), dtype=jnp.float32)}
    _L1_ffn_in = _L1_ffn_setup()
    _d = {'L0_attn_hidden_states': _L0_attn_in['hidden_states'], 'L0_attn_W_qkv': _L0_attn_in['W_qkv'], 'L0_attn_conv_w': _L0_attn_in['conv_w'], 'L0_attn_W_z': _L0_attn_in['W_z'], 'L0_attn_W_b': _L0_attn_in['W_b'], 'L0_attn_W_a': _L0_attn_in['W_a'], 'L0_attn_dt_bias': _L0_attn_in['dt_bias'], 'L0_attn_A_log': _L0_attn_in['A_log'], 'L0_attn_norm_weight': _L0_attn_in['norm_weight'], 'L0_attn_W_out': _L0_attn_in['W_out'], 'L0_ffn_ln_g': _L0_ffn_in['ln_g'], 'L0_ffn_ln_b': _L0_ffn_in['ln_b'], 'L0_ffn_router_w': _L0_ffn_in['router_w'], 'L0_ffn_up_W': _L0_ffn_in['up_W'], 'L0_ffn_up_b': _L0_ffn_in['up_b'], 'L0_ffn_down_W': _L0_ffn_in['down_W'], 'L0_ffn_down_b': _L0_ffn_in['down_b'], 'L0_ffn_spec0_W': _L0_ffn_in['spec0_W'], 'L0_ffn_spec0_b': _L0_ffn_in['spec0_b'], 'L0_ffn_ln0_g': _L0_ffn_in['ln0_g'], 'L0_ffn_ln0_b': _L0_ffn_in['ln0_b'], 'L0_ffn_spec1a_W': _L0_ffn_in['spec1a_W'], 'L0_ffn_spec1a_b': _L0_ffn_in['spec1a_b'], 'L0_ffn_spec1b_W': _L0_ffn_in['spec1b_W'], 'L0_ffn_spec1b_b': _L0_ffn_in['spec1b_b'], 'L0_ffn_ln1_g': _L0_ffn_in['ln1_g'], 'L0_ffn_ln1_b': _L0_ffn_in['ln1_b'], 'L0_ffn_spec2_W': _L0_ffn_in['spec2_W'], 'L0_ffn_spec2_b': _L0_ffn_in['spec2_b'], 'L1_attn_ln1_w': _L1_attn_in['ln1_w'], 'L1_attn_ln1_b': _L1_attn_in['ln1_b'], 'L1_attn_ln2_w': _L1_attn_in['ln2_w'], 'L1_attn_ln2_b': _L1_attn_in['ln2_b'], 'L1_attn_q_w': _L1_attn_in['q_w'], 'L1_attn_q_b': _L1_attn_in['q_b'], 'L1_attn_k_w': _L1_attn_in['k_w'], 'L1_attn_k_b': _L1_attn_in['k_b'], 'L1_attn_v_w': _L1_attn_in['v_w'], 'L1_attn_v_b': _L1_attn_in['v_b'], 'L1_attn_o_w': _L1_attn_in['o_w'], 'L1_attn_o_b': _L1_attn_in['o_b'], 'L1_attn_in_proj_w': _L1_attn_in['in_proj_w'], 'L1_attn_conv_w': _L1_attn_in['conv_w'], 'L1_attn_conv_b': _L1_attn_in['conv_b'], 'L1_attn_x_proj_w': _L1_attn_in['x_proj_w'], 'L1_attn_dt_w': _L1_attn_in['dt_w'], 'L1_attn_dt_b': _L1_attn_in['dt_b'], 'L1_attn_A_log': _L1_attn_in['A_log'], 'L1_attn_D_param': _L1_attn_in['D_param'], 'L1_attn_ssm_out_w': _L1_attn_in['ssm_out_w'], 'L1_attn_mix_weight': _L1_attn_in['mix_weight'], 'L1_attn_ffn_w1': _L1_attn_in['ffn_w1'], 'L1_attn_ffn_b1': _L1_attn_in['ffn_b1'], 'L1_attn_ffn_w2': _L1_attn_in['ffn_w2'], 'L1_attn_ffn_b2': _L1_attn_in['ffn_b2'], 'L1_ffn_centroids': _L1_ffn_in['centroids'], 'L1_ffn_ln_g': _L1_ffn_in['ln_g'], 'L1_ffn_ln_b': _L1_ffn_in['ln_b'], 'L1_ffn_w1': _L1_ffn_in['w1'], 'L1_ffn_b1': _L1_ffn_in['b1'], 'L1_ffn_w2': _L1_ffn_in['w2'], 'L1_ffn_b2': _L1_ffn_in['b2']}
    _x0 = _d['L0_attn_hidden_states']
    _d['L0_attn_hidden_states'] = jax.random.normal(jax.random.fold_in(jax.random.key(seed), 1), (8, 512, 128), dtype=_x0.dtype)
    del _x0
    return _d

def reference(L0_attn_hidden_states, L0_attn_W_qkv, L0_attn_conv_w, L0_attn_W_z, L0_attn_W_b, L0_attn_W_a, L0_attn_dt_bias, L0_attn_A_log, L0_attn_norm_weight, L0_attn_W_out, L0_ffn_ln_g, L0_ffn_ln_b, L0_ffn_router_w, L0_ffn_up_W, L0_ffn_up_b, L0_ffn_down_W, L0_ffn_down_b, L0_ffn_spec0_W, L0_ffn_spec0_b, L0_ffn_ln0_g, L0_ffn_ln0_b, L0_ffn_spec1a_W, L0_ffn_spec1a_b, L0_ffn_spec1b_W, L0_ffn_spec1b_b, L0_ffn_ln1_g, L0_ffn_ln1_b, L0_ffn_spec2_W, L0_ffn_spec2_b, L1_attn_ln1_w, L1_attn_ln1_b, L1_attn_ln2_w, L1_attn_ln2_b, L1_attn_q_w, L1_attn_q_b, L1_attn_k_w, L1_attn_k_b, L1_attn_v_w, L1_attn_v_b, L1_attn_o_w, L1_attn_o_b, L1_attn_in_proj_w, L1_attn_conv_w, L1_attn_conv_b, L1_attn_x_proj_w, L1_attn_dt_w, L1_attn_dt_b, L1_attn_A_log, L1_attn_D_param, L1_attn_ssm_out_w, L1_attn_mix_weight, L1_attn_ffn_w1, L1_attn_ffn_b1, L1_attn_ffn_w2, L1_attn_ffn_b2, L1_ffn_centroids, L1_ffn_ln_g, L1_ffn_ln_b, L1_ffn_w1, L1_ffn_b1, L1_ffn_w2, L1_ffn_b2):

    def _L0_attn_ref(hidden_states, W_qkv, conv_w, W_z, W_b, W_a, dt_bias, A_log, norm_weight, W_out):
        import jax, jax.numpy as jnp
        import numpy as np
        B, S, H = (2, 512, 128)
        NKH, NVH, DK, DV = (8, 16, 64, 64)
        KEY_DIM = NKH * DK
        VAL_DIM = NVH * DV
        CONV_DIM = 2 * KEY_DIM + VAL_DIM
        KSZ = 4
        EPS = 1e-06

        def _forward(hidden_states, W_qkv, conv_w, W_z, W_b, W_a, dt_bias, A_log, norm_weight, W_out):
            b, s, _ = hidden_states.shape
            mixed = hidden_states @ W_qkv.T
            x = mixed.transpose(0, 2, 1)
            y = jax.lax.conv_general_dilated(x, conv_w, (1,), [(KSZ - 1, 0)], dimension_numbers=('NCH', 'OIH', 'NCH'), feature_group_count=CONV_DIM)
            mixed = jax.nn.silu(y).transpose(0, 2, 1)
            z = (hidden_states @ W_z.T).reshape(b, s, NVH, DV)
            beta = jax.nn.sigmoid(hidden_states @ W_b.T)
            a = hidden_states @ W_a.T
            g = -jnp.exp(A_log) * jax.nn.softplus(a + dt_bias)
            q, k, v = jnp.split(mixed, [KEY_DIM, 2 * KEY_DIM], axis=-1)
            q = q.reshape(b, s, NKH, DK)
            k = k.reshape(b, s, NKH, DK)
            v = v.reshape(b, s, NVH, DV)
            rep = NVH // NKH
            if rep > 1:
                q = jnp.repeat(q, rep, axis=2)
                k = jnp.repeat(k, rep, axis=2)
            q = q * DK ** (-0.5)

            def step(Sst, inp):
                q_t, k_t, v_t, g_t, b_t = inp
                Sst = Sst * jnp.exp(g_t)[..., None, None]
                kv = jnp.einsum('bhkv,bhk->bhv', Sst, k_t)
                delta = (v_t - kv) * b_t[..., None]
                Sst = Sst + k_t[..., None] * delta[..., None, :]
                o = jnp.einsum('bhkv,bhk->bhv', Sst, q_t)
                return (Sst, o)
            S0 = jnp.zeros((b, NVH, DK, DV), jnp.float32)
            xs = (q.transpose(1, 0, 2, 3), k.transpose(1, 0, 2, 3), v.transpose(1, 0, 2, 3), g.transpose(1, 0, 2), beta.transpose(1, 0, 2))
            _, o = jax.lax.scan(step, S0, xs)
            o = o.transpose(1, 0, 2, 3)
            h_ = o * jax.nn.silu(z)
            var = jnp.mean(h_ * h_, axis=-1, keepdims=True)
            h_ = h_ * jax.lax.rsqrt(var + EPS) * norm_weight
            return h_.reshape(b, s, VAL_DIM) @ W_out.T
        return _forward(hidden_states, W_qkv, conv_w, W_z, W_b, W_a, dt_bias, A_log, norm_weight, W_out)

    def _L0_ffn_ref(hidden_states, ln_g, ln_b, router_w, up_W, up_b, down_W, down_b, spec0_W, spec0_b, ln0_g, ln0_b, spec1a_W, spec1a_b, spec1b_W, spec1b_b, ln1_g, ln1_b, spec2_W, spec2_b):
        import jax, jax.numpy as jnp
        import numpy as np
        B, S, H, F, E, K = (2, 256, 128, 512, 8, 2)

        def _ln(x, g, b, eps=1e-05):
            m = jnp.mean(x, axis=-1, keepdims=True)
            v = jnp.var(x, axis=-1, keepdims=True)
            return (x - m) / jnp.sqrt(v + eps) * g + b

        def _gelu(x):
            return jax.nn.gelu(x, approximate=False)
        b, s, h = hidden_states.shape
        x = hidden_states.reshape(-1, h)
        nx = _ln(x, ln_g, ln_b)
        logits = nx @ router_w
        probs = jax.nn.softmax(logits, axis=-1)
        _, idx = jax.lax.top_k(probs, K)
        mask = jnp.sum(jax.nn.one_hot(idx, probs.shape[-1], dtype=probs.dtype), axis=1)
        w = probs * mask
        w = w / jnp.sum(w, axis=-1, keepdims=True)
        h1 = _gelu(jnp.einsum('th,ehf->etf', nx, up_W) + up_b[:, None, :])
        i0 = jnp.array([0, 4])
        i1 = jnp.array([1, 5])
        i2 = jnp.array([2, 6])
        s0 = _gelu(_ln(jnp.einsum('etf,efg->etg', h1[i0], spec0_W) + spec0_b[:, None, :], ln0_g[:, None, :], ln0_b[:, None, :]))
        t1 = _gelu(jnp.einsum('etf,efg->etg', h1[i1], spec1a_W) + spec1a_b[:, None, :])
        s1 = _ln(jnp.einsum('etg,egf->etf', t1, spec1b_W) + spec1b_b[:, None, :], ln1_g[:, None, :], ln1_b[:, None, :])
        s2 = _gelu(jnp.einsum('etf,efg->etg', h1[i2], spec2_W) + spec2_b[:, None, :])
        h2 = h1.at[i0].set(s0).at[i1].set(s1).at[i2].set(s2)
        out_e = jnp.einsum('etf,efh->eth', h2, down_W) + down_b[:, None, :]
        y = jnp.einsum('eth,te->th', out_e, w) + x
        return y.reshape(hidden_states.shape)

    def _L1_attn_ref(x, ln1_w, ln1_b, ln2_w, ln2_b, q_w, q_b, k_w, k_b, v_w, v_b, o_w, o_b, in_proj_w, conv_w, conv_b, x_proj_w, dt_w, dt_b, A_log, D_param, ssm_out_w, mix_weight, ffn_w1, ffn_b1, ffn_w2, ffn_b2):
        import jax, jax.numpy as jnp
        import numpy as np
        D_MODEL = 128
        N_HEADS = 16
        D_FF = 512
        D_STATE = 16
        D_CONV = 4
        EXPAND = 2
        D_INNER = D_MODEL * EXPAND
        DT_RANK = D_MODEL // 16
        BATCH = 4
        SEQ = 128

        def _ln(x, w, b):
            m = jnp.mean(x, axis=-1, keepdims=True)
            v = jnp.var(x, axis=-1, keepdims=True)
            return (x - m) / jnp.sqrt(v + 1e-05) * w + b
        B, L, Dm = x.shape
        H = N_HEADS
        hd = Dm // H
        xn = _ln(x, ln1_w, ln1_b)
        q = (xn @ q_w + q_b).reshape(B, L, H, hd)
        k = (xn @ k_w + k_b).reshape(B, L, H, hd)
        v = (xn @ v_w + v_b).reshape(B, L, H, hd)
        scores = jnp.einsum('bqhd,bkhd->bhqk', q, k) * hd ** (-0.5)
        causal = jnp.tril(jnp.ones((L, L), bool))
        scores = jnp.where(causal[None, None], scores, -jnp.inf)
        attn = jax.nn.softmax(scores, axis=-1)
        attn_out = jnp.einsum('bhqk,bkhd->bqhd', attn, v).reshape(B, L, Dm) @ o_w + o_b
        xz = xn @ in_proj_w
        Di = xz.shape[-1] // 2
        x_ssm, z = (xz[..., :Di], xz[..., Di:])
        K = conv_w.shape[1]
        xp = jnp.pad(x_ssm, ((0, 0), (K - 1, 0), (0, 0)))
        x_c = sum((xp[:, j:j + L, :] * conv_w[:, j] for j in range(K))) + conv_b
        x_c = jax.nn.silu(x_c)
        x_dbc = x_c @ x_proj_w
        R = dt_w.shape[0]
        N = A_log.shape[1]
        dt = jax.nn.softplus(x_dbc[..., :R] @ dt_w + dt_b)
        Bm = x_dbc[..., R:R + N]
        Cm = x_dbc[..., R + N:]
        A = -jnp.exp(A_log)

        def step(h, inp):
            xt, dtt, Bt, Ct = inp
            h = jnp.exp(dtt[..., None] * A) * h + (xt * dtt)[..., None] * Bt[:, None, :]
            y = jnp.einsum('bn,bdn->bd', Ct, h)
            return (h, y)
        h0 = jnp.zeros((B, Di, N), x.dtype)
        _, ys = jax.lax.scan(step, h0, (x_c.swapaxes(0, 1), dt.swapaxes(0, 1), Bm.swapaxes(0, 1), Cm.swapaxes(0, 1)))
        y = ys.swapaxes(0, 1)
        y = (y + x_c * D_param) * jax.nn.silu(z)
        ssm_out = y @ ssm_out_w
        alpha = jax.nn.sigmoid(mix_weight)
        x = x + alpha * attn_out + (1.0 - alpha) * ssm_out
        h2 = _ln(x, ln2_w, ln2_b)
        ffn = jax.nn.gelu(h2 @ ffn_w1 + ffn_b1, approximate=False) @ ffn_w2 + ffn_b2
        return x + ffn

    def _L1_ffn_ref(x, centroids, ln_g, ln_b, w1, b1, w2, b2):
        import jax, jax.numpy as jnp
        import numpy as np
        LN_EPS = 1e-05

        def layer_norm(x, g, b):
            mu = jnp.mean(x, axis=-1, keepdims=True)
            var = jnp.var(x, axis=-1, keepdims=True)
            return (x - mu) / jnp.sqrt(var + LN_EPS) * g + b

        def balanced_assignment(scores):
            T, E = scores.shape
            C = T // E
            taken = jnp.zeros((T,), dtype=bool)
            parts = []
            for e in range(E):
                s = jnp.where(taken, -jnp.inf, scores[:, e])
                _, idx = jax.lax.top_k(s, C)
                parts.append(idx)
                taken = taken.at[idx].set(True)
            return jnp.concatenate(parts)
        D = x.shape[-1]
        feat = x.reshape(-1, D)
        T = feat.shape[0]
        E = centroids.shape[0]
        C = T // E
        norm = layer_norm(feat, ln_g, ln_b)
        scores = jax.lax.stop_gradient(norm @ centroids.T)
        sort_by_expert = balanced_assignment(scores)
        routed = feat[sort_by_expert].reshape(E, C, D)
        h = layer_norm(routed, ln_g, ln_b)
        h = jax.nn.gelu(jnp.einsum('ecd,edf->ecf', h, w1) + b1[:, None, :])
        h = jnp.einsum('ecf,efd->ecd', h, w2) + b2[:, None, :]
        out = routed + h
        inv = jnp.zeros((T,), dtype=jnp.int32).at[sort_by_expert].set(jnp.arange(T, dtype=jnp.int32))
        return out.reshape(T, D)[inv].reshape(x.shape)
    x = L0_attn_hidden_states
    xn = _layernorm(x, axis=-1)
    s = _L0_attn_ref(xn, L0_attn_W_qkv, L0_attn_conv_w, L0_attn_W_z, L0_attn_W_b, L0_attn_W_a, L0_attn_dt_bias, L0_attn_A_log, L0_attn_norm_weight, L0_attn_W_out)
    g = _silu(_L0_ffn_ref(xn, L0_ffn_ln_g, L0_ffn_ln_b, L0_ffn_router_w, L0_ffn_up_W, L0_ffn_up_b, L0_ffn_down_W, L0_ffn_down_b, L0_ffn_spec0_W, L0_ffn_spec0_b, L0_ffn_ln0_g, L0_ffn_ln0_b, L0_ffn_spec1a_W, L0_ffn_spec1a_b, L0_ffn_spec1b_W, L0_ffn_spec1b_b, L0_ffn_ln1_g, L0_ffn_ln1_b, L0_ffn_spec2_W, L0_ffn_spec2_b))
    x = x + s * g
    xn = _layernorm(x, axis=-1)
    s = _L1_attn_ref(xn, L1_attn_ln1_w, L1_attn_ln1_b, L1_attn_ln2_w, L1_attn_ln2_b, L1_attn_q_w, L1_attn_q_b, L1_attn_k_w, L1_attn_k_b, L1_attn_v_w, L1_attn_v_b, L1_attn_o_w, L1_attn_o_b, L1_attn_in_proj_w, L1_attn_conv_w, L1_attn_conv_b, L1_attn_x_proj_w, L1_attn_dt_w, L1_attn_dt_b, L1_attn_A_log, L1_attn_D_param, L1_attn_ssm_out_w, L1_attn_mix_weight, L1_attn_ffn_w1, L1_attn_ffn_b1, L1_attn_ffn_w2, L1_attn_ffn_b2)
    g = _silu(_L1_ffn_ref(xn, L1_ffn_centroids, L1_ffn_ln_g, L1_ffn_ln_b, L1_ffn_w1, L1_ffn_b1, L1_ffn_w2, L1_ffn_b2))
    x = x + s * g
    return x

_drawn_inputs = setup_inputs


def setup_inputs(seed=0):
    import zlib

    import numpy as np

    out = dict(_drawn_inputs(seed))
    spreads = {'L0_attn_dt_bias': (1.0, 0.2),
     'L0_attn_norm_weight': (1.0, 0.2),
     'L0_ffn_ln_g': (1.0, 0.2),
     'L0_ffn_ln_b': (0.0, 0.1),
     'L0_ffn_up_b': (0.0, 0.1),
     'L0_ffn_down_b': (0.0, 0.1),
     'L0_ffn_spec0_b': (0.0, 0.1),
     'L0_ffn_ln0_g': (1.0, 0.2),
     'L0_ffn_ln0_b': (0.0, 0.1),
     'L0_ffn_spec1a_b': (0.0, 0.1),
     'L0_ffn_spec1b_b': (0.0, 0.1),
     'L0_ffn_ln1_g': (1.0, 0.2),
     'L0_ffn_ln1_b': (0.0, 0.1),
     'L0_ffn_spec2_b': (0.0, 0.1),
     'L1_attn_ln1_w': (1.0, 0.2),
     'L1_attn_ln1_b': (0.0, 0.1),
     'L1_attn_ln2_w': (1.0, 0.2),
     'L1_attn_ln2_b': (0.0, 0.1),
     'L1_attn_q_b': (0.0, 0.1),
     'L1_attn_k_b': (0.0, 0.1),
     'L1_attn_v_b': (0.0, 0.1),
     'L1_attn_o_b': (0.0, 0.1),
     'L1_attn_conv_b': (0.0, 0.1),
     'L1_attn_D_param': (1.0, 0.2),
     'L1_attn_mix_weight': (0.5, 0.2),
     'L1_attn_ffn_b1': (0.0, 0.1),
     'L1_attn_ffn_b2': (0.0, 0.1),
     'L1_ffn_ln_g': (1.0, 0.2),
     'L1_ffn_ln_b': (0.0, 0.1),
     'L1_ffn_b1': (0.0, 0.1),
     'L1_ffn_b2': (0.0, 0.1)}
    factors = {}
    for name, (base, spread) in spreads.items():
        noise = np.random.default_rng([zlib.crc32(name.encode()), seed]).standard_normal(out[name].shape)
        drawn = base * np.exp(spread * noise) if base else spread * noise
        out[name] = jnp.asarray(drawn.astype(out[name].dtype))
    for name, factor in factors.items():
        out[name] = (out[name] * factor).astype(out[name].dtype)
    return out
```

```python
from contextlib import ExitStack

import concourse.bass as bass
import numpy as np
from concourse import mybir

F32 = mybir.dt.float32
I32 = mybir.dt.int32
ALU = mybir.AluOpType
ACT = mybir.ActivationFunctionType
AX = mybir.AxisListType

P = 128
H = 128
S = 512
CH = S // P
NVH, NKH, DK = 16, 8, 64
NG = 4
LEVELS = 7
E = 8
F = 512
FB = F // P
NH1, HD = 16, 8
DI, DS, DTR = 256, 16, 8
DB = DI // P
FF = 512
SCORE_BIG = 1e30
ROUNDS, WAYS = 8, 16
LN_EPS = 1e-5
RMS_EPS = 1e-6
SLOT_HEADS = [4 * g + s for g in range(NG) for s in (0, 2, 1, 3)]


class Arena:

    def __init__(self, core, name, columns):
        self.whole, self.columns, self.at = core.sb(name, [P, columns]), columns, 0

    def reset(self):
        self.at = 0

    def __call__(self, shape):
        n = int(np.prod(shape[1:]))
        assert self.at + n <= self.columns, (self.at, n, self.columns)
        view = self.whole[0:shape[0], self.at:self.at + n]
        self.at += n
        names = "abcd"[:len(shape) - 1]
        if len(shape) == 2:
            return view
        return view.rearrange(f"p ({' '.join(names)}) -> p {' '.join(names)}", **dict(zip(names, shape[1:])))


def flat(tickets):
    for t in tickets:
        if t is None:
            continue
        if isinstance(t, list):
            yield from flat(t)
        else:
            yield t


class Core:

    def __init__(self, nc, ctx):
        self.nc, self.ctx = nc, ctx
        self.seen = {}
        self.streams, self.dmas = [], []

    def sb(self, name, shape, dtype=F32):
        return self.ctx.enter_context(self.nc.sbuf_tensor(name, shape, dtype))

    def sem(self, name):
        return self.ctx.enter_context(self.nc.semaphore(name))

    def fence(self):
        last = [(st.sems[who], st.count[who]) for st in self.streams for who in st.sems]
        last += [(d.sem, d.count) for d in self.dmas if d.count]
        nc = self.nc
        for name, engine in (("pe", nc.tensor), ("act", nc.scalar), ("dve", nc.vector), ("pool", nc.gpsimd), ("sp", nc.sync)):
            self.wait(name, engine, last)

    def wait(self, name, engine, tickets):
        for sem, value in flat(tickets):
            key = (name, id(sem))
            if self.seen.get(key, 0) < value:
                self.seen[key] = value
                engine.wait_ge(sem, value)


class Stream:

    def __init__(self, core, name):
        self.core, self.name = core, name
        core.streams.append(self)
        nc = core.nc
        self.engines = {"pe": nc.tensor, "act": nc.scalar, "dve": nc.vector, "pool": nc.gpsimd}
        self.sems, self.count = {}, {}

    def run(self, who, fn, waits, chain):
        engine = self.engines[who]
        if who not in self.sems:
            self.sems[who] = self.core.sem(f"{self.name}_{who}")
            self.count[who] = 0
        sem = self.sems[who]
        if chain and self.count[who]:
            waits = [*waits, (sem, self.count[who])]
        self.core.wait(who, engine, waits)
        fn(engine).then_inc(sem, 1)
        self.count[who] += 1
        return sem, self.count[who]

    def pe(self, fn, *waits, chain=False):
        return self.run("pe", fn, waits, chain)

    def act(self, fn, *waits, chain=True):
        return self.run("act", fn, waits, chain)

    def dve(self, fn, *waits, chain=True):
        return self.run("dve", fn, waits, chain)

    def pool(self, fn, *waits, chain=True):
        return self.run("pool", fn, waits, chain)


class Dma:

    def __init__(self, core, name):
        self.core, self.sem, self.count = core, core.sem(name), 0
        core.dmas.append(self)

    def start(self, out, in_, *waits, who="sp"):
        engine = {"sp": self.core.nc.sync, "act": self.core.nc.scalar, "pool": self.core.nc.gpsimd}[who]
        self.core.wait(who, engine, waits)
        engine.dma_start(out, in_).then_inc(self.sem, 16)
        self.count += 16
        return self.sem, self.count


class Ring:

    def __init__(self, items):
        self.items, self.readers, self.at = items, [[] for _ in items], -1

    def take(self):
        self.at = (self.at + 1) % len(self.items)
        return self.items[self.at], self.readers[self.at], self.at

    def read_by(self, slot, *tickets):
        self.readers[slot] = list(tickets)


def interleave(lines):
    lines = list(lines)
    while lines:
        for line in list(lines):
            try:
                next(line)
            except StopIteration:
                lines.remove(line)


def layer_norm_tok(st, src, dst, work, *waits, n=CH):
    stats, mv, rstd = work
    for c in range(n):
        t = st.dve(lambda e: e.bn_stats(stats[:, c, :], src[:, c, :]), *waits)
        t = st.dve(lambda e: e.bn_aggr(mv[:, c, :], stats[:, c, :]))
    t = st.act(lambda e: e.activation(rstd[:, 0:n], mv[:, 0:n, 1], ACT.Ln, bias=st.core.eps_ln[:, 0:1]), t)
    t = st.act(lambda e: e.activation(rstd[:, 0:n], rstd[:, 0:n], ACT.Exp, scale=-0.5))
    for c in range(n):
        t = st.dve(lambda e: e.tensor_scalar(dst[:, c, :], src[:, c, :], mv[:, c, 0:1], rstd[:, c:c + 1],
                                             ALU.subtract, ALU.mult), t)
    return t


def transpose_tiles(st, banks, src, dst, scale, bias, *waits, n=CH):
    bank, free, slot = banks.take()
    for c in range(n):
        t = st.pe(lambda e: e.transpose(bank[:, c * P:(c + 1) * P], src[:, c, :], st.core.ident[:, :]), *waits, free)
    if scale is None:
        t = st.act(lambda e: e.activation(dst[:, 0:n * P], bank[:, 0:n * P], ACT.Copy), t, *waits)
    else:
        t = st.act(lambda e: e.activation(dst[:, 0:n * P], bank[:, 0:n * P], ACT.Identity, bias=bias, scale=scale), t, *waits)
    banks.read_by(slot, t)
    return t


def softplus_parts(st, src, neg_abs, out, ready):
    t = st.dve(lambda e: e.scalar_tensor_tensor(out=neg_abs, in0=src, scalar=-1.0, in1=src, op0=ALU.mult, op1=ALU.min), ready)
    t = st.act(lambda e: e.activation(neg_abs, neg_abs, ACT.Exp), t)
    return st.act(lambda e: e.activation(out, neg_abs, ACT.Ln, bias=1.0))


def build_constants(core):
    st = core.const = Stream(core, "const")
    core.ident = core.sb("ident", [P, P])
    core.ones = core.sb("ones", [P, P])
    core.mask_incl = core.sb("mask_incl", [P, P])
    core.mask_strict = core.sb("mask_strict", [P, P])
    core.last_row = core.sb("last_row", [P, P])
    core.before = core.sb("before", [P, E, E])
    core.eps_ln = core.sb("eps_ln", [P, 1])
    core.eps_rms = core.sb("eps_rms", [P, 1])
    core.ln_qscale = core.sb("ln_qscale", [P, 1])
    st.pool(lambda e: e.memset(core.ones[:, :], 1.0))
    st.pool(lambda e: e.memset(core.eps_ln[:, :], LN_EPS))
    st.pool(lambda e: e.memset(core.eps_rms[:, :], RMS_EPS))
    st.pool(lambda e: e.memset(core.ln_qscale[:, :], float(np.log(DK ** -0.5))))

    def keep(dst, op, base, mult, step):
        st.pool(lambda e: e.affine_select(out=dst[:, :], in_=core.ones[:, :], compare_op=op, fill=0.0, base=base,
                                          pattern=[[step, P]], channel_multiplier=mult))
    keep(core.ident, ALU.is_equal, 0, 1, -1)
    keep(core.mask_incl, ALU.is_ge, 0, -1, 1)
    keep(core.mask_strict, ALU.is_ge, -1, -1, 1)
    st.pool(lambda e: e.memset(core.before[:, :, :], 1.0))
    st.pool(lambda e: e.affine_select(out=core.before[:, :, :], in_=core.before[:, :, :], compare_op=ALU.is_ge, fill=0.0, base=-1,
                                      pattern=[[1, E], [-1, E]], channel_multiplier=0))
    keep(core.last_row, ALU.is_ge, 1 - P, 1, 0)
    core.mask_neg = core.sb("mask_neg", [P, P])
    core.iota = core.sb("iota", [P, WAYS + 1])
    st.pool(lambda e: e.memset(core.mask_neg[:, :], 0.0))
    st.pool(lambda e: e.affine_select(out=core.mask_neg[:, :], in_=core.mask_neg[:, :], compare_op=ALU.is_ge, fill=-SCORE_BIG, base=0,
                                      pattern=[[-1, P]], channel_multiplier=1))
    for i in range(WAYS + 1):
        st.pool(lambda e: e.memset(core.iota[:, i:i + 1], float(i)), chain=False)
    return (st.sems["pool"], st.count["pool"])



class DeltaGroup:

    def __init__(self, carve, core, n, banks):
        def sb(name, shape):
            return carve(shape)
        self.st = Stream(core, f"dg{n}")
        self.raw = Ring([sb(f"raw{i}", [P, S + 3]) for i in range(2)])
        self.chan = sb("chan", [P, 4, S])
        self.gate = Ring([sb(f"gate{i}", [P, 4, P]) for i in range(2)])
        self.gate_dma = [Dma(core, f"dg{n}_gate{i}") for i in range(2)]
        self.decay = sb("decay", [P, 4, P])
        self.conv = self.decay[:, :, :].rearrange("p s i -> p (s i)")
        self.attn = sb("attn", [P, 4, P])
        self.pt = [sb(f"pt{i}", [P, 4, P]) for i in range(2)]
        self.pw = sb("pw", [P, 4, P])
        self.rhs = sb("rhs", [P, 2, 4, DK])
        self.kdec = sb("kdec", [P, 4, DK])
        self.wt = sb("wt", [P, 2, P])
        self.qdec = sb("qdec", [P, 2, P])
        self.err = sb("err", [P, 4, DK])
        self.state = sb("state", [P, 2, P])
        self.sz = sb("sz", [P, 4 * DK])
        self.h = sb("h", [P, 4 * DK])
        self.sq = sb("sq", [P, 4 * DK])
        self.ss = sb("ss", [P, 4])
        self.ht = sb("ht", [P, 2, P])
        self.banks = banks
        self.fresh()

    def fresh(self):
        for buf in self.raw.items:
            self.st.pool(lambda e: e.memset(buf[:, 0:3], 0.0))
        self.zeroed = self.st.pool(lambda e: e.memset(self.state[:, :, :], 0.0))
        self.chan_free = self.rhs_free = self.kdec_free = self.decay_free = self.qdec_free = self.pt_free = None
        self.attn_free = self.wt_free = self.sz_free = self.err_free = self.h_free = self.ht_free = self.state_free = None


def delta_group(core, L, D, b, g):
    st, banks = D.st, D.banks
    w = core.w
    ready = L.ready
    silu_done = None
    for n, block in enumerate((g, NG + g, 2 * NG + 2 * g, 2 * NG + 2 * g + 1)):
        bank, free, slot = banks.take()
        raw, raw_free, raw_slot = D.raw.take()
        t = st.pe(lambda e: e.matmul(bank[:, :], w["w_qkv"][:, block * P:(block + 1) * P], L.xn_chan[:, :],
                                     start=True, stop=True), ready, free)
        t = st.act(lambda e: e.activation(raw[:, 3:], bank[:, :], ACT.Copy), t, raw_free, D.zeroed)
        banks.read_by(slot, t)
        cw = w["conv0"]
        t = st.dve(lambda e: e.tensor_scalar(D.conv, raw[:, 3:3 + S], cw[:, block, 3:4], None, ALU.mult), t, silu_done, D.decay_free)
        for j in (2, 1, 0):
            t = st.dve(lambda e: e.scalar_tensor_tensor(out=D.conv, in0=raw[:, j:j + S], scalar=cw[:, block, j:j + 1],
                                                        in1=D.conv, op0=ALU.mult, op1=ALU.add))
        D.raw.read_by(raw_slot, t)
        silu_done = st.act(lambda e: e.activation(D.chan[:, n, :], D.conv, ACT.Silu), t, D.chan_free)
        yield
    t_state = st.dve(lambda e: e.memset(D.state[0:DK, :, 0:DK], 0.0), D.state_free, D.zeroed)
    t_state = st.dve(lambda e: e.memset(D.state[DK:P, :, DK:P], 0.0))
    for c in range(CH):
        tok = slice(c * P, (c + 1) * P)
        hs = slice(4 * g, 4 * g + 4)
        gate, gate_free, gate_slot = D.gate.take()
        t_gate = D.gate_dma[gate_slot].start(
            gate[:, :, :], L.gate_dram[b, hs, tok].partition_broadcast(P), L.gate_stored, gate_free)
        bank, free, slot = banks.take()
        for n in range(2):
            st.pe(lambda e: e.transpose(bank[:, n * P:(n + 1) * P], D.chan[:, 2 + n, tok], core.ident[:, :]), silu_done, free)
        t = st.pe(lambda e: e.transpose(bank[:, 2 * P:3 * P], D.chan[:, 1, tok], core.ident[:, :]))
        vsrc = bank[:, 0:2 * P].rearrange("p (j u d) -> p u j d", j=2, u=2)
        t_rv = st.act(lambda e: e.activation(D.rhs[:, 0, :, :].rearrange("p (u j) d -> p u j d", u=2), vsrc, ACT.Copy), t, D.rhs_free)
        ktok = bank[:, 2 * P:3 * P].rearrange("p (a u d) -> p a u d", a=1, u=2).to_broadcast([P, 2, 2, DK])

        def col(a):
            return a[:, c, hs].rearrange("p (a u) -> p a u", a=2).unsqueeze(3).to_broadcast([P, 2, 2, DK])
        t_rk = st.dve(lambda e: e.tensor_tensor(D.rhs[:, 1, :, :].rearrange("p (a u) d -> p a u d", a=2), ktok, col(L.grow), ALU.mult),
                      t_rv, D.rhs_free)
        t_kd = st.dve(lambda e: e.tensor_tensor(D.kdec[:, :, :].rearrange("p (a u) d -> p a u d", a=2), ktok, col(L.kfall), ALU.mult),
                      D.kdec_free)
        banks.read_by(slot, t_rv, t_kd)
        yield
        for s in range(4):
            h = 4 * g + s
            t = st.dve(lambda e: e.tensor_scalar(D.decay[:, s, :], gate[:, s, :], L.lnb_minus_g[:, c, h:h + 1], L.lnb[:, c, h:h + 1],
                                                 ALU.add, ALU.min), t_gate, D.decay_free, silu_done, chain=(s == 0))
        for u in range(2):
            rows = slice(u * DK, (u + 1) * DK)
            t_q = st.act(lambda e: e.activation(D.qdec[rows, :, :], gate[rows, :, :].rearrange("p (a u) i -> p a u i", u=2)[:, :, u, :], ACT.Exp,
                                          bias=core.ln_qscale[rows, 0:1]), t_gate, D.qdec_free, chain=(u == 0))
        t_dec = st.act(lambda e: e.activation(D.decay[:, :, :], D.decay[:, :, :], ACT.Exp), t)
        D.gate.read_by(gate_slot, t, t_q)
        qsrc = D.chan[:, 0, tok].unsqueeze(1).to_broadcast([P, 2, P])
        t_q = st.pool(lambda e: e.tensor_tensor(D.qdec[:, :, :], D.qdec[:, :, :], qsrc, ALU.mult), t_q)
        incl = core.mask_incl[:, :].unsqueeze(1).to_broadcast([P, 4, P])
        strict = core.mask_strict[:, :].unsqueeze(1).to_broadcast([P, 4, P])
        t_ms = st.pool(lambda e: e.tensor_tensor(D.pt[0][:, :, :], D.decay[:, :, :], strict, ALU.mult), t_dec, D.pt_free)
        t_mi = st.pool(lambda e: e.tensor_tensor(D.attn[:, :, :], D.decay[:, :, :], incl, ALU.mult), D.attn_free, chain=False)
        D.decay_free = t_mi
        t_kk = []
        halves = []
        for u in range(2):
            rows = slice(u * DK, (u + 1) * DK)
            bank, free, slot = banks.take()
            st.pe(lambda e: e.matmul(bank[:, 0:P], D.chan[rows, 1, tok], D.chan[rows, 1, tok], start=True, stop=True), free)
            t = st.pe(lambda e: e.matmul(bank[:, P:2 * P], D.chan[rows, 1, tok], D.chan[rows, 0, tok], start=True, stop=True))
            halves.append((bank, slot))
            t_kk.append(t)
        for u, (bank, slot) in enumerate(halves):
            pt = D.pt[0][:, :, :].rearrange("p (a u) i -> p a u i", u=2)[:, :, u, :]
            at = D.attn[:, :, :].rearrange("p (a u) i -> p a u i", u=2)[:, :, u, :]
            kk = bank[:, 0:P].unsqueeze(1).to_broadcast([P, 2, P])
            qk = bank[:, P:2 * P].unsqueeze(1).to_broadcast([P, 2, P])
            t_pt = st.dve(lambda e: e.scalar_tensor_tensor(out=pt, in0=kk, scalar=-1.0, in1=pt, op0=ALU.mult, op1=ALU.mult),
                          t_kk[u], t_ms)
            t_at = st.dve(lambda e: e.scalar_tensor_tensor(out=at, in0=qk, scalar=DK ** -0.5, in1=at, op0=ALU.mult, op1=ALU.mult),
                          t_mi, chain=False)
            banks.read_by(slot, t_at)
        yield
        t_r = [t_rv, t_rk]
        t_pw = None
        for k in range(LEVELS):
            cur, nxt = D.pt[k % 2], D.pt[(k + 1) % 2]
            if k < LEVELS - 1:
                bank, free, slot = banks.take()
                for s in range(4):
                    t = st.pe(lambda e: e.transpose(bank[:, s * P:(s + 1) * P], cur[:, s, :], core.ident[:, :]), t_pt, free)
                t_pw = st.act(lambda e: e.activation(D.pw[:, :, :].rearrange("p s i -> p (s i)"), bank[:, :], ACT.Copy), t, t_pw)
                banks.read_by(slot, t_pw)
            bank, free, slot = banks.take()
            for s in range(4):
                t_ap = st.pe(lambda e: e.matmul(bank[:, s * P:(s + 1) * P], cur[:, s, :], D.rhs[:, :, s, :], start=True, stop=True),
                             t_pt, t_r, free)
            rview = D.rhs[:, :, :, :].rearrange("p t s d -> p s t d")
            t_r = [st.dve(lambda e: e.tensor_tensor(rview, bank[:, :].rearrange("p (s t d) -> p s t d", s=4, t=2), rview, ALU.add), t_ap)]
            banks.read_by(slot, t_r)
            if k < LEVELS - 1:
                bank, free, slot = banks.take()
                for s in range(4):
                    t = st.pe(lambda e: e.matmul(bank[:, s * P:(s + 1) * P], D.pw[:, s, :], cur[:, s, :], start=True, stop=True), t_pw, free)
                t_pt = st.act(lambda e: e.activation(nxt[:, :, :].rearrange("p s i -> p (s i)"), bank[:, :], ACT.Copy), t)
                banks.read_by(slot, t_pt)
            yield
        D.pt_free = t_ap
        bank, free, slot = banks.take()
        for p in range(2):
            t = st.pe(lambda e: e.transpose(bank[:, p * P:(p + 1) * P], D.rhs[:, 1, 2 * p:2 * p + 2, :].rearrange("p s d -> p (s d)"),
                                            core.ident[:, :]), t_r, free)
        t_wt = st.act(lambda e: e.activation(D.wt[:, :, :].rearrange("p a i -> p (a i)"), bank[:, 0:2 * P], ACT.Copy), t, D.wt_free)
        banks.read_by(slot, t_wt)
        bank, free, slot = banks.take()
        t = st.pe(lambda e: e.matmul(bank[:, 0:4 * DK], L.xn_chan[:, tok], w["w_z"][:, g * 4 * DK:(g + 1) * 4 * DK],
                                     start=True, stop=True), free)
        t_sz = st.act(lambda e: e.activation(D.sz[:, :], bank[:, 0:4 * DK], ACT.Silu), t, D.sz_free)
        banks.read_by(slot, t_sz)
        bank, free, slot = banks.take()
        for p in range(2):
            t = st.pe(lambda e: e.matmul(bank[:, p * P:(p + 1) * P], D.wt[:, p, :], D.state[:, p, :], start=True, stop=True),
                      t_wt, t_state, free)
        D.wt_free = t
        t_e = st.dve(lambda e: e.tensor_tensor(D.err[:, :, :], D.rhs[:, 0, :, :], bank[:, 0:2 * P].rearrange("p (s d) -> p s d", s=4),
                                               ALU.subtract), t, D.err_free)
        D.rhs_free = [t_wt, t_e]
        banks.read_by(slot, t_e)
        sbank, free, sslot = banks.take()
        for p in range(2):
            t_su = st.pe(lambda e: e.matmul(sbank[:, p * P:(p + 1) * P], D.kdec[:, 2 * p:2 * p + 2, :].rearrange("p s d -> p (s d)"),
                                            D.err[:, 2 * p:2 * p + 2, :].rearrange("p s d -> p (s d)"), start=True, stop=True),
                         t_kd, t_e, free)
        D.kdec_free = t_su
        bank, free, slot = banks.take()
        for p in range(2):
            st.pe(lambda e: e.matmul(bank[:, p * P:(p + 1) * P], D.qdec[:, p, :], D.state[:, p, :], start=(p == 0), stop=False,
                                     skip_group_check=True), t_q, free)
        for s in range(4):
            t_o = st.pe(lambda e: e.matmul(bank[:, s * DK:(s + 1) * DK], D.attn[:, s, :], D.err[:, s, :], start=False, stop=(s == 3),
                                           skip_group_check=True), t_at)
        D.qdec_free = D.attn_free = D.err_free = t_o
        for s in range(4):
            u, p = s % 2, s // 2
            rows = slice(u * DK, (u + 1) * DK)
            blk = D.state[rows, p, u * DK:(u + 1) * DK]
            t_state = st.dve(lambda e: e.scalar_tensor_tensor(
                out=blk, in0=blk, scalar=L.chunk_decay[rows, c, 4 * g + s:4 * g + s + 1],
                in1=sbank[rows, p * P + u * DK:p * P + (u + 1) * DK], op0=ALU.mult, op1=ALU.add), t_su, t_o, chain=(s == 0))
        banks.read_by(sslot, t_state)
        D.state_free = t_o
        yield
        t = st.dve(lambda e: e.tensor_tensor(D.h[:, :], bank[:, 0:4 * DK], D.sz[:, :], ALU.mult), t_o, t_sz, D.h_free)
        banks.read_by(slot, t)
        D.sz_free = t
        t = st.dve(lambda e: e.tensor_tensor(D.sq[:, :], D.h[:, :], D.h[:, :], ALU.mult))
        t = st.dve(lambda e: e.tensor_reduce(D.ss[:, :], D.sq[:, :].rearrange("p (s d) -> p s d", s=4), AX.X, ALU.add))
        t = st.act(lambda e: e.activation(D.ss[:, :], D.ss[:, :], ACT.Ln, bias=core.eps_rms[:, 0:1], scale=1.0 / DK), t)
        t = st.act(lambda e: e.activation(D.ss[:, :], D.ss[:, :], ACT.Exp, scale=-0.5))
        hv = D.h[:, :].rearrange("p (s d) -> p s d", s=4)
        t = st.pool(lambda e: e.tensor_tensor(hv, hv, D.ss[:, :].unsqueeze(2).to_broadcast([P, 4, DK]), ALU.mult), t)
        yield
        bank, free, slot = banks.take()
        for p in range(2):
            t = st.pe(lambda e: e.transpose(bank[:, p * P:(p + 1) * P], D.h[:, p * P:(p + 1) * P], core.ident[:, :]), t, free)
        D.h_free = t
        t = st.act(lambda e: e.activation(D.ht[:, :, :].rearrange("p a i -> p (a i)"), bank[:, 0:2 * P], ACT.Copy), t, D.ht_free)
        banks.read_by(slot, t)
        bank, free, slot = banks.take()
        for p in range(2):
            t = st.pe(lambda e: e.matmul(bank[:, 0:P], D.ht[:, p, :], w["w_out"][:, 2 * g + p, :], start=(p == 0), stop=(p == 1)), t, free)
        D.ht_free = t
        sdst = L.s_tok[:, c, :]
        if g == 0:
            t = st.dve(lambda e: e.tensor_copy(sdst, bank[:, 0:P]), t, L.s_free)
        else:
            t = st.dve(lambda e: e.tensor_tensor(sdst, sdst, bank[:, 0:P], ALU.add), t, L.s_done[c])
        L.s_done[c] = t
        banks.read_by(slot, t)
        yield
    D.chan_free = t_o
    L.group_done.append(t_o)


class Layer0:

    def __init__(self, core, dram):
        self.st = Stream(core, "l0")
        sb = core.sb
        self.xn_tok = sb("xn_tok", [P, CH, H])
        self.xn_chan = sb("xn_chan", [P, S])
        self.s_tok = sb("s_tok", [P, CH, H])
        self.ln_work = (sb("ln_stats", [P, CH, 6]), sb("ln_mv", [P, CH, 2]), sb("ln_rstd", [P, CH]))
        self.beta_in = sb("beta_in", [P, CH, NVH])
        self.lnb = sb("lnb", [P, CH, NVH])
        self.lnb_minus_g = sb("lnb_minus_g", [P, CH, NVH])
        self.g_tok = sb("g_tok", [P, CH, NVH])
        self.grow = sb("grow", [P, CH, NVH])
        self.kfall = sb("kfall", [P, CH, NVH])
        self.chunk_decay = sb("chunk_decay", [P, CH, NVH])
        self.gate_a = sb("gate_a", [NVH, S])
        self.gate_t = sb("gate_t", [NVH, S])
        self.gate_g = sb("gate_g", [NVH, S])
        self.gate_dram = dram["gate"]
        self.gate_dma = Dma(core, "gate_store")
        self.s_done = [None] * CH
        self.s_free = None
        self.group_done = []


def layer0_prologue(core, L, banks, x_tile, x_ready):
    st, w = L.st, core.w
    prev = list(L.group_done)
    t = layer_norm_tok(st, x_tile, L.xn_tok, L.ln_work, x_ready, prev, L.xn_free)
    L.xn_ready = t
    t_x = transpose_tiles(st, banks, L.xn_tok, L.xn_chan, None, None, t, prev)
    bank, free, slot = banks.take()
    for c in range(CH):
        t = st.pe(lambda e: e.matmul(bank[:, c * NVH:(c + 1) * NVH], L.xn_chan[:, c * P:(c + 1) * P], w["w_b"][:, :],
                                     start=True, stop=True), t_x, free)
    def n2(a):
        return a[:, :, :].rearrange("p c h -> p (c h)")
    t = st.dve(lambda e: e.tensor_copy(n2(L.beta_in), bank[:, 0:CH * NVH]), t, prev)
    banks.read_by(slot, t)
    t_l = softplus_parts(st, n2(L.beta_in), n2(L.kfall), n2(L.grow), t)
    t = st.dve(lambda e: e.tensor_scalar(n2(L.beta_in), n2(L.beta_in), 0.0, None, ALU.min))
    t_b = st.dve(lambda e: e.tensor_tensor(n2(L.lnb), n2(L.beta_in), n2(L.grow), ALU.subtract), t_l)
    bank, free, slot = banks.take()
    t = st.pe(lambda e: e.matmul(bank[0:NVH, :], w["w_a"][:, :], L.xn_chan[:, :], start=True, stop=True), free)
    t = st.act(lambda e: e.activation(L.gate_a[:, :], bank[0:NVH, :], ACT.Identity, bias=w["dt_bias"][:, 0:1]), t)
    banks.read_by(slot, t)
    t_l = softplus_parts(st, L.gate_a[:, :], L.gate_t[:, :], L.gate_t[:, :], t)
    t = st.dve(lambda e: e.scalar_tensor_tensor(out=L.gate_a[:, :], in0=L.gate_a[:, :], scalar=0.0, in1=L.gate_t[:, :],
                                                op0=ALU.max, op1=ALU.add), t_l)
    t = st.dve(lambda e: e.tensor_scalar(L.gate_a[:, :], L.gate_a[:, :], core.neg_exp_a0[:, 0:1], None, ALU.mult), core.prep_done)
    for c in range(CH):
        tok = slice(c * P, (c + 1) * P)
        t = st.dve(lambda e: e.tensor_tensor_scan(L.gate_g[:, tok], core.ones[0:NVH, :], L.gate_a[:, tok], 0.0, ALU.mult, ALU.add),
                   L.gate_stored)
    L.gate_stored = L.gate_dma.start(L.gate_dram[L.b], L.gate_g[:, :], t)
    bank, free, slot = banks.take()
    for c in range(CH):
        t2 = st.pe(lambda e: e.transpose(bank[:, c * NVH:(c + 1) * NVH], L.gate_g[:, c * P:(c + 1) * P], core.ident[0:NVH, 0:NVH]), t, free)
    t = st.dve(lambda e: e.tensor_copy(n2(L.g_tok), bank[:, 0:CH * NVH]), t2)
    t_m = st.dve(lambda e: e.tensor_tensor(n2(L.lnb_minus_g), n2(L.lnb), n2(L.g_tok), ALU.subtract))
    t = st.pe(lambda e: e.matmul(bank[:, CH * NVH:2 * CH * NVH], core.last_row[:, :], n2(L.g_tok), start=True, stop=True), t)
    t = st.dve(lambda e: e.tensor_tensor(n2(L.kfall), bank[:, CH * NVH:2 * CH * NVH], n2(L.lnb_minus_g), ALU.add), t)
    t = st.act(lambda e: e.activation(n2(L.kfall), n2(L.kfall), ACT.Exp), t)
    t_c = st.act(lambda e: e.activation(n2(L.chunk_decay), bank[:, CH * NVH:2 * CH * NVH], ACT.Exp), chain=False)
    banks.read_by(slot, t_c)
    t = st.act(lambda e: e.activation(n2(L.grow), n2(L.g_tok), ACT.Exp))
    L.ready = [t, t_m, t_b]
    L.group_done = []
    for c in range(CH):
        L.s_done[c] = None



def center_weights(core, st, wt, bias, nk, sums, bank, *waits):
    t = st.dve(lambda e: e.tensor_reduce(sums[:, 0:2 * nk].rearrange("p (s k) -> p s k", s=2), wt[:, :, :, :], AX.X, ALU.add), *waits)
    t = st.dve(lambda e: e.tensor_scalar(sums[:, 0:2 * nk], sums[:, 0:2 * nk], 1.0 / F, None, ALU.mult))
    for s in range(2):
        for k in range(nk):
            t = st.dve(lambda e: e.tensor_scalar(wt[:, s, k, :], wt[:, s, k, :], sums[:, s * nk + k:s * nk + k + 1], None, ALU.subtract),
                       chain=(s + k == 0))
    t = st.pe(lambda e: e.matmul(bank[:, 0:2 * FB], core.ones[:, :], bias[:, :, :].rearrange("p s k -> p (s k)"), start=True, stop=True), t)
    t = st.dve(lambda e: e.tensor_reduce(sums[:, 0:2], bank[:, 0:2 * FB].rearrange("p (s k) -> p s k", s=2), AX.X, ALU.add), t)
    t = st.dve(lambda e: e.tensor_scalar(sums[:, 0:2], sums[:, 0:2], 1.0 / F, None, ALU.mult))
    return st.dve(lambda e: e.tensor_tensor(bias[:, :, :], bias[:, :, :], sums[:, 0:2].unsqueeze(2).to_broadcast([P, 2, FB]), ALU.subtract))


class ExpertLine:

    def __init__(self, sb, core, n, banks):
        self.st, self.banks = Stream(core, f"ex{n}"), banks
        self.h1 = sb([P, FB, S])
        self.h2 = sb([P, FB, S])
        self.sq = Ring([sb([P, S]) for _ in range(2)])
        self.rstd = sb([P, S])
        self.t1 = sb([P, 2, S])
        self.h1_free = self.h2_free = self.t1_free = None


def dense(X, nblk, nk, weight, src, src_ready, evac):
    out = []
    for m in range(nblk):
        bank, free, slot = X.banks.take()
        for k in range(nk):
            t = X.st.pe(lambda e: e.matmul(bank[:, :], weight(k, m), src[:, k, :], start=(k == 0), stop=(k == nk - 1)), src_ready, free)
        t = evac(m, bank, t)
        X.banks.read_by(slot, t)
        out.append(t)
    return out


def centered_norm(core, X, g, b, last, func):
    st = X.st
    bank, free, slot = X.banks.take()
    for m in range(FB):
        sq, sq_free, sq_slot = X.sq.take()
        t = st.pool(lambda e: e.tensor_tensor(sq[:, :], X.h2[:, m, :], X.h2[:, m, :], ALU.mult), last[m], sq_free)
        t = st.pe(lambda e: e.matmul(bank[:, :], core.ones[:, :], sq[:, :], start=(m == 0), stop=(m == FB - 1)), t, free)
        X.sq.read_by(sq_slot, t)
    t = st.act(lambda e: e.activation(X.rstd[:, :], bank[:, :], ACT.Ln, bias=core.eps_ln[:, 0:1], scale=1.0 / F), t)
    X.banks.read_by(slot, t)
    t = st.act(lambda e: e.activation(X.rstd[:, :], X.rstd[:, :], ACT.Exp, scale=-0.5))
    done = []
    for m in range(FB):
        t = st.dve(lambda e: e.tensor_tensor(X.h2[:, m, :], X.h2[:, m, :], X.rstd[:, :], ALU.mult), t, chain=(m == 0))
        if func is None:
            done.append(st.dve(lambda e: e.tensor_scalar(X.h2[:, m, :], X.h2[:, m, :], g[:, m:m + 1], b[:, m:m + 1], ALU.mult, ALU.add)))
        else:
            done.append(st.act(lambda e: e.activation(X.h2[:, m, :], X.h2[:, m, :], func, bias=b[:, m:m + 1], scale=g[:, m:m + 1]),
                               t, chain=(m == 0)))
    return done


def expert0(core, X, M, e):
    st, w = X.st, core.w
    kind, s = e % 4, e // 4

    def gelu_into(dst, bias):
        return lambda m, bank, t: st.act(
            lambda e: e.activation(dst[:, m, :], bank[:, :], ACT.Gelu, bias=bias[:, m:m + 1]), t, chain=(m == 0))
    t_h = dense(X, FB, 1, lambda k, m: w["up_w"][:, e, m * P:(m + 1) * P], M.nx_chan[:, :].unsqueeze(1), [M.ready, X.h1_free],
                gelu_into(X.h1, w["up_b"][:, e, :]))
    yield
    hid = X.h2
    if kind == 0:
        def with_bias(m, bank, t):
            return st.act(lambda en: en.activation(X.h2[:, m, :], bank[:, :], ACT.Identity, bias=w["spec0_b"][:, s, m:m + 1]), t,
                          X.h2_free, chain=(m == 0))
        t_x = dense(X, FB, FB, lambda k, m: w["spec0_w"][:, s, k, m * P:(m + 1) * P], X.h1, t_h, with_bias)
        X.h1_free = t_x
        yield
        t_h = centered_norm(core, X, w["ln0_g"][:, s, :], w["ln0_b"][:, s, :], t_x, ACT.Gelu)
    elif kind == 1:
        t_t = dense(X, 2, FB, lambda k, m: w["spec1a_w"][:, s, k, m * P:(m + 1) * P], X.h1, [t_h, X.t1_free],
                    gelu_into(X.t1, w["spec1a_b"][:, s, :]))
        X.h1_free = t_t

        def with_bias(m, bank, t):
            return st.act(lambda en: en.activation(X.h2[:, m, :], bank[:, :], ACT.Identity, bias=w["spec1b_b"][:, s, m:m + 1]), t,
                          X.h2_free, chain=(m == 0))
        t_x = dense(X, FB, 2, lambda k, m: w["spec1b_w"][:, s, k, m * P:(m + 1) * P], X.t1, t_t, with_bias)
        X.t1_free = t_x
        yield
        t_h = centered_norm(core, X, w["ln1_g"][:, s, :], w["ln1_b"][:, s, :], t_x, None)
    elif kind == 2:
        def gelu_h2(m, bank, t):
            return st.act(lambda en: en.activation(X.h2[:, m, :], bank[:, :], ACT.Gelu, bias=w["spec2_b"][:, s, m:m + 1]), t,
                          X.h2_free, chain=(m == 0))
        t_h = dense(X, FB, FB, lambda k, m: w["spec2_w"][:, s, k, m * P:(m + 1) * P], X.h1, t_h, gelu_h2)
        X.h1_free = t_h
    else:
        hid = X.h1
    yield
    bank, free, slot = X.banks.take()
    for c in range(CH):
        for k in range(FB):
            t = st.pe(lambda en: en.matmul(bank[:, c * P:(c + 1) * P], hid[:, k, c * P:(c + 1) * P], w["down_w"][:, e, k, :],
                                           start=(k == 0), stop=(k == FB - 1)), t_h, free)
    if kind == 3:
        X.h1_free = t
    else:
        X.h2_free = t
    for c in range(CH):
        M.acc_done[c] = st.dve(lambda en: en.scalar_tensor_tensor(
            out=M.acc[:, c, :], in0=bank[:, c * P:(c + 1) * P], scalar=M.weight[:, c, e:e + 1], in1=M.acc[:, c, :],
            op0=ALU.mult, op1=ALU.add), t, M.acc_done[c], chain=False)
    X.banks.read_by(slot, M.acc_done[CH - 1])
    yield


class Mixture0:
    def __init__(self, sb, core):
        self.st = Stream(core, "mix0")
        self.nx_tok = sb([P, CH, H])
        self.nx_chan = sb([P, S])
        self.acc = sb([P, CH, H])
        self.logit = sb([P, CH, E])
        self.cmp = sb([P, CH * E, E])
        self.eq = sb([P, CH * E, E])
        self.pick = sb([P, CH, E])
        self.weight = sb([P, CH, E])
        self.red = sb([P, CH])
        self.wt = sb([E, S])
        self.acc_done = [None] * CH


def mixture0(core, L, M, lines, banks):
    st, w = M.st, core.w
    t = layer_norm_tok(st, L.xn_tok, M.nx_tok, L.ln_work)
    t_x = transpose_tiles(st, banks, M.nx_tok, M.nx_chan, w["f_ln_g"][:, 0:1], w["f_ln_b"][:, 0:1], t)
    bank, free, slot = banks.take()
    for c in range(CH):
        t = st.pe(lambda e: e.matmul(bank[:, c * E:(c + 1) * E], M.nx_chan[:, c * P:(c + 1) * P], w["router_w"][:, :], start=True, stop=True),
                  t_x, free)
    lg = M.logit[:, :, :].rearrange("p c e -> p (c e)")
    t = st.dve(lambda e: e.tensor_copy(lg, bank[:, 0:CH * E]), t)
    banks.read_by(slot, t)
    mine = lg.unsqueeze(2).to_broadcast([P, CH * E, E])
    for c in range(CH):
        others = M.logit[:, c, :].unsqueeze(1).to_broadcast([P, E, E])
        rows = slice(c * E, (c + 1) * E)
        st.dve(lambda e: e.tensor_tensor(M.cmp[:, rows, :], others, mine[:, rows, :], ALU.is_gt), chain=(c == 0))
        st.dve(lambda e: e.tensor_tensor(M.eq[:, rows, :], others, mine[:, rows, :], ALU.is_equal), chain=False)
        st.dve(lambda e: e.tensor_tensor(M.eq[:, rows, :], M.eq[:, rows, :], core.before[:, :, :], ALU.mult))
    st.dve(lambda e: e.tensor_tensor(M.cmp[:, :, :], M.cmp[:, :, :], M.eq[:, :, :], ALU.add))
    pk = M.pick[:, :, :].rearrange("p c e -> p (c e)")
    st.dve(lambda e: e.tensor_reduce(pk, M.cmp[:, :, :], AX.X, ALU.add))
    st.dve(lambda e: e.tensor_scalar(pk, pk, 2.0, None, ALU.is_lt))
    st.dve(lambda e: e.tensor_reduce(M.red[:, :], M.logit[:, :, :], AX.X, ALU.max))
    t = st.dve(lambda e: e.tensor_tensor(M.weight[:, :, :], M.logit[:, :, :], M.red[:, :].unsqueeze(2).to_broadcast([P, CH, E]), ALU.subtract))
    t = st.act(lambda e: e.activation(M.weight[:, :, :], M.weight[:, :, :], ACT.Exp), t)
    st.dve(lambda e: e.tensor_tensor(M.weight[:, :, :], M.weight[:, :, :], M.pick[:, :, :], ALU.mult), t)
    st.dve(lambda e: e.tensor_reduce(M.red[:, :], M.weight[:, :, :], AX.X, ALU.add))
    st.dve(lambda e: e.reciprocal(M.red[:, :], M.red[:, :]))
    t_w = st.dve(lambda e: e.tensor_tensor(M.weight[:, :, :], M.weight[:, :, :], M.red[:, :].unsqueeze(2).to_broadcast([P, CH, E]), ALU.mult))
    bank, free, slot = banks.take()
    for c in range(CH):
        t = st.pe(lambda e: e.transpose(bank[0:E, c * P:(c + 1) * P], M.weight[:, c, :], core.ident[:, :]), t_w, free)
    t = st.act(lambda e: e.activation(M.wt[:, :], bank[0:E, :], ACT.Copy), t)
    for c in range(CH):
        t = st.pe(lambda e: e.matmul(bank[:, c * P:(c + 1) * P], M.wt[:, c * P:(c + 1) * P], w["down_b"][:, :], start=True, stop=True), t)
    t = st.dve(lambda e: e.tensor_tensor(M.acc[:, :, :].rearrange("p c h -> p (c h)"), bank[:, :],
                                         L.xn_tok[:, :, :].rearrange("p c h -> p (c h)"), ALU.add), t)
    banks.read_by(slot, t)
    M.acc_done = [t] * CH
    M.ready = [t_x, t]

    def line(n):
        for e in range(n, E, 2):
            yield from expert0(core, lines[n], M, e)
    interleave([line(0), line(1)])



class Attention:
    def __init__(self, sb, core, score_banks, banks):
        self.st, self.scores, self.banks = Stream(core, "attn"), score_banks, banks
        self.x_chan = sb([P, S])
        self.q = sb([P, 4, S])
        self.k = sb([P, 4, S])
        self.v = sb([P, CH, NH1, HD + 1])
        self.p = sb([P, 4, S])
        self.pt = sb([P, CH, 4, P])
        self.o = sb([P, CH, NH1, HD])
        self.mx = sb([P, 4])
        self.rden = sb([P, NH1])
        self.o_chan = sb([P, S])
        self.x2 = sb([P, CH, H])
        self.n_tok = sb([P, CH, H])
        self.n_chan = sb([P, S])
        self.hid = sb([P, FB, S])
        self.ones_set = self.st.pool(lambda e: e.memset(self.v[:, :, :, :], 1.0))
        self.scores_free = self.p_free = self.pt_free = None


def attention(core, A, Z, b):
    st, w, banks = A.st, core.w, A.banks
    xh = core.xhat_chan[:, b * S:(b + 1) * S]
    t_x = st.dve(lambda e: e.tensor_scalar(A.x_chan[:, :], xh, w["pre_w"][:, 0:1], w["pre_b"][:, 0:1], ALU.mult, ALU.add), core.xhat_ready[b],
                 A.x_free, Z.x_free)
    Z.x_ready = t_x
    for name, dst in (("q", A.q), ("k", A.k)):
        for g in range(4):
            bank, free, slot = banks.take()
            t = st.pe(lambda e: e.matmul(bank[:, :], w[name + "_w"][:, g * P:(g + 1) * P], A.x_chan[:, :], start=True, stop=True), t_x, free)
            t_qk = st.act(lambda e: e.activation(dst[:, g, :], bank[:, :], ACT.Identity, bias=w[name + "_b"][:, g:g + 1]), t, chain=False)
            banks.read_by(slot, t_qk)
    yield
    bank, free, slot = banks.take()
    for c in range(CH):
        t = st.pe(lambda e: e.matmul(bank[:, c * P:(c + 1) * P], A.x_chan[:, c * P:(c + 1) * P], w["v_w"][:, :], start=True, stop=True), free)
    for c in range(CH):
        t_v = st.dve(lambda e: e.tensor_tensor(A.v[:, c, :, 0:HD], bank[:, c * P:(c + 1) * P].rearrange("p (h d) -> p h d", h=NH1),
                                               w["v_b"][:, :].rearrange("p (h d) -> p h d", h=NH1), ALU.add), t, A.ones_set, chain=False)
    banks.read_by(slot, t_v)
    A.x_free = t
    yield
    scale = HD ** -0.5
    for i in range(CH):
        nk = (i + 1) * P
        obank, ofree, oslot = banks.take()
        for g in range(4):
            sc = A.scores
            for a in range(4):
                rows = slice(32 * a, 32 * a + HD)
                t = st.pe(lambda e: e.matmul(sc[:, a, 0:nk], A.q[rows, g, i * P:(i + 1) * P], A.k[rows, g, 0:nk], start=True, stop=True),
                          t_qk, A.scores_free)
            diag = sc[:, :, i * P:nk]
            t = st.dve(lambda e: e.tensor_tensor(diag, diag, core.mask_neg[:, :].unsqueeze(1).to_broadcast([P, 4, P]), ALU.add), t)
            st.dve(lambda e: e.tensor_reduce(A.mx[:, :], sc[:, :, 0:nk], AX.X, ALU.max), t)
            t = st.dve(lambda e: e.tensor_scalar(A.mx[:, :], A.mx[:, :], -scale, None, ALU.mult))
            for a in range(4):
                t_p = st.act(lambda e: e.activation(A.p[:, a, 0:nk], sc[:, a, 0:nk], ACT.Exp, bias=A.mx[:, a:a + 1], scale=scale),
                             t, A.p_free, chain=False)
            A.scores_free = t_p
            yield
            for kt in range(i + 1):
                bank, free, slot = banks.take()
                if slot == oslot:
                    bank, free, slot = banks.take()
                for a in range(4):
                    t = st.pe(lambda e: e.transpose(bank[:, a * P:(a + 1) * P], A.p[:, a, kt * P:(kt + 1) * P], core.ident[:, :]), t_p, free)
                dst = A.pt[:, kt, :, :].rearrange("p a q -> p (a q)")
                if kt % 2:
                    t_t = st.dve(lambda e: e.tensor_copy(dst, bank[:, :]), t, A.pt_free, chain=False)
                    t_odd = t_t
                else:
                    t_t = st.act(lambda e: e.activation(dst, bank[:, :], ACT.Copy), t, A.pt_free, chain=False)
                    t_even = t_t
                banks.read_by(slot, t_t)
            A.p_free = t
            for a in range(4):
                h = 4 * g + a
                for kt in range(i + 1):
                    t_o = st.pe(lambda e: e.matmul(obank[:, h * 9:h * 9 + 9], A.pt[:, kt, a, :], A.v[:, kt, h, :], start=(kt == 0),
                                                   stop=(kt == i), skip_group_check=True), t_even, t_odd if i else None, t_v, ofree)
            A.pt_free = t_o
            yield
        ov = obank[:, 0:NH1 * 9].rearrange("p (h d) -> p h d", h=NH1)
        t = st.dve(lambda e: e.reciprocal(A.rden[:, :], ov[:, :, HD]), t_o)
        t = st.dve(lambda e: e.tensor_tensor(A.o[:, i, :, :], ov[:, :, 0:HD], A.rden[:, :].unsqueeze(2).to_broadcast([P, NH1, HD]), ALU.mult))
        banks.read_by(oslot, t)
    t = transpose_tiles(st, banks, A.o[:, :, :, :].rearrange("p c h d -> p c (h d)"), A.o_chan, None, None, t)
    yield
    while not Z.done:
        yield
    bank, free, slot = banks.take()
    for c in range(CH):
        tok = slice(c * P, (c + 1) * P)
        st.pe(lambda e: e.matmul(bank[:, tok], A.o_chan[:, tok], w["o_w"][:, :], start=True, stop=False), t, free)
        for k in range(DB):
            t2 = st.pe(lambda e: e.matmul(bank[:, tok], Z.y[:, k, tok], w["ssm_out_w"][:, k, :], start=False, stop=(k == DB - 1)), Z.y_ready)
    Z.y_free = t2
    xb = core.xn1[:, b * CH:(b + 1) * CH, :]

    def bias(name):
        return w[name][:, :].unsqueeze(1).to_broadcast([P, CH, H])
    bview = bank[:, :].rearrange("p (c h) -> p c h", c=CH)
    t = st.dve(lambda e: e.tensor_tensor(A.x2[:, :, :], bview, xb, ALU.add), t2)
    banks.read_by(slot, t)
    t = st.dve(lambda e: e.tensor_tensor(A.x2[:, :, :], A.x2[:, :, :], bias("o_b"), ALU.add))
    t = layer_norm_tok(st, A.x2, A.n_tok, core.ln_work1)
    t_n = transpose_tiles(st, banks, A.n_tok, A.n_chan, w["mid_w"][:, 0:1], w["mid_b"][:, 0:1], t)
    yield
    for m in range(FB):
        bank, free, slot = banks.take()
        t = st.pe(lambda e: e.matmul(bank[:, :], w["ffn_w1"][:, m * P:(m + 1) * P], A.n_chan[:, :], start=True, stop=True), t_n, free)
        t_h = st.act(lambda e: e.activation(A.hid[:, m, :], bank[:, :], ACT.Gelu, bias=w["ffn_b1"][:, m:m + 1]), t, chain=False)
        banks.read_by(slot, t_h)
    yield
    bank, free, slot = banks.take()
    for c in range(CH):
        tok = slice(c * P, (c + 1) * P)
        for m in range(FB):
            t_f = st.pe(lambda e: e.matmul(bank[:, tok], A.hid[:, m, tok], w["ffn_w2"][:, m, :], start=(m == 0), stop=(m == FB - 1)), t_h, free)
    st.dve(lambda e: e.tensor_tensor(A.x2[:, :, :], A.x2[:, :, :], bias("ffn_b2"), ALU.add))
    bview2 = bank[:, :].rearrange("p (c h) -> p c h", c=CH)
    t = st.dve(lambda e: e.tensor_tensor(core.s1[:, b * CH:(b + 1) * CH, :], bview2, A.x2[:, :, :], ALU.add), t_f)
    banks.read_by(slot, t)
    yield


class StateSpace:
    def __init__(self, sb, core, banks):
        self.st, self.banks = Stream(core, "ssm"), banks
        self.raw = Ring([sb([P, S + 3]) for _ in range(2)])
        for buf in self.raw.items:
            self.zeroed = self.st.pool(lambda e: e.memset(buf[:, 0:3], 0.0))
        self.xc = sb([P, DB, S])
        self.sz = sb([P, DB, S])
        self.dt_in = sb([DTR, S])
        self.bc = sb([2 * DS, S])
        self.dt = sb([P, DB, S])
        self.tmp = sb([P, DB, S])
        self.dtx = sb([P, DB, S])
        self.da = Ring([sb([P, S]) for _ in range(2)])
        self.h = sb([P, S])
        self.hc = Ring([sb([P, S]) for _ in range(2)])
        self.y = sb([P, DB, S])
        self.x_free = self.y_free = None
        self.done = False


def state_space(core, A, Z, b):
    st, w, banks = Z.st, core.w, Z.banks
    while Z.x_ready is None:
        yield
    for m in range(2 * DB):
        bank, free, slot = banks.take()
        t = st.pe(lambda e: e.matmul(bank[:, :], w["in_proj_w"][:, m * P:(m + 1) * P], A.x_chan[:, :], start=True, stop=True), Z.x_ready, free)
        if m == 2 * DB - 1:
            Z.x_free = t
        if m >= DB:
            t = st.act(lambda e: e.activation(Z.sz[:, m - DB, :], bank[:, :], ACT.Silu), t)
            banks.read_by(slot, t)
            continue
        raw, raw_free, raw_slot = Z.raw.take()
        t = st.act(lambda e: e.activation(raw[:, 3:], bank[:, :], ACT.Copy), t, raw_free, Z.zeroed)
        banks.read_by(slot, t)
        cw, xc = w["conv1"], Z.xc[:, m, :]
        t = st.dve(lambda e: e.tensor_scalar(xc, raw[:, 3:3 + S], cw[:, m, 3:4], w["conv1_b"][:, m:m + 1], ALU.mult, ALU.add), t)
        for j in (2, 1, 0):
            t = st.dve(lambda e: e.scalar_tensor_tensor(out=xc, in0=raw[:, j:j + S], scalar=cw[:, m, j:j + 1], in1=xc, op0=ALU.mult, op1=ALU.add))
        Z.raw.read_by(raw_slot, t)
        t_c = st.act(lambda e: e.activation(xc, xc, ACT.Silu), t)
        yield
    for dst, cols in ((Z.dt_in, slice(0, DTR)), (Z.bc, slice(DTR, DTR + 2 * DS))):
        bank, free, slot = banks.take()
        n = cols.stop - cols.start
        for k in range(DB):
            t = st.pe(lambda e: e.matmul(bank[0:n, :], w["x_proj_w"][:, k, cols], Z.xc[:, k, :], start=(k == 0), stop=(k == DB - 1)), t_c, free)
        t_bc = st.act(lambda e: e.activation(dst[:, :], bank[0:n, :], ACT.Copy), t)
        banks.read_by(slot, t_bc)
    for m in range(DB):
        bank, free, slot = banks.take()
        t = st.pe(lambda e: e.matmul(bank[:, :], w["dt_w"][:, m * P:(m + 1) * P], Z.dt_in[:, :], start=True, stop=True), t_bc, free)
        t = st.act(lambda e: e.activation(Z.dt[:, m, :], bank[:, :], ACT.Identity, bias=w["dt_b"][:, m:m + 1]), t)
        banks.read_by(slot, t)
        t = softplus_parts(st, Z.dt[:, m, :], Z.tmp[:, m, :], Z.tmp[:, m, :], t)
        t_dt = st.dve(lambda e: e.scalar_tensor_tensor(out=Z.dt[:, m, :], in0=Z.dt[:, m, :], scalar=0.0, in1=Z.tmp[:, m, :], op0=ALU.max, op1=ALU.add), t)
        st.dve(lambda e: e.tensor_tensor(Z.dtx[:, m, :], Z.dt[:, m, :], Z.xc[:, m, :], ALU.mult))
        yield
    for m in range(DB):
        t_y = st.act(lambda e: e.activation(Z.y[:, m, :], Z.xc[:, m, :], ACT.Identity, scale=w["d_param"][:, m:m + 1]), Z.y_free)
    for n in range(DS):
        bcast = []
        for r in (n, DS + n):
            bank, free, slot = banks.take()
            t = st.pe(lambda e: e.matmul(bank[:, :], core.ident[0:2 * DS, r:r + 1].to_broadcast([2 * DS, P]), Z.bc[:, :], start=True, stop=True),
                      t_bc, free)
            bcast.append((bank, slot, t))
        (bb, bslot, t_b), (cb, cslot, t_c) = bcast
        for m in range(DB):
            da, da_free, da_slot = Z.da.take()
            t_a = st.act(lambda e: e.activation(da[:, :], Z.dt[:, m, :], ACT.Exp, scale=core.neg_a1[:, m, n:n + 1]), t_dt, da_free, chain=False)
            hc, hc_free, hc_slot = Z.hc.take()
            t = st.dve(lambda e: e.tensor_tensor(Z.h[:, :], bb[:, :], Z.dtx[:, m, :], ALU.mult), t_b)
            if m == DB - 1:
                banks.read_by(bslot, t)
            t = st.dve(lambda e: e.tensor_tensor_scan(Z.h[:, :], da[:, :], Z.h[:, :], 0.0, ALU.mult, ALU.add), t_a)
            Z.da.read_by(da_slot, t)
            t = st.dve(lambda e: e.tensor_tensor(hc[:, :], cb[:, :], Z.h[:, :], ALU.mult), t_c, hc_free)
            if m == DB - 1:
                banks.read_by(cslot, t)
            t = st.pool(lambda e: e.tensor_tensor(Z.y[:, m, :], Z.y[:, m, :], hc[:, :], ALU.add), t, t_y)
            Z.hc.read_by(hc_slot, t)
        yield
    for m in range(DB):
        t = st.dve(lambda e: e.tensor_tensor(Z.y[:, m, :], Z.y[:, m, :], Z.sz[:, m, :], ALU.mult), t)
    Z.y_ready = t
    Z.done = True



class Selection:
    def __init__(self, sb, core, nt, bank):
        self.st, self.bank, self.nt = Stream(core, "sel"), bank, nt
        self.avail = sb([P, nt])
        self.sm = sb([P, nt])
        self.cmp = sb([P, WAYS - 1, nt])
        self.cnt = sb([P, WAYS - 1])
        self.th = sb([P, WAYS + 1])
        self.ge = sb([P, WAYS + 1])
        self.tmp = sb([P, WAYS + 1])
        self.step = sb([P, 1])
        self.lohi = sb([P, 2])
        self.sure = sb([P, nt])
        self.tie = sb([P, nt])
        self.rank = sb([P, nt])
        self.need = sb([P, 1])
        self.picks = sb([P, E, nt])
        self.excl = sb([P, E, nt + 1])
        self.pos = sb([P, E, nt])
        self.slot_f = sb([P, nt])
        self.done = None


def prefix_ranks(core, G, src, n, out, *waits):
    st, nt, bank = G.st, G.nt, G.bank
    cols = src.rearrange("p n t -> p (n t)")
    t = st.pe(lambda e: e.matmul(bank[:, 0:n * nt], core.ones[:, :], cols, start=True, stop=True), *waits)
    for k in range(n):
        t = st.dve(lambda e: e.tensor_tensor_scan(G.excl[:, k, 1:nt + 1], core.ones[:, 0:nt], bank[:, k * nt:(k + 1) * nt], 0.0, ALU.mult, ALU.add), t)
    t = st.pe(lambda e: e.matmul(bank[:, 0:n * nt], core.mask_strict[:, :], cols, start=True, stop=True), t)
    return st.dve(lambda e: e.tensor_tensor(out, bank[:, 0:n * nt].rearrange("p (n t) -> p n t", n=n), G.excl[:, 0:n, 0:nt], ALU.add), t)


def selection(core, G, scores, cap):
    st, nt, bank = G.st, G.nt, G.bank
    st.dve(lambda e: e.memset(G.avail[:, :], 1.0))
    st.dve(lambda e: e.memset(G.excl[:, :, :], 0.0))
    st.dve(lambda e: e.memset(G.ge[:, 0:1], 1.0))
    st.dve(lambda e: e.memset(G.ge[:, WAYS:WAYS + 1], 0.0))
    flat_scores = scores[:, :, :].rearrange("p e t -> p (e t)")
    st.dve(lambda e: e.tensor_reduce(G.lohi[:, 0:1], flat_scores, AX.X, ALU.max), core.xhat_ready)
    t = st.dve(lambda e: e.tensor_reduce(G.lohi[:, 1:2], flat_scores, AX.X, ALU.min))
    t = st.dve(lambda e: e.tensor_scalar(G.lohi[:, 1:2], G.lohi[:, 1:2], -1.0, None, ALU.mult))
    t = st.dve(lambda e: e.tensor_reduce(G.step[:, :], G.lohi[:, :], AX.X, ALU.max))
    t = st.pool(lambda e: e.partition_all_reduce(G.need[:, :], G.step[:, :], P, bass.bass_isa.ReduceOp.max), t)
    t = st.dve(lambda e: e.tensor_scalar(G.lohi[:, 1:2], G.need[:, :], 1.001, 1e-30, ALU.mult, ALU.add), t)
    t = st.dve(lambda e: e.tensor_scalar(G.lohi[:, 0:1], G.lohi[:, 1:2], -1.0, None, ALU.mult))
    yield
    for x in range(E):
        st.dve(lambda e: e.tensor_scalar(G.tie[:, :], G.avail[:, :], 1.0, SCORE_BIG, ALU.subtract, ALU.mult))
        st.dve(lambda e: e.tensor_tensor(G.sm[:, :], scores[:, x, :], G.avail[:, :], ALU.mult))
        st.dve(lambda e: e.tensor_tensor(G.sm[:, :], G.sm[:, :], G.tie[:, :], ALU.add))
        st.dve(lambda e: e.tensor_copy(G.th[:, 0:1], G.lohi[:, 0:1]), chain=False)
        st.dve(lambda e: e.tensor_copy(G.th[:, WAYS:WAYS + 1], G.lohi[:, 1:2]), chain=False)
        for _ in range(ROUNDS):
            st.dve(lambda e: e.tensor_scalar(G.step[:, :], G.th[:, WAYS:WAYS + 1], G.th[:, 0:1], 1.0 / WAYS, ALU.subtract, ALU.mult))
            st.dve(lambda e: e.tensor_scalar(G.th[:, 1:WAYS], core.iota[:, 1:WAYS], G.step[:, 0:1], G.th[:, 0:1], ALU.mult, ALU.add))
            st.dve(lambda e: e.tensor_tensor(G.cmp[:, :, :], G.sm[:, :].unsqueeze(1).to_broadcast([P, WAYS - 1, nt]),
                                             G.th[:, 1:WAYS].unsqueeze(2).to_broadcast([P, WAYS - 1, nt]), ALU.is_ge))
            t = st.dve(lambda e: e.tensor_reduce(G.cnt[:, :], G.cmp[:, :, :], AX.X, ALU.add))
            t = st.pe(lambda e: e.matmul(bank[:, 0:WAYS - 1], core.ones[:, :], G.cnt[:, :], start=True, stop=True), t)
            yield
            st.dve(lambda e: e.tensor_scalar(G.ge[:, 1:WAYS], bank[:, 0:WAYS - 1], float(cap), None, ALU.is_ge), t)
            st.dve(lambda e: e.scalar_tensor_tensor(out=G.tmp[:, :], in0=G.ge[:, :], scalar=SCORE_BIG, in1=G.th[:, :], op0=ALU.mult, op1=ALU.add))
            st.dve(lambda e: e.tensor_reduce(G.need[:, :], G.tmp[:, :], AX.X, ALU.min))
            st.dve(lambda e: e.tensor_scalar(G.tmp[:, :], G.ge[:, :], 1.0, SCORE_BIG, ALU.subtract, ALU.mult))
            st.dve(lambda e: e.tensor_tensor(G.tmp[:, :], G.tmp[:, :], G.th[:, :], ALU.add))
            st.dve(lambda e: e.tensor_reduce(G.th[:, 0:1], G.tmp[:, :], AX.X, ALU.max))
            st.dve(lambda e: e.tensor_copy(G.th[:, WAYS:WAYS + 1], G.need[:, :]))
            yield
        st.dve(lambda e: e.tensor_scalar(G.sure[:, :], G.sm[:, :], G.th[:, WAYS:WAYS + 1], None, ALU.is_ge))
        st.dve(lambda e: e.tensor_scalar(G.tie[:, :], G.sm[:, :], G.th[:, 0:1], None, ALU.is_ge))
        st.dve(lambda e: e.tensor_tensor(G.tie[:, :], G.tie[:, :], G.sure[:, :], ALU.subtract))
        t = st.dve(lambda e: e.tensor_reduce(G.step[:, :], G.sure[:, :], AX.X, ALU.add))
        t = st.pe(lambda e: e.matmul(bank[:, 0:1], core.ones[:, :], G.step[:, :], start=True, stop=True), t)
        t = st.dve(lambda e: e.tensor_scalar(G.need[:, :], bank[:, 0:1], -1.0, float(cap), ALU.mult, ALU.add), t)
        prefix_ranks(core, G, G.tie[:, :].unsqueeze(1), 1, G.rank[:, :].unsqueeze(1), t)
        st.dve(lambda e: e.tensor_scalar(G.rank[:, :], G.rank[:, :], G.need[:, 0:1], None, ALU.is_lt))
        st.dve(lambda e: e.tensor_tensor(G.tie[:, :], G.tie[:, :], G.rank[:, :], ALU.mult))
        st.dve(lambda e: e.tensor_tensor(G.picks[:, x, :], G.tie[:, :], G.sure[:, :], ALU.add))
        t = st.dve(lambda e: e.tensor_tensor(G.avail[:, :], G.avail[:, :], G.picks[:, x, :], ALU.subtract))
        yield
    prefix_ranks(core, G, G.picks[:, :, :], E, G.pos[:, :, :], t)
    for x in range(E):
        st.dve(lambda e: e.tensor_scalar(G.pos[:, x, :], G.pos[:, x, :], float(x * cap), None, ALU.add), chain=(x == 0))
    st.dve(lambda e: e.tensor_tensor(G.pos[:, :, :], G.pos[:, :, :], G.picks[:, :, :], ALU.mult))
    st.dve(lambda e: e.tensor_reduce(G.slot_f[:, :], G.pos[:, :, :].rearrange("p e t -> p t e"), AX.X, ALU.add))
    G.done = st.dve(lambda e: e.tensor_copy(core.slot_i[:, :], G.slot_f[:, :]))


class Expert1:
    def __init__(self, sb, core, n, ct, banks):
        self.st, self.banks = Stream(core, f"bx{n}"), banks
        self.tok = sb([P, ct, H])
        self.n_tok = sb([P, ct, H])
        self.n_chan = sb([P, ct * P])
        self.hid = sb([P, FB, ct * P])
        self.out = sb([P, ct, H])
        self.work = (sb([P, ct, 6]), sb([P, ct, 2]), sb([P, ct]))
        self.load, self.store = Dma(core, f"bx{n}_load"), Dma(core, f"bx{n}_store")
        self.tok_free = self.stored = None


def expert1(core, X, routed, answered, x, ct, scattered):
    st, w, banks = X.st, core.w, X.banks
    rows = routed[x * ct * P:(x + 1) * ct * P, :].rearrange("(c p) h -> p c h", p=P)
    t = X.load.start(X.tok[:, :, :], rows, scattered, X.tok_free)
    t = layer_norm_tok(st, X.tok, X.n_tok, X.work, t, n=ct)
    X.tok_free = t
    t_n = transpose_tiles(st, banks, X.n_tok, X.n_chan, w["m_ln_g"][:, 0:1], w["m_ln_b"][:, 0:1], t, n=ct)
    yield
    for m in range(FB):
        bank, free, slot = banks.take()
        t = st.pe(lambda e: e.matmul(bank[:, 0:ct * P], w["m_w1"][:, x, m * P:(m + 1) * P], X.n_chan[:, :], start=True, stop=True), t_n, free)
        t_h = st.act(lambda e: e.activation(X.hid[:, m, :], bank[:, 0:ct * P], ACT.Gelu_apprx_tanh, bias=w["m_b1"][:, x, m:m + 1]), t,
                     chain=(m == 0))
        banks.read_by(slot, t_h)
    yield
    bank, free, slot = banks.take()
    for c in range(ct):
        for m in range(FB):
            t = st.pe(lambda e: e.matmul(bank[:, c * P:(c + 1) * P], X.hid[:, m, c * P:(c + 1) * P], w["m_w2"][:, x, m, :],
                                         start=(m == 0), stop=(m == FB - 1)), t_h, free)
    t = st.dve(lambda e: e.tensor_tensor(X.out[:, :, :], bank[:, 0:ct * P].rearrange("p (c h) -> p c h", c=ct),
                                         w["m_b2"][:, x, :].unsqueeze(1).to_broadcast([P, ct, H]), ALU.add), t, X.stored)
    banks.read_by(slot, t)
    rows_out = answered[x * ct * P:(x + 1) * ct * P, :].rearrange("(c p) h -> p c h", p=P)
    X.stored = X.store.start(rows_out, X.out[:, :, :], t)
    yield



def layer1_weights(core, ins, dma):
    w, nc = core.w, core.nc

    def weight(name, shape):
        w[name] = core.sb(name, shape)
        dma.start(w[name][tuple(slice(None) for _ in shape)], ins[name])

    def row(name, n):
        w[name] = core.sb(name, [P, n])
        dma.start(w[name][:, :], ins[name].partition_broadcast(P))
    for name in ("pre_w", "pre_b", "mid_w", "mid_b", "m_ln_g", "m_ln_b"):
        weight(name, [P, 1])
    weight("centroids", [P, E])
    weight("q_w", [P, 4 * P])
    weight("q_b", [P, 4])
    weight("k_w", [P, 4 * P])
    weight("k_b", [P, 4])
    weight("v_w", [P, H])
    row("v_b", H)
    weight("o_w", [P, H])
    row("o_b", H)
    row("mix", H)
    weight("ssm_out_w", [P, DB, H])
    weight("in_proj_w", [P, 2 * DI])
    weight("conv1", [P, DB, 4])
    weight("conv1_b", [P, DB])
    weight("x_proj_w", [P, DB, DTR + 2 * DS])
    weight("dt_w", [DTR, DI])
    weight("dt_b", [P, DB])
    weight("a_log1", [P, DB, DS])
    weight("d_param", [P, DB])
    weight("ffn_w1", [P, FF])
    weight("ffn_b1", [P, FB])
    weight("ffn_w2", [P, FB, H])
    row("ffn_b2", H)
    loaded = (dma.sem, dma.count)
    st = Stream(core, "prep1")
    core.neg_a1 = core.sb("neg_a1", [P, DB, DS])
    t = st.act(lambda e: e.activation(core.neg_a1[:, :, :], w["a_log1"][:, :, :], ACT.Exp), loaded)
    st.dve(lambda e: e.tensor_scalar(core.neg_a1[:, :, :], core.neg_a1[:, :, :], -1.0, None, ALU.mult), t)
    t = st.act(lambda e: e.activation(w["mix"][:, :], w["mix"][:, :], ACT.Exp, scale=-1.0), chain=False)
    st.dve(lambda e: e.tensor_scalar(w["mix"][:, :], w["mix"][:, :], 1.0, None, ALU.add), t)
    st.dve(lambda e: e.reciprocal(w["mix"][:, :], w["mix"][:, :]))
    st.dve(lambda e: e.tensor_tensor(w["o_w"][:, :], w["o_w"][:, :], w["mix"][:, :], ALU.mult))
    st.dve(lambda e: e.tensor_tensor(w["o_b"][:, :], w["o_b"][:, :], w["mix"][:, :], ALU.mult))
    st.dve(lambda e: e.tensor_scalar(w["mix"][:, :], w["mix"][:, :], -1.0, 1.0, ALU.mult, ALU.add))
    st.dve(lambda e: e.tensor_tensor(w["ssm_out_w"][:, :, :], w["ssm_out_w"][:, :, :],
                                     w["mix"][:, :].unsqueeze(1).to_broadcast([P, DB, H]), ALU.mult))
    return loaded


def layer1_norms(core, T, x_tok, nb, scores, banks):
    w, st = core.w, T
    core.xhat_ready = []
    for b in range(nb):
        rows = slice(b * CH, (b + 1) * CH)
        xhat = core.xhat_chan[:, b * S:(b + 1) * S]
        t = layer_norm_tok(st, x_tok[:, rows, :], core.xn1[:, rows, :], core.ln_work1)
        t = layer_norm_tok(st, core.xn1[:, rows, :], core.n_tok1, core.ln_work1)
        t = transpose_tiles(st, banks, core.n_tok1, xhat, None, None, t)
        core.xhat_ready.append(t)
        t = st.dve(lambda e: e.tensor_scalar(core.n_chan1[:, :], xhat, w["m_ln_g"][:, 0:1], w["m_ln_b"][:, 0:1], ALU.mult, ALU.add), t)
        bank, free, slot = banks.take()
        for c in range(CH):
            t = st.pe(lambda e: e.matmul(bank[:, c * E:(c + 1) * E], core.n_chan1[:, c * P:(c + 1) * P], w["centroids"][:, :],
                                         start=True, stop=True), t, free)
        t = st.dve(lambda e: e.tensor_copy(scores[:, :, rows], bank[:, 0:CH * E].rearrange("p (c e) -> p e c", c=CH)), t)
        banks.read_by(slot, t)


def layer1(core, ctx, ins, outs, x_tok, psum, bank, dram, nb, dbg):
    nc, w, nt = core.nc, core.w, nb * CH
    names = iter(range(1000))

    def sb(shape):
        return core.sb(f"l1_{next(names)}", shape)
    core.xn1 = sb([P, nt, H])
    core.s1 = sb([P, nt, H])
    core.slot_i = core.sb("slot_i", [P, nt], I32)
    scores = sb([P, E, nt])
    G = Selection(sb, core, nt, bank[0])
    with ExitStack() as inner:
        core.ctx = inner
        dma = Dma(core, "weights1")
        layer1_weights(core, ins, dma)
        core.xhat_chan = sb([P, nt * P])
        core.ln_work1 = (sb([P, CH, 6]), sb([P, CH, 2]), sb([P, CH]))
        core.n_tok1 = sb([P, CH, H])
        core.n_chan1 = sb([P, S])
        A = Attention(sb, core, psum[:, 0:4, :], Ring(bank[4:6]))
        Z = StateSpace(sb, core, Ring(bank[6:8]))
        core.fence()
        layer1_norms(core, Stream(core, "norm1"), x_tok, nb, scores, Ring(bank[0:4]))
        core.fence()
        for _ in selection(core, G, scores, nb * S // E):
            pass
        core.fence()
        A.x_free = None
        for b in range(nb):
            Z.done, Z.x_ready = False, None
            interleave([attention(core, A, Z, b), state_space(core, A, Z, b)])
        core.fence()
    with ExitStack() as inner:
        core.ctx = inner
        ct = nt // E
        dma = Dma(core, "weights2")

        def weight(name, shape):
            w[name] = core.sb(name, shape)
            return dma.start(w[name][tuple(slice(None) for _ in shape)], ins[name])
        weight("m_w1", [P, E, F])
        weight("m_b1", [P, E, FB])
        weight("m_w2", [P, E, FB, H])
        w["m_b2"] = core.sb("m_b2", [P, E, H])
        t_w = dma.start(w["m_b2"][:, :, :], ins["m_b2"].partition_broadcast(P))
        weight("m_g", [P, 1])
        t_w = weight("m_b", [P, 1])
        w["m_ln_g"], w["m_ln_b"] = w["m_g"], w["m_b"]
        hg = sb([P, nt, H])
        X = [Expert1(sb, core, n, ct, Ring(bank[4 * n:4 * n + 4])) for n in range(2)]
        move = Dma(core, "route")
        for n in range(nt):
            nc.gpsimd.indirect_dma_start(out=dram["routed"], out_offset=bass.IndirectOffsetOnAxis(ap=core.slot_i[:, n:n + 1], axis=0),
                                         in_=core.xn1[:, n, :], in_offset=None).then_inc(move.sem, 16)
            move.count += 16
        scattered = (move.sem, move.count)

        def line(n):
            for x in range(n, E, 2):
                yield from expert1(core, X[n], dram["routed"], dram["answered"], x, ct, [scattered, t_w])
        interleave([line(0), line(1)])
        core.wait("pool", nc.gpsimd, [X[0].stored, X[1].stored])
        for n in range(nt):
            nc.gpsimd.indirect_dma_start(out=hg[:, n, :], out_offset=None, in_=dram["answered"],
                                         in_offset=bass.IndirectOffsetOnAxis(ap=core.slot_i[:, n:n + 1], axis=0)).then_inc(move.sem, 16)
            move.count += 16
        st = Stream(core, "final")
        store = Dma(core, "store_out")
        for b in range(nb):
            rows = slice(b * CH, (b + 1) * CH)

            def n2(a):
                return a[:, rows, :].rearrange("p c h -> p (c h)")
            t = st.dve(lambda e: e.tensor_tensor(n2(hg), n2(hg), n2(core.xn1), ALU.add), (move.sem, move.count), chain=False)
            t = st.act(lambda e: e.activation(n2(hg), n2(hg), ACT.Silu), t, chain=False)
            t = st.dve(lambda e: e.tensor_tensor(n2(core.s1), n2(core.s1), n2(hg), ALU.mult), t, chain=False) if dbg not in ("s1", "g1") else t
            t = st.dve(lambda e: e.tensor_tensor(n2(x_tok), n2(x_tok), n2(core.s1), ALU.add), t)
            src = {"s1": core.s1, "g1": hg}.get(dbg, x_tok)
            t = store.start(outs["out"][b].rearrange("(c p) h -> p c h", p=P), src[:, rows, :], t)
        core.fence()


def build(nc, ins, outs, nb, dbg=None):
    with ExitStack() as ctx:
        core = Core(nc, ctx)
        const_done = build_constants(core)
        load = {}
        nt = nb * CH
        w = core.w = {}
        wl = Dma(core, "weights")

        def weight(name, shape):
            w[name] = core.sb(name, shape)
            wl.start(w[name][tuple(slice(None) for _ in shape)], ins[name])
        x_tok = core.sb("x_tok", [P, nt, H])
        psum = ctx.enter_context(nc.psum_tensor("psum", [P, 8, 512], F32))
        layer0_ctx = ctx.enter_context(ExitStack())
        core.ctx = layer0_ctx
        x_dma = [Dma(core, f"x{b}") for b in range(nb)]
        x_ready = [x_dma[b].start(x_tok[:, b * CH:(b + 1) * CH, :], ins["x"][b].rearrange("(c p) h -> p c h", p=P)) for b in range(nb)]
        weight("w_qkv", [P, 4 * NKH * DK])
        weight("w_z", [P, NVH * DK])
        weight("w_a", [P, NVH])
        weight("w_b", [P, NVH])
        weight("dt_bias", [NVH, 1])
        weight("a_log", [NVH, 1])
        weight("conv0", [P, 16, 4])
        weight("w_out", [P, 2 * NG, H])
        weight("norm_w", [P, 1])
        weight("up_w", [P, E, F])
        weight("up_b", [P, E, FB])
        weight("down_w", [P, E, FB, H])
        weight("down_b", [E, H])
        weight("router_w", [P, E])
        weight("f_ln_g", [P, 1])
        weight("f_ln_b", [P, 1])
        weight("spec0_w", [P, 2, FB, F])
        weight("spec1a_w", [P, 2, FB, F // 2])
        weight("spec1b_w", [P, 2, FB // 2, F])
        weight("spec2_w", [P, 2, FB, F])
        for name in ("spec0_b", "ln0_g", "ln0_b", "spec1b_b", "ln1_g", "ln1_b", "spec2_b"):
            weight(name, [P, 2, FB])
        weight("spec1a_b", [P, 2, FB // 2])
        w_ready = (wl.sem, wl.count)
        prep = Stream(core, "prep")
        core.neg_exp_a0 = core.sb("neg_exp_a0", [NVH, 1])
        t = prep.act(lambda e: e.activation(core.neg_exp_a0[:, :], w["a_log"][:, :], ACT.Exp), w_ready, const_done)
        t = prep.dve(lambda e: e.tensor_scalar(core.neg_exp_a0[:, :], core.neg_exp_a0[:, :], -1.0, None, ALU.mult), t)
        t = prep.dve(lambda e: e.tensor_scalar(w["w_out"][:, :, :], w["w_out"][:, :, :], w["norm_w"][:, 0:1], None, ALU.mult))
        core.prep_done = t
        dram = {"gate": nc.dram_tensor("gate_scratch", [nb, NVH, S], F32).ap(),
                "routed": nc.dram_tensor("routed", [nt * P, H], F32).ap(),
                "answered": nc.dram_tensor("answered", [nt * P, H], F32).ap()}
        bank = [psum[:, i, :] for i in range(8)]
        sums = core.sb("sums", [P, 2 * FB])
        center_weights(core, prep, w["spec0_w"], w["spec0_b"], FB, sums, bank[0])
        center_weights(core, prep, w["spec1b_w"], w["spec1b_b"], 2, sums, bank[0])
        L = Layer0(core, dram)
        arena = Arena(core, "arena", 19100)
        rings = [Ring(bank[0:4]), Ring(bank[4:8])]
        D = [DeltaGroup(arena, core, n, rings[n]) for n in range(2)]
        arena.reset()
        M = Mixture0(arena, core)
        X = [ExpertLine(arena, core, n, rings[n]) for n in range(2)]
        L.xn_free = L.gate_stored = None
        for b in range(nb):
            core.fence()
            L.b = b
            for d in D:
                d.fresh()
            x_b = x_tok[:, b * CH:(b + 1) * CH, :]
            layer0_prologue(core, L, rings[0], x_b, [x_ready[b]])

            def line(n):
                for g in (n, n + 2):
                    yield from delta_group(core, L, D[n], b, g)
            interleave([line(0), line(1)])
            core.fence()
            mixture0(core, L, M, X, rings[0])
            st = M.st
            n2 = lambda a: a[:, :, :].rearrange("p c h -> p (c h)")
            t = st.act(lambda e: e.activation(n2(M.acc), n2(M.acc), ACT.Silu), M.acc_done)
            if dbg == "g0":
                st.dve(lambda e: e.tensor_copy(n2(x_b), n2(M.acc)), t)
                continue
            t = st.dve(lambda e: e.tensor_tensor(n2(M.acc), n2(M.acc), n2(L.s_tok), ALU.mult), t)
            t = st.dve(lambda e: e.tensor_tensor(n2(x_b), n2(x_b), n2(M.acc), ALU.add))
        if dbg in ("x1", "g0"):
            core.fence()
            d = Dma(core, "dbg")
            for b in range(nb):
                t2 = d.start(outs["out"][b].rearrange("(c p) h -> p c h", p=P), x_tok[:, b * CH:(b + 1) * CH, :])
            core.wait("sp", nc.sync, [t2])
            return
        core.fence()
        layer0_ctx.close()
        layer1_ctx = ctx.enter_context(ExitStack())
        core.ctx = layer1_ctx
        layer1(core, layer1_ctx, ins, outs, x_tok, psum, bank, dram, nb, dbg)


def host_layout(x):
    a = {}
    heads = np.array(SLOT_HEADS)
    a["x"] = x["L0_attn_hidden_states"]
    a["w_qkv"] = x["L0_attn_W_qkv"].T
    a["w_z"] = x["L0_attn_W_z"].reshape(NVH, DK, H)[heads].reshape(NVH * DK, H).T
    a["w_a"] = x["L0_attn_W_a"][heads].T
    a["w_b"] = x["L0_attn_W_b"][heads].T
    a["dt_bias"] = x["L0_attn_dt_bias"][heads].reshape(NVH, 1)
    a["a_log"] = x["L0_attn_A_log"][heads].reshape(NVH, 1)
    a["conv0"] = x["L0_attn_conv_w"].reshape(16, P, 4).transpose(1, 0, 2)
    a["w_out"] = x["L0_attn_W_out"].reshape(H, NVH, DK)[:, heads].reshape(H, 2 * NG, P).transpose(2, 1, 0)
    a["norm_w"] = np.concatenate([x["L0_attn_norm_weight"]] * 2).reshape(P, 1)
    f = {k[7:]: v for k, v in x.items() if k.startswith("L0_ffn_")}
    a["up_w"] = f["up_W"].transpose(1, 0, 2)
    a["up_b"] = f["up_b"].reshape(E, FB, P).transpose(2, 0, 1)
    a["down_w"] = f["down_W"].reshape(E, FB, P, H).transpose(2, 0, 1, 3)
    a["down_b"] = f["down_b"]
    a["router_w"] = f["router_w"]
    a["f_ln_g"] = f["ln_g"].reshape(P, 1)
    a["f_ln_b"] = f["ln_b"].reshape(P, 1)
    for name in ("spec0_W", "spec1a_W", "spec1b_W", "spec2_W"):
        s, k, n = f[name].shape
        a[name.replace("W", "w")] = f[name].reshape(s, k // P, P, n).transpose(2, 0, 1, 3)
    for name in ("spec0_b", "ln0_g", "ln0_b", "spec1a_b", "spec1b_b", "ln1_g", "ln1_b", "spec2_b"):
        a[name] = f[name].reshape(2, -1, P).transpose(2, 0, 1)
    f = {k[8:]: v for k, v in x.items() if k.startswith("L1_attn_")}
    for name, source in (("pre_w", "ln1_w"), ("pre_b", "ln1_b"), ("mid_w", "ln2_w"), ("mid_b", "ln2_b")):
        a[name] = f[source].reshape(P, 1)
    for name in ("q", "k"):
        wide = np.zeros((H, 4, 4, 32), f[name + "_w"].dtype)
        wide[:, :, :, :HD] = f[name + "_w"].reshape(H, 4, 4, HD)
        a[name + "_w"] = wide.reshape(H, 4 * P)
        wide = np.zeros((4, 4, 32), f[name + "_b"].dtype)
        wide[:, :, :HD] = f[name + "_b"].reshape(4, 4, HD)
        a[name + "_b"] = wide.reshape(4, P).T
    for name in ("v_w", "v_b", "o_w", "o_b", "in_proj_w", "dt_w", "ffn_w1", "ffn_b2"):
        a[name] = f[name]
    a["mix"] = f["mix_weight"]
    a["ssm_out_w"] = f["ssm_out_w"].reshape(DB, P, H).transpose(1, 0, 2)
    a["conv1"] = f["conv_w"].reshape(DB, P, 4).transpose(1, 0, 2)
    a["conv1_b"] = f["conv_b"].reshape(DB, P).T
    a["x_proj_w"] = f["x_proj_w"].reshape(DB, P, DTR + 2 * DS).transpose(1, 0, 2)
    a["dt_b"] = f["dt_b"].reshape(DB, P).T
    a["a_log1"] = f["A_log"].reshape(DB, P, DS).transpose(1, 0, 2)
    a["d_param"] = f["D_param"].reshape(DB, P).T
    a["ffn_b1"] = f["ffn_b1"].reshape(FB, P).T
    a["ffn_w2"] = f["ffn_w2"].reshape(FB, P, H).transpose(1, 0, 2)
    f = {k[7:]: v for k, v in x.items() if k.startswith("L1_ffn_")}
    a["centroids"] = f["centroids"].T
    a["m_ln_g"] = a["m_g"] = f["ln_g"].reshape(P, 1)
    a["m_ln_b"] = a["m_b"] = f["ln_b"].reshape(P, 1)
    a["m_w1"] = f["w1"].transpose(1, 0, 2)
    a["m_b1"] = f["b1"].reshape(E, FB, P).transpose(2, 0, 1)
    a["m_w2"] = f["w2"].reshape(E, FB, P, H).transpose(2, 0, 1, 3)
    a["m_b2"] = f["b2"]
    return {k: np.ascontiguousarray(v) for k, v in a.items()}


def kernel(**inputs):
    import concourse.bacc as bacc
    from concourse.bass_utils import run_bass_kernel_spmd

    arrays = {f"in_{k}": v for k, v in host_layout({k: np.asarray(v) for k, v in inputs.items()}).items()}
    nb = arrays["in_x"].shape[0]
    nc = bacc.Bacc("TRN2", target_bir_lowering=False, num_devices=1)
    ins = {k[3:]: nc.dram_tensor(k, v.shape, F32, kind="ExternalInput").ap() for k, v in arrays.items()}
    outs = {"out": nc.dram_tensor("out", [nb, S, H], F32, kind="ExternalOutput").ap()}
    build(nc, ins, outs, nb)
    return run_bass_kernel_spmd(nc, [arrays], core_ids=[0]).results[0]["out"]
```

```python
from contextlib import ExitStack

import concourse.bass as bass
import numpy as np
from concourse import mybir

F32 = mybir.dt.float32
I32 = mybir.dt.int32
BF16 = mybir.dt.bfloat16
ALU = mybir.AluOpType
ACT = mybir.ActivationFunctionType
AX = mybir.AxisListType

P = 128
H = 128
S = 512
CH = S // P
NVH, NKH, DK = 16, 8, 64
NG = 4
LEVELS = 7
E = 8
F = 512
FB = F // P
NH1, HD = 16, 8
DI, DS, DTR = 256, 16, 8
DB = DI // P
FF = 512
SCORE_BIG = 1e30
ROUNDS, WAYS = 8, 16
DELTA_LINES = 3
ATTENTION_STEPS = 4
LN_EPS = 1e-5
RMS_EPS = 1e-6
SLOT_HEADS = [4 * g + s for g in range(NG) for s in (0, 2, 1, 3)]


class Arena:

    def __init__(self, core, name, columns):
        self.whole, self.columns, self.at = core.sb(name, [P, columns]), columns, 0

    def reset(self):
        self.at = 0

    def __call__(self, shape):
        n = int(np.prod(shape[1:]))
        assert self.at + n <= self.columns, (self.at, n, self.columns)
        view = self.whole[0:shape[0], self.at:self.at + n]
        self.at += n
        names = "abcd"[:len(shape) - 1]
        if len(shape) == 2:
            return view
        return view.rearrange(f"p ({' '.join(names)}) -> p {' '.join(names)}", **dict(zip(names, shape[1:])))


def flat(tickets):
    for t in tickets:
        if t is None:
            continue
        if isinstance(t, list):
            yield from flat(t)
        else:
            yield t


class Core:

    def __init__(self, nc, ctx):
        self.nc, self.ctx = nc, ctx
        self.seen = {}
        self.streams, self.dmas = [], []

    def sb(self, name, shape, dtype=F32):
        return self.ctx.enter_context(self.nc.sbuf_tensor(name, shape, dtype))

    def sem(self, name):
        return self.ctx.enter_context(self.nc.semaphore(name))

    def fence(self):
        last = [(st.sems[who], st.count[who]) for st in self.streams for who in st.sems]
        last += [(d.sem, d.count) for d in self.dmas if d.count]
        nc = self.nc
        for name, engine in (("pe", nc.tensor), ("act", nc.scalar), ("dve", nc.vector), ("pool", nc.gpsimd), ("sp", nc.sync)):
            self.wait(name, engine, last)

    def wait(self, name, engine, tickets):
        for sem, value in flat(tickets):
            key = (name, id(sem))
            if self.seen.get(key, 0) < value:
                self.seen[key] = value
                engine.wait_ge(sem, value)


class Stream:

    def __init__(self, core, name):
        self.core, self.name = core, name
        core.streams.append(self)
        nc = core.nc
        self.engines = {"pe": nc.tensor, "act": nc.scalar, "dve": nc.vector, "pool": nc.gpsimd}
        self.sems, self.count = {}, {}

    def run(self, who, fn, waits, chain):
        engine = self.engines[who]
        if who not in self.sems:
            self.sems[who] = self.core.sem(f"{self.name}_{who}")
            self.count[who] = 0
        sem = self.sems[who]
        if chain and self.count[who]:
            waits = [*waits, (sem, self.count[who])]
        self.core.wait(who, engine, waits)
        fn(engine).then_inc(sem, 1)
        self.count[who] += 1
        return sem, self.count[who]

    def pe(self, fn, *waits, chain=False):
        return self.run("pe", fn, waits, chain)

    def act(self, fn, *waits, chain=True):
        return self.run("act", fn, waits, chain)

    def dve(self, fn, *waits, chain=True):
        return self.run("dve", fn, waits, chain)

    def pool(self, fn, *waits, chain=True):
        return self.run("pool", fn, waits, chain)


class Dma:

    def __init__(self, core, name):
        self.core, self.sem, self.count = core, core.sem(name), 0
        core.dmas.append(self)

    def start(self, out, in_, *waits, who="sp"):
        engine = {"sp": self.core.nc.sync, "act": self.core.nc.scalar, "pool": self.core.nc.gpsimd}[who]
        self.core.wait(who, engine, waits)
        engine.dma_start(out, in_).then_inc(self.sem, 16)
        self.count += 16
        return self.sem, self.count


class Ring:

    def __init__(self, items):
        self.items, self.readers = items, [[] for _ in items]
        self.released = list(range(len(items)))

    def take(self):
        slot = self.released.pop(0)
        return self.items[slot], self.readers[slot], slot

    def waited(self):
        while not self.released:
            yield

    def read_by(self, slot, *tickets):
        self.readers[slot] = list(tickets)
        self.released.append(slot)


def interleave(lines):
    lines = list(lines)
    while lines:
        for line in list(lines):
            try:
                next(line)
            except StopIteration:
                lines.remove(line)


def paced(line, steps):
    n = 0
    for _ in line:
        n += 1
        if n % steps == 0:
            yield


def layer_norm_tok(st, src, dst, work, *waits, n=CH):
    stats, mv, rstd = work
    for c in range(n):
        t = st.dve(lambda e: e.bn_stats(stats[:, c, :], src[:, c, :]), *waits)
        t = st.dve(lambda e: e.bn_aggr(mv[:, c, :], stats[:, c, :]))
    t = st.act(lambda e: e.activation(rstd[:, 0:n], mv[:, 0:n, 1], ACT.Ln, bias=st.core.eps_ln[:, 0:1]), t)
    t = st.act(lambda e: e.activation(rstd[:, 0:n], rstd[:, 0:n], ACT.Exp, scale=-0.5))
    for c in range(n):
        t = st.dve(lambda e: e.tensor_scalar(dst[:, c, :], src[:, c, :], mv[:, c, 0:1], rstd[:, c:c + 1],
                                             ALU.subtract, ALU.mult), t)
    return t


def transpose_tiles(st, banks, src, dst, scale, bias, *waits, n=CH):
    bank, free, slot = banks.take()
    for c in range(n):
        t = st.pe(lambda e: e.transpose(bank[:, c * P:(c + 1) * P], src[:, c, :], st.core.ident[:, :]), *waits, free)
    if scale is None:
        t = st.act(lambda e: e.activation(dst[:, 0:n * P], bank[:, 0:n * P], ACT.Copy), t, *waits)
    else:
        t = st.act(lambda e: e.activation(dst[:, 0:n * P], bank[:, 0:n * P], ACT.Identity, bias=bias, scale=scale), t, *waits)
    banks.read_by(slot, t)
    return t


def softplus_parts(st, src, neg_abs, out, ready):
    t = st.dve(lambda e: e.scalar_tensor_tensor(out=neg_abs, in0=src, scalar=-1.0, in1=src, op0=ALU.mult, op1=ALU.min), ready)
    t = st.act(lambda e: e.activation(neg_abs, neg_abs, ACT.Exp), t)
    return st.act(lambda e: e.activation(out, neg_abs, ACT.Ln, bias=1.0))


def build_constants(core):
    st = core.const = Stream(core, "const")
    core.ident = core.sb("ident", [P, P])
    core.ones = core.sb("ones", [P, P])
    core.qk_mask = core.sb("qk_mask", [P, P])
    core.kk_mask = core.sb("kk_mask", [P, P])
    core.head_ones = core.sb("head_ones", [P, P])
    core.mask_strict = core.sb("mask_strict", [P, P])
    core.last_row = core.sb("last_row", [P, P])
    core.before = core.sb("before", [P, E, E])
    core.eps_ln = core.sb("eps_ln", [P, 1])
    core.eps_rms = core.sb("eps_rms", [P, 1])
    core.ln_qscale = core.sb("ln_qscale", [P, 1])
    st.pool(lambda e: e.memset(core.ones[:, :], 1.0))
    st.pool(lambda e: e.memset(core.eps_ln[:, :], LN_EPS))
    st.pool(lambda e: e.memset(core.eps_rms[:, :], RMS_EPS))
    st.pool(lambda e: e.memset(core.ln_qscale[:, :], float(np.log(DK ** -0.5))))

    def keep(dst, op, base, mult, step):
        st.pool(lambda e: e.affine_select(out=dst[:, :], in_=core.ones[:, :], compare_op=op, fill=0.0, base=base,
                                          pattern=[[step, P]], channel_multiplier=mult))
    keep(core.ident, ALU.is_equal, 0, 1, -1)
    keep(core.qk_mask, ALU.is_ge, 0, -1, 1)
    st.pool(lambda e: e.tensor_scalar(core.qk_mask[:, :], core.qk_mask[:, :], DK ** -0.5, None, ALU.mult))
    st.pool(lambda e: e.memset(core.head_ones[:, :], 0.0))
    st.pool(lambda e: e.memset(core.head_ones[0:DK, 0:DK], 1.0))
    st.pool(lambda e: e.memset(core.head_ones[DK:P, DK:P], 1.0))
    keep(core.mask_strict, ALU.is_ge, -1, -1, 1)
    st.pool(lambda e: e.tensor_scalar(core.kk_mask[:, :], core.mask_strict[:, :], -1.0, None, ALU.mult))
    st.pool(lambda e: e.memset(core.before[:, :, :], 1.0))
    st.pool(lambda e: e.affine_select(out=core.before[:, :, :], in_=core.before[:, :, :], compare_op=ALU.is_ge, fill=0.0, base=-1,
                                      pattern=[[1, E], [-1, E]], channel_multiplier=0))
    keep(core.last_row, ALU.is_ge, 1 - P, 1, 0)
    core.mask_neg = core.sb("mask_neg", [P, P], BF16)
    core.ident16 = core.sb("ident16", [P, P], BF16)
    st.pool(lambda e: e.tensor_copy(core.ident16[:, :], core.ident[:, :]))
    core.ones16 = core.sb("ones16", [P, P], BF16)
    st.pool(lambda e: e.memset(core.ones16[:, :], 1.0))
    core.mask_wide = core.sb("mask_wide", [P, P])
    core.iota = core.sb("iota", [P, WAYS + 1])
    st.pool(lambda e: e.memset(core.mask_wide[:, :], 0.0))
    st.pool(lambda e: e.affine_select(out=core.mask_wide[:, :], in_=core.mask_wide[:, :], compare_op=ALU.is_ge, fill=-SCORE_BIG, base=0,
                                      pattern=[[-1, P]], channel_multiplier=1))
    st.pool(lambda e: e.tensor_copy(core.mask_neg[:, :], core.mask_wide[:, :]))
    core.head_of = core.sb("head_of", [P, NH1])
    st.pool(lambda e: e.memset(core.head_of[:, :], HD ** -0.5))
    st.pool(lambda e: e.affine_select(out=core.head_of[:, :], in_=core.head_of[:, :], compare_op=ALU.is_ge, fill=0.0, base=0,
                                      pattern=[[-HD, NH1]], channel_multiplier=1))
    st.pool(lambda e: e.affine_select(out=core.head_of[:, :], in_=core.head_of[:, :], compare_op=ALU.is_ge, fill=0.0, base=HD - 1,
                                      pattern=[[HD, NH1]], channel_multiplier=-1))
    core.pick3 = core.sb("pick3", [3 * 2 * DS, 2 * DS], BF16)
    st.pool(lambda e: e.tensor_tensor(core.pick3[:, :], core.ident[0:96, 0:32], core.ident[0:96, 32:64], ALU.add))
    st.pool(lambda e: e.tensor_tensor(core.pick3[:, :], core.pick3[:, :], core.ident[0:96, 64:96], ALU.add))
    for i in range(WAYS + 1):
        st.pool(lambda e: e.memset(core.iota[:, i:i + 1], float(i)), chain=False)
    return (st.sems["pool"], st.count["pool"])



class DeltaLine:

    def __init__(self, sb, core, n, banks):
        self.st, self.banks = Stream(core, f"dl{n}"), banks
        self.raw = Ring([sb([P, S + 3]) for _ in range(2)])
        self.chan = sb([P, 4, S])
        self.k_pad = sb([P, 2, S])
        self.sz = sb([P, 2, S])
        self.gate = Ring([sb([P, 4, P]) for _ in range(2)])
        self.gate_dma = [Dma(core, f"dl{n}_gate{i}") for i in range(2)]
        self.decay = sb([P, 4, P])
        self.attn = sb([P, 4, P])
        self.pt = [sb([P, 4, P]) for _ in range(2)]
        self.pw = sb([P, 4, P])
        self.rhs = sb([P, 2, 4, DK])
        self.kdec = sb([P, 4, DK])
        self.wt = sb([P, 2, P])
        self.qdec = sb([P, 2, P])
        self.err = sb([P, 4, DK])
        self.state = sb([P, 2, P])
        self.h = sb([P, 2, P])
        self.sq = sb([P, 2, P])
        self.rstd = sb([P, 2, P])
        for buf in self.raw.items:
            self.st.pool(lambda e: e.memset(buf[:, 0:3], 0.0), chain=False)
        self.st.pool(lambda e: e.memset(self.k_pad[:, :, :], 0.0), chain=False)
        self.zeroed = self.st.pool(lambda e: e.memset(self.state[:, :, :], 0.0), chain=False)
        self.chan_free = self.sz_free = self.rhs_free = self.kdec_free = self.decay_free = self.qdec_free = self.pt_free = None
        self.attn_free = self.wt_free = self.err_free = self.h_free = self.sq_free = self.state_free = None
        self.k_pad_free = self.rstd_free = None


def delta_group(core, L, D, b, g):
    st, banks = D.st, D.banks
    w = core.w
    while b not in L.ready:
        yield
    ready, B = L.ready[b], L.sets[b % 2]
    hs = slice(4 * g, 4 * g + 4)
    for n, block in enumerate((NG + g, g, 2 * NG + 2 * g, 2 * NG + 2 * g + 1)):
        yield from banks.waited()
        bank, free, slot = banks.take()
        raw, raw_free, raw_slot = D.raw.take()
        t = st.pe(lambda e: e.matmul(bank[:, :], w["w_qkv"][:, block * P:(block + 1) * P], B.xn_chan[:, :],
                                     start=True, stop=True), ready, free)
        t = st.act(lambda e: e.activation(raw[:, 3:], bank[:, :], ACT.Copy), t, raw_free, D.zeroed, chain=False)
        banks.read_by(slot, t)
        yield
        cw = w["conv0"]
        t = st.dve(lambda e: e.tensor_scalar(D.chan[:, n, :], raw[:, 3:3 + S], cw[:, block, 3:4], None, ALU.mult), t, D.chan_free)
        for j in (2, 1, 0):
            t = st.dve(lambda e: e.scalar_tensor_tensor(out=D.chan[:, n, :], in0=raw[:, j:j + S], scalar=cw[:, block, j:j + 1],
                                                        in1=D.chan[:, n, :], op0=ALU.mult, op1=ALU.add))
        D.raw.read_by(raw_slot, t)
    t_conv = t
    yield from banks.waited()
    zs = []
    for p in range(2):
        yield from banks.waited()
        bank, free, slot = banks.take()
        zs.append((bank, slot, st.pe(lambda e: e.matmul(bank[:, :], w["w_z"][:, (2 * g + p) * P:(2 * g + p + 1) * P], B.xn_chan[:, :],
                                                        start=True, stop=True), free)))
    yield
    for p, (bank, slot, t) in enumerate(zs):
        t = st.act(lambda e: e.activation(D.sz[:, p, :], bank[:, :], ACT.Silu), t, D.sz_free, chain=False)
        banks.read_by(slot, t)
    t_silu = st.act(lambda e: e.activation(D.chan[:, 0:2, :], D.chan[:, 0:2, :], ACT.Silu), t_conv, chain=False)
    for u in range(2):
        rows = slice(u * DK, (u + 1) * DK)
        t_kp = st.dve(lambda e: e.tensor_copy(D.k_pad[rows, u, :], D.chan[rows, 0, :]), t_silu, D.zeroed, D.k_pad_free, chain=False)
    t_silu = st.act(lambda e: e.activation(D.chan[:, 2:4, :], D.chan[:, 2:4, :], ACT.Silu), chain=False)
    t_state = st.dve(lambda e: e.memset(D.state[0:DK, :, 0:DK], 0.0), D.state_free, D.zeroed)
    t_state = st.dve(lambda e: e.memset(D.state[DK:P, :, DK:P], 0.0))
    yield
    for c in range(CH):
        tok = slice(c * P, (c + 1) * P)
        gate, gate_free, gate_slot = D.gate.take()
        t_gate = D.gate_dma[gate_slot].start(
            gate[:, :, :], L.gate_dram[b, hs, tok].partition_broadcast(P), L.gate_stored[b], gate_free)
        yield from banks.waited()
        bank, free, slot = banks.take()
        for n in range(2):
            st.pe(lambda e: e.transpose(bank[:, n * P:(n + 1) * P], D.chan[:, 2 + n, tok], core.ident[:, :]), t_silu, free)
        t = st.pe(lambda e: e.transpose(bank[:, 2 * P:3 * P], D.chan[:, 0, tok], core.ident[:, :]))
        yield from banks.waited()
        kbank, free, kslot = banks.take()
        for u in range(2):
            t_kk = st.pe(lambda e: e.matmul(kbank[:, u * 2 * P:(u + 1) * 2 * P], D.k_pad[:, u, tok], D.chan[:, 0:2, tok],
                                            start=True, stop=True), t_kp, free)
        yield
        vsrc = bank[:, 0:2 * P].rearrange("p (j u d) -> p u j d", j=2, u=2)
        t_rv = st.act(lambda e: e.activation(D.rhs[:, 0, :, :].rearrange("p (u j) d -> p u j d", u=2), vsrc, ACT.Copy), t, D.rhs_free, chain=False)
        ktok = bank[:, 2 * P:3 * P].rearrange("p (a u d) -> p a u d", a=1, u=2).to_broadcast([P, 2, 2, DK])

        def col(a):
            return a[:, c, hs].rearrange("p (a u) -> p a u", a=2).unsqueeze(3).to_broadcast([P, 2, 2, DK])
        for s in range(4):
            h = 4 * g + s
            t = st.dve(lambda e: e.tensor_scalar(D.decay[:, s, :], gate[:, s, :], B.lnb_minus_g[:, c, h:h + 1], B.lnb[:, c, h:h + 1],
                                                 ALU.add, ALU.min), t_gate, D.decay_free, chain=False)
        t_rk = st.dve(lambda e: e.tensor_tensor(D.rhs[:, 1, :, :].rearrange("p (a u) d -> p a u d", a=2), ktok, col(B.grow), ALU.mult),
                      t_rv, D.rhs_free, chain=False)
        t_kd = st.dve(lambda e: e.tensor_tensor(D.kdec[:, :, :].rearrange("p (a u) d -> p a u d", a=2), ktok, col(B.kfall), ALU.mult),
                      D.kdec_free, chain=False)
        banks.read_by(slot, t_rv, t_kd)
        t_dec = st.act(lambda e: e.activation(D.decay[:, :, :], D.decay[:, :, :], ACT.Exp), t, chain=False)
        for u in range(2):
            rows = slice(u * DK, (u + 1) * DK)
            t_q = st.act(lambda e: e.activation(D.qdec[rows, :, :], gate[rows, :, :].rearrange("p (a u) i -> p a u i", u=2)[:, :, u, :], ACT.Exp,
                                                bias=core.ln_qscale[rows, 0:1]), t_gate, D.qdec_free, chain=False)
        D.gate.read_by(gate_slot, t, t_q)
        yield
        kk_mask = core.kk_mask[:, :].unsqueeze(1).to_broadcast([P, 4, P])
        qk_mask = core.qk_mask[:, :].unsqueeze(1).to_broadcast([P, 4, P])
        t_ms = st.pool(lambda e: e.tensor_tensor(D.pt[0][:, :, :], D.decay[:, :, :], kk_mask, ALU.mult), t_dec, D.pt_free, chain=False)
        t_mi = st.pool(lambda e: e.tensor_tensor(D.attn[:, :, :], D.decay[:, :, :], qk_mask, ALU.mult), D.attn_free, chain=False)
        D.decay_free = t_mi
        qsrc = D.chan[:, 1, tok].unsqueeze(1).to_broadcast([P, 2, P])
        t_q = st.pool(lambda e: e.tensor_tensor(D.qdec[:, :, :], D.qdec[:, :, :], qsrc, ALU.mult), t_q, chain=False)
        yield

        def products(kq):
            return kbank[:, :].rearrange("p (a u k i) -> p a u k i", a=1, u=2, k=2)[:, :, :, kq, :].to_broadcast([P, 2, 2, P])

        def by_pair(a):
            return a[:, :, :].rearrange("p (a u) i -> p a u i", u=2)
        t_pt = st.dve(lambda e: e.tensor_tensor(by_pair(D.pt[0]), products(0), by_pair(D.pt[0]), ALU.mult), t_kk, t_ms, chain=False)
        t_at = st.dve(lambda e: e.tensor_tensor(by_pair(D.attn), products(1), by_pair(D.attn), ALU.mult), t_mi, chain=False)
        banks.read_by(kslot, t_at)
        yield
        t_r = [t_rv, t_rk]
        t_pw = None
        rview = D.rhs[:, :, :, :].rearrange("p t s d -> p s t d")
        for k in range(LEVELS):
            cur, nxt = D.pt[k % 2], D.pt[(k + 1) % 2]
            if k < LEVELS - 1:
                yield from banks.waited()
                bank, free, slot = banks.take()
                for s in range(4):
                    t = st.pe(lambda e: e.transpose(bank[:, s * P:(s + 1) * P], cur[:, s, :], core.ident[:, :]), t_pt, free)
                t_pw = st.act(lambda e: e.activation(D.pw[:, :, :].rearrange("p s i -> p (s i)"), bank[:, :], ACT.Copy), t, t_pw, chain=False)
                banks.read_by(slot, t_pw)
            yield from banks.waited()
            bank, free, slot = banks.take()
            for s in range(4):
                t_ap = st.pe(lambda e: e.matmul(bank[:, s * P:(s + 1) * P], cur[:, s, :], D.rhs[:, :, s, :], start=True, stop=True),
                             t_pt, t_r, free)
            t_r = [st.dve(lambda e: e.tensor_tensor(rview, bank[:, :].rearrange("p (s t d) -> p s t d", s=4, t=2), rview, ALU.add), t_ap)]
            banks.read_by(slot, t_r)
            yield
            if k < LEVELS - 1:
                yield from banks.waited()
                bank, free, slot = banks.take()
                for s in range(4):
                    t = st.pe(lambda e: e.matmul(bank[:, s * P:(s + 1) * P], D.pw[:, s, :], cur[:, s, :], start=True, stop=True), t_pw, free)
                t_pt = st.act(lambda e: e.activation(nxt[:, :, :].rearrange("p s i -> p (s i)"), bank[:, :], ACT.Copy), t, chain=False)
                banks.read_by(slot, t_pt)
                yield
        D.pt_free = t_ap
        yield from banks.waited()
        bank, free, slot = banks.take()
        for p in range(2):
            t = st.pe(lambda e: e.transpose(bank[:, p * P:(p + 1) * P], D.rhs[:, 1, 2 * p:2 * p + 2, :].rearrange("p s d -> p (s d)"),
                                            core.ident[:, :]), t_r, free)
        t_wt = st.act(lambda e: e.activation(D.wt[:, :, :].rearrange("p a i -> p (a i)"), bank[:, 0:2 * P], ACT.Copy), t, D.wt_free, chain=False)
        banks.read_by(slot, t_wt)
        yield
        yield from banks.waited()
        bank, free, slot = banks.take()
        for p in range(2):
            t = st.pe(lambda e: e.matmul(bank[:, p * P:(p + 1) * P], D.wt[:, p, :], D.state[:, p, :], start=True, stop=True),
                      t_wt, t_state, free)
        D.wt_free = t
        t_e = st.dve(lambda e: e.tensor_tensor(D.err[:, :, :], D.rhs[:, 0, :, :], bank[:, 0:2 * P].rearrange("p (s d) -> p s d", s=4),
                                               ALU.subtract), t, D.err_free)
        D.rhs_free = [t_wt, t_e]
        banks.read_by(slot, t_e)
        yield
        yield from banks.waited()
        sbank, free, sslot = banks.take()
        for p in range(2):
            t_su = st.pe(lambda e: e.matmul(sbank[:, p * P:(p + 1) * P], D.kdec[:, 2 * p:2 * p + 2, :].rearrange("p s d -> p (s d)"),
                                            D.err[:, 2 * p:2 * p + 2, :].rearrange("p s d -> p (s d)"), start=True, stop=True),
                         t_kd, t_e, free)
        D.kdec_free = t_su
        yield from banks.waited()
        bank, free, slot = banks.take()
        for p in range(2):
            t_qs = st.pe(lambda e: e.matmul(bank[:, p * P:(p + 1) * P], D.state[:, p, :], D.qdec[:, p, :], start=(p == 0), stop=False,
                                            skip_group_check=True), t_q, free)
        for s in range(4):
            u, p = s % 2, s // 2
            t_o = st.pe(lambda e: e.matmul(bank[u * DK:(u + 1) * DK, p * P:(p + 1) * P], D.err[:, s, :], D.attn[:, s, :], start=False,
                                           stop=(s == 3), skip_group_check=True), t_at)
        D.qdec_free = D.attn_free = D.err_free = t_o
        for s in range(4):
            u, p = s % 2, s // 2
            rows = slice(u * DK, (u + 1) * DK)
            blk = D.state[rows, p, u * DK:(u + 1) * DK]
            t_state = st.dve(lambda e: e.scalar_tensor_tensor(
                out=blk, in0=blk, scalar=B.chunk_decay[rows, c, 4 * g + s:4 * g + s + 1],
                in1=sbank[rows, p * P + u * DK:p * P + (u + 1) * DK], op0=ALU.mult, op1=ALU.add), t_su, t_qs, chain=False)
        banks.read_by(sslot, t_state)
        D.state_free = t_qs
        yield
        t_h = st.dve(lambda e: e.tensor_tensor(D.h[:, :, :], bank[:, 0:2 * P].rearrange("p (a i) -> p a i", a=2), D.sz[:, :, tok], ALU.mult),
                     t_o, D.h_free)
        banks.read_by(slot, t_h)
        t = st.pool(lambda e: e.tensor_tensor(D.sq[:, :, :], D.h[:, :, :], D.h[:, :, :], ALU.mult), t_h, D.sq_free, chain=False)
        yield
        yield from banks.waited()
        bank, free, slot = banks.take()
        t = st.pe(lambda e: e.matmul(bank[:, 0:2 * P], core.head_ones[:, :], D.sq[:, :, :].rearrange("p a i -> p (a i)"), start=True, stop=True),
                  t, free)
        D.sq_free = t
        rstd = D.rstd[:, :, :].rearrange("p a i -> p (a i)")
        t = st.act(lambda e: e.activation(rstd, bank[:, 0:2 * P], ACT.Ln, bias=core.eps_rms[:, 0:1], scale=1.0 / DK), t, D.rstd_free)
        banks.read_by(slot, t)
        t = st.act(lambda e: e.activation(rstd, rstd, ACT.Exp, scale=-0.5))
        yield
        t = st.pool(lambda e: e.tensor_tensor(D.h[:, :, :], D.h[:, :, :], D.rstd[:, :, :], ALU.mult), t, chain=False)
        D.rstd_free = t
        yield
        yield from banks.waited()
        bank, free, slot = banks.take()
        for p in range(2):
            t = st.pe(lambda e: e.matmul(bank[:, 0:P], D.h[:, p, :], w["w_out"][:, 2 * g + p, :], start=(p == 0), stop=(p == 1)), t, free)
        D.h_free = t
        sdst = core.s0[:, b * CH + c, :]
        if (b, c) in L.s_done:
            t = st.dve(lambda e: e.tensor_tensor(sdst, sdst, bank[:, 0:P], ALU.add), t, L.s_done[b, c], chain=False)
        else:
            t = st.dve(lambda e: e.tensor_copy(sdst, bank[:, 0:P]), t, chain=False)
        L.s_done[b, c] = t
        banks.read_by(slot, t)
        yield
    D.chan_free, D.sz_free, D.k_pad_free = t_o, t_h, t_kk
    L.group_done[b].append([t_o, t_state])


class SequenceSet:

    def __init__(self, sb):
        self.xn_chan = sb([P, S])
        self.lnb = sb([P, CH, NVH])
        self.lnb_minus_g = sb([P, CH, NVH])
        self.grow = sb([P, CH, NVH])
        self.kfall = sb([P, CH, NVH])
        self.chunk_decay = sb([P, CH, NVH])


class Layer0:
    def __init__(self, sb, core, gate_dram, banks, nb):
        self.st, self.banks = Stream(core, "l0"), banks
        self.sets = [SequenceSet(sb) for _ in range(2)]
        self.xn_tok = sb([P, CH, H])
        self.work = (sb([P, CH, 6]), sb([P, CH, 2]), sb([P, CH]))
        self.beta_in = sb([P, CH, NVH])
        self.beta_t = sb([P, CH, NVH])
        self.beta_l = sb([P, CH, NVH])
        self.g_tok = sb([P, CH, NVH])
        self.gate_a = sb([NVH, S])
        self.gate_t = sb([NVH, S])
        self.gate_g = sb([NVH, S])
        self.gate_dram = gate_dram
        self.gate_dma = Dma(core, "gate_store")
        self.ready, self.s_done, self.gate_stored = {}, {}, {-1: None}
        self.group_done = [[] for _ in range(nb)]


def layer0_prologue(core, L, b, x_tile, x_ready):
    st, w, banks = L.st, core.w, L.banks
    while b >= 2 and len(L.group_done[b - 2]) < NG:
        yield
    B = L.sets[b % 2]
    prev = L.group_done[b - 2] if b >= 2 else None
    t = layer_norm_tok(st, x_tile, L.xn_tok, L.work, x_ready)
    yield from banks.waited()
    t_x = transpose_tiles(st, banks, L.xn_tok, B.xn_chan, None, None, t, prev)
    yield
    yield from banks.waited()
    bank, free, slot = banks.take()
    for c in range(CH):
        t = st.pe(lambda e: e.matmul(bank[:, c * NVH:(c + 1) * NVH], B.xn_chan[:, c * P:(c + 1) * P], w["w_b"][:, :],
                                     start=True, stop=True), t_x, free)

    def n2(a):
        return a[:, :, :].rearrange("p c h -> p (c h)")
    t = st.dve(lambda e: e.tensor_copy(n2(L.beta_in), bank[:, 0:CH * NVH]), t, prev)
    banks.read_by(slot, t)
    yield
    t_l = softplus_parts(st, n2(L.beta_in), n2(L.beta_t), n2(L.beta_l), t)
    st.dve(lambda e: e.tensor_scalar(n2(L.beta_in), n2(L.beta_in), 0.0, None, ALU.min))
    t_b = st.dve(lambda e: e.tensor_tensor(n2(B.lnb), n2(L.beta_in), n2(L.beta_l), ALU.subtract), t_l)
    yield
    yield from banks.waited()
    bank, free, slot = banks.take()
    t = st.pe(lambda e: e.matmul(bank[0:NVH, :], w["w_a"][:, :], B.xn_chan[:, :], start=True, stop=True), free)
    t = st.act(lambda e: e.activation(L.gate_a[:, :], bank[0:NVH, :], ACT.Identity, bias=w["dt_bias"][:, 0:1]), t)
    banks.read_by(slot, t)
    yield
    t_l = softplus_parts(st, L.gate_a[:, :], L.gate_t[:, :], L.gate_t[:, :], t)
    yield
    st.dve(lambda e: e.scalar_tensor_tensor(out=L.gate_a[:, :], in0=L.gate_a[:, :], scalar=0.0, in1=L.gate_t[:, :],
                                            op0=ALU.max, op1=ALU.add), t_l)
    st.dve(lambda e: e.tensor_scalar(L.gate_a[:, :], L.gate_a[:, :], core.neg_exp_a0[:, 0:1], None, ALU.mult), core.prep_done)
    yield
    for c in range(CH):
        tok = slice(c * P, (c + 1) * P)
        t = st.dve(lambda e: e.tensor_tensor_scan(L.gate_g[:, tok], core.ones[0:NVH, :], L.gate_a[:, tok], 0.0, ALU.mult, ALU.add),
                   L.gate_stored[b - 1], chain=(c == 0))
    L.gate_stored[b] = L.gate_dma.start(L.gate_dram[b], L.gate_g[:, :], t)
    yield
    yield from banks.waited()
    bank, free, slot = banks.take()
    for c in range(CH):
        t2 = st.pe(lambda e: e.transpose(bank[:, c * NVH:(c + 1) * NVH], L.gate_g[:, c * P:(c + 1) * P], core.ident[0:NVH, 0:NVH]), t, free)
    t = st.dve(lambda e: e.tensor_copy(n2(L.g_tok), bank[:, 0:CH * NVH]), t2)
    t_m = st.dve(lambda e: e.tensor_tensor(n2(B.lnb_minus_g), n2(B.lnb), n2(L.g_tok), ALU.subtract))
    t = st.pe(lambda e: e.matmul(bank[:, CH * NVH:2 * CH * NVH], core.last_row[:, :], n2(L.g_tok), start=True, stop=True), t)
    t = st.dve(lambda e: e.tensor_tensor(n2(B.kfall), bank[:, CH * NVH:2 * CH * NVH], n2(B.lnb_minus_g), ALU.add), t)
    t = st.act(lambda e: e.activation(n2(B.kfall), n2(B.kfall), ACT.Exp), t)
    t_c = st.act(lambda e: e.activation(n2(B.chunk_decay), bank[:, CH * NVH:2 * CH * NVH], ACT.Exp), chain=False)
    banks.read_by(slot, t_c)
    t = st.act(lambda e: e.activation(n2(B.grow), n2(L.g_tok), ACT.Exp))
    L.ready[b] = [t, t_m, t_b]
    yield



def center_weights(core, st, wt, bias, nk, sums, bank, *waits):
    t = st.dve(lambda e: e.tensor_reduce(sums[:, 0:2 * nk].rearrange("p (s k) -> p s k", s=2), wt[:, :, :, :], AX.X, ALU.add), *waits)
    t = st.dve(lambda e: e.tensor_scalar(sums[:, 0:2 * nk], sums[:, 0:2 * nk], 1.0 / F, None, ALU.mult))
    for s in range(2):
        for k in range(nk):
            t = st.dve(lambda e: e.tensor_scalar(wt[:, s, k, :], wt[:, s, k, :], sums[:, s * nk + k:s * nk + k + 1], None, ALU.subtract),
                       chain=(s + k == 0))
    t = st.pe(lambda e: e.matmul(bank[:, 0:2 * FB], core.ones[:, :], bias[:, :, :].rearrange("p s k -> p (s k)"), start=True, stop=True), t)
    t = st.dve(lambda e: e.tensor_reduce(sums[:, 0:2], bank[:, 0:2 * FB].rearrange("p (s k) -> p s k", s=2), AX.X, ALU.add), t)
    t = st.dve(lambda e: e.tensor_scalar(sums[:, 0:2], sums[:, 0:2], 1.0 / F, None, ALU.mult))
    return st.dve(lambda e: e.tensor_tensor(bias[:, :, :], bias[:, :, :], sums[:, 0:2].unsqueeze(2).to_broadcast([P, 2, FB]), ALU.subtract))


class ExpertLine:

    def __init__(self, sb, core, n, banks):
        self.st, self.banks = Stream(core, f"ex{n}"), banks
        self.h1 = sb([P, FB, S])
        self.h2 = sb([P, FB, S])
        self.sq = Ring([sb([P, S]) for _ in range(2)])
        self.rstd = sb([P, S])
        self.t1 = sb([P, 2, S])
        self.h1_free = self.h2_free = self.t1_free = None


def dense(X, nblk, nk, weight, src, src_ready, evac):
    X.out = []
    for m in range(nblk):
        yield from X.banks.waited()
        bank, free, slot = X.banks.take()
        for k in range(nk):
            t = X.st.pe(lambda e: e.matmul(bank[:, :], weight(k, m), src[:, k, :], start=(k == 0), stop=(k == nk - 1)), src_ready, free)
        t = evac(m, bank, t)
        X.banks.read_by(slot, t)
        X.out.append(t)
        if m % 2:
            yield


def centered_norm(core, X, g, b, last, func):
    st = X.st
    yield from X.banks.waited()
    bank, free, slot = X.banks.take()
    for m in range(FB):
        sq, sq_free, sq_slot = X.sq.take()
        t = st.pool(lambda e: e.tensor_tensor(sq[:, :], X.h2[:, m, :], X.h2[:, m, :], ALU.mult), last[m], sq_free)
        t = st.pe(lambda e: e.matmul(bank[:, :], core.ones[:, :], sq[:, :], start=(m == 0), stop=(m == FB - 1)), t, free)
        X.sq.read_by(sq_slot, t)
        yield
    t = st.act(lambda e: e.activation(X.rstd[:, :], bank[:, :], ACT.Ln, bias=core.eps_ln[:, 0:1], scale=1.0 / F), t)
    X.banks.read_by(slot, t)
    t = st.act(lambda e: e.activation(X.rstd[:, :], X.rstd[:, :], ACT.Exp, scale=-0.5))
    yield
    done = []
    for m in range(FB):
        t = st.dve(lambda e: e.tensor_tensor(X.h2[:, m, :], X.h2[:, m, :], X.rstd[:, :], ALU.mult), t, chain=(m == 0))
        if func is None:
            done.append(st.dve(lambda e: e.tensor_scalar(X.h2[:, m, :], X.h2[:, m, :], g[:, m:m + 1], b[:, m:m + 1], ALU.mult, ALU.add)))
        else:
            done.append(st.act(lambda e: e.activation(X.h2[:, m, :], X.h2[:, m, :], func, bias=b[:, m:m + 1], scale=g[:, m:m + 1]),
                               t, chain=(m == 0)))
    X.out = done


def expert0(core, X, M, e):
    st, w = X.st, core.w
    kind, s = e % 4, e // 4

    def gelu_into(dst, bias, free):
        return lambda m, bank, t: st.act(
            lambda en: en.activation(dst[:, m, :], bank[:, :], ACT.Gelu, bias=bias[:, m:m + 1]), t, free, chain=False)

    def biased_into(dst, bias, free):
        return lambda m, bank, t: st.act(
            lambda en: en.activation(dst[:, m, :], bank[:, :], ACT.Identity, bias=bias[:, m:m + 1]), t, free, chain=False)
    yield from dense(X, FB, 1, lambda k, m: w["up_w"][:, e, m * P:(m + 1) * P], M.nx_chan[:, :].unsqueeze(1), [M.ready, core.up_ready],
                     gelu_into(X.h1, w["up_b"][:, e, :], X.h1_free))
    t_h = X.out
    M.users.append(t_h)
    hid = X.h2
    if kind == 0:
        yield from dense(X, FB, FB, lambda k, m: w["spec0_w"][:, s, k, m * P:(m + 1) * P], X.h1, [t_h, core.spec0_ready],
                         biased_into(X.h2, w["spec0_b"][:, s, :], X.h2_free))
        X.h1_free = X.out
        yield from centered_norm(core, X, w["ln0_g"][:, s, :], w["ln0_b"][:, s, :], X.out, ACT.Gelu)
        t_h = X.out
    elif kind == 1:
        yield from dense(X, 2, FB, lambda k, m: w["spec1a_w"][:, s, k, m * P:(m + 1) * P], X.h1, [t_h, core.spec1a_ready],
                         gelu_into(X.t1, w["spec1a_b"][:, s, :], X.t1_free))
        X.h1_free = X.out
        yield from dense(X, FB, 2, lambda k, m: w["spec1b_w"][:, s, k, m * P:(m + 1) * P], X.t1, [X.out, core.spec1b_ready],
                         biased_into(X.h2, w["spec1b_b"][:, s, :], X.h2_free))
        X.t1_free = X.out
        yield from centered_norm(core, X, w["ln1_g"][:, s, :], w["ln1_b"][:, s, :], X.out, None)
        t_h = X.out
    elif kind == 2:
        yield from dense(X, FB, FB, lambda k, m: w["spec2_w"][:, s, k, m * P:(m + 1) * P], X.h1, [t_h, core.spec2_ready],
                         gelu_into(X.h2, w["spec2_b"][:, s, :], X.h2_free))
        X.h1_free = t_h = X.out
    else:
        hid = X.h1
    yield
    yield from X.banks.waited()
    bank, free, slot = X.banks.take()
    for c in range(CH):
        for k in range(FB):
            t = st.pe(lambda en: en.matmul(bank[:, c * P:(c + 1) * P], hid[:, k, c * P:(c + 1) * P], w["down_w"][:, e, k, :],
                                           start=(k == 0), stop=(k == FB - 1)), t_h, core.down_ready, free)
        if c % 2:
            yield
    if kind == 3:
        X.h1_free = t
    else:
        X.h2_free = t
    for c in range(CH):
        M.acc_done[c] = st.dve(lambda en: en.scalar_tensor_tensor(
            out=M.acc[:, c, :], in0=bank[:, c * P:(c + 1) * P], scalar=M.weight[:, c, e:e + 1], in1=M.acc[:, c, :],
            op0=ALU.mult, op1=ALU.add), t, M.acc_done[c], chain=False)
    X.banks.read_by(slot, M.acc_done[CH - 1])
    M.experts_done += 1


class Mixture0:

    def __init__(self, sb, core, n, banks):
        self.st, self.banks = Stream(core, f"mix{n}"), banks
        self.xn_tok = sb([P, CH, H])
        self.nx_tok = sb([P, CH, H])
        self.nx_chan = sb([P, S])
        self.acc = sb([P, CH, H])
        self.work = (sb([P, CH, 6]), sb([P, CH, 2]), sb([P, CH]))
        self.logit = sb([P, CH, E])
        self.cmp = sb([P, CH * E, E])
        self.eq = sb([P, CH * E, E])
        self.pick = sb([P, CH, E])
        self.weight = sb([P, CH, E])
        self.red = sb([P, CH])
        self.wt = sb([E, S])
        self.users, self.experts_done, self.started = [], 0, -1


def mixture0_start(core, M, b, x_tile):
    st, w, banks = M.st, core.w, M.banks
    users, M.users, M.experts_done = M.users, [], 0
    t = layer_norm_tok(st, x_tile, M.xn_tok, M.work)
    yield
    t = layer_norm_tok(st, M.xn_tok, M.nx_tok, M.work)
    yield
    yield from banks.waited()
    t_x = transpose_tiles(st, banks, M.nx_tok, M.nx_chan, w["f_ln_g"][:, 0:1], w["f_ln_b"][:, 0:1], t, users, core.small_ready)
    yield
    yield from banks.waited()
    bank, free, slot = banks.take()
    for c in range(CH):
        t = st.pe(lambda e: e.matmul(bank[:, c * E:(c + 1) * E], M.nx_chan[:, c * P:(c + 1) * P], w["router_w"][:, :], start=True, stop=True),
                  t_x, free)
    lg = M.logit[:, :, :].rearrange("p c e -> p (c e)")
    t = st.dve(lambda e: e.tensor_copy(lg, bank[:, 0:CH * E]), t)
    banks.read_by(slot, t)
    yield
    mine = lg.unsqueeze(2).to_broadcast([P, CH * E, E])
    for c in range(CH):
        others = M.logit[:, c, :].unsqueeze(1).to_broadcast([P, E, E])
        rows = slice(c * E, (c + 1) * E)
        st.dve(lambda e: e.tensor_tensor(M.cmp[:, rows, :], others, mine[:, rows, :], ALU.is_gt), chain=(c == 0))
        st.dve(lambda e: e.tensor_tensor(M.eq[:, rows, :], others, mine[:, rows, :], ALU.is_equal), chain=False)
        st.dve(lambda e: e.tensor_tensor(M.eq[:, rows, :], M.eq[:, rows, :], core.before[:, :, :], ALU.mult))
        yield
    st.dve(lambda e: e.tensor_tensor(M.cmp[:, :, :], M.cmp[:, :, :], M.eq[:, :, :], ALU.add))
    pk = M.pick[:, :, :].rearrange("p c e -> p (c e)")
    st.dve(lambda e: e.tensor_reduce(pk, M.cmp[:, :, :], AX.X, ALU.add))
    st.dve(lambda e: e.tensor_scalar(pk, pk, 2.0, None, ALU.is_lt))
    yield
    st.dve(lambda e: e.tensor_reduce(M.red[:, :], M.logit[:, :, :], AX.X, ALU.max))
    t = st.dve(lambda e: e.tensor_tensor(M.weight[:, :, :], M.logit[:, :, :], M.red[:, :].unsqueeze(2).to_broadcast([P, CH, E]), ALU.subtract))
    t = st.act(lambda e: e.activation(M.weight[:, :, :], M.weight[:, :, :], ACT.Exp), t)
    yield
    st.dve(lambda e: e.tensor_tensor(M.weight[:, :, :], M.weight[:, :, :], M.pick[:, :, :], ALU.mult), t)
    st.dve(lambda e: e.tensor_reduce(M.red[:, :], M.weight[:, :, :], AX.X, ALU.add))
    st.dve(lambda e: e.reciprocal(M.red[:, :], M.red[:, :]))
    t_w = st.dve(lambda e: e.tensor_tensor(M.weight[:, :, :], M.weight[:, :, :], M.red[:, :].unsqueeze(2).to_broadcast([P, CH, E]), ALU.mult))
    yield
    yield from banks.waited()
    bank, free, slot = banks.take()
    for c in range(CH):
        t = st.pe(lambda e: e.transpose(bank[0:E, c * P:(c + 1) * P], M.weight[:, c, :], core.ident[:, :]), t_w, free)
    t = st.act(lambda e: e.activation(M.wt[:, :], bank[0:E, :], ACT.Copy), t)
    for c in range(CH):
        t = st.pe(lambda e: e.matmul(bank[:, c * P:(c + 1) * P], M.wt[:, c * P:(c + 1) * P], w["down_b"][:, :], start=True, stop=True), t)
    t = st.dve(lambda e: e.tensor_tensor(M.acc[:, :, :].rearrange("p c h -> p (c h)"), bank[:, :],
                                         M.xn_tok[:, :, :].rearrange("p c h -> p (c h)"), ALU.add), t)
    banks.read_by(slot, t)
    M.acc_done = [t] * CH
    M.ready = [t_x, t]
    M.started = b


def mixture0_end(core, M, b, x_tile):
    st = M.st
    while M.experts_done < E:
        yield

    def n2(a):
        return a.rearrange("p c h -> p (c h)")
    t = st.act(lambda e: e.activation(n2(M.acc[:, :, :]), n2(M.acc[:, :, :]), ACT.Silu), M.acc_done)
    yield
    t = st.dve(lambda e: e.tensor_tensor(n2(M.acc[:, :, :]), n2(M.acc[:, :, :]), n2(core.s0[:, b * CH:(b + 1) * CH, :]), ALU.mult), t)
    st.dve(lambda e: e.tensor_tensor(n2(x_tile), n2(x_tile), n2(M.acc[:, :, :]), ALU.add))



class Attention:

    def __init__(self, sb, core, score_banks, banks):
        self.st, self.banks = Stream(core, "attn"), banks
        self.lines = [Stream(core, f"attn{a}") for a in range(4)]
        self.scores = score_banks
        self.x_chan = Ring([sb([P, S]) for _ in range(2)])
        self.q = sb([P, S])
        self.k = Ring([sb([P, S]) for _ in range(2)])
        self.q_head = Ring([sb([P, NH1, P]) for _ in range(2)])
        self.v = [sb([P, CH, NH1, 32]) for _ in range(2)]
        self.p = [sb([P, S]) for _ in range(4)]
        self.pt = [sb([P, CH, P]) for _ in range(4)]
        self.mx = [sb([P, 1]) for _ in range(4)]
        self.o_raw = sb([P, 4 * P])
        self.o = sb([P, NH1, HD])
        self.rden = sb([P, NH1])
        self.o_chan = Ring([sb([P, S]) for _ in range(2)])
        for v in self.v:
            self.ones_set = self.st.pool(lambda e: e.memset(v[:, :, :, :], 1.0))
        self.scores_free, self.p_free, self.pt_free = [None] * 4, [None] * 4, [None] * 4
        self.v_free, self.o_ready = [None] * 2, [None] * 4
        self.q_free = None
        self.projected, self.finished = {}, {}


def attention_inputs(core, A, b):
    st, w, banks = A.st, core.w, A.banks
    xh = core.xhat_chan[:, b * S:(b + 1) * S]
    x_chan, x_free, x_slot = A.x_chan.take()
    t_x = st.act(lambda e: e.activation(x_chan[:, :], xh, ACT.Identity, scale=w["pre_w"][:, 0:1], bias=w["pre_b"][:, 0:1]), core.xhat_ready[b], x_free)
    yield
    yield from banks.waited()
    k, k_free, k_slot = A.k.take()
    qk_ready = []
    for name, dst, dst_free in (("q", A.q, A.q_free), ("k", k, k_free)):
        bank, free, slot = banks.take()
        t = st.pe(lambda e: e.matmul(bank[:, :], w[name + "_w"][:, :], x_chan[:, :], start=True, stop=True), t_x, free)
        t = st.act(lambda e: e.activation(dst[:, :], bank[:, :], ACT.Identity, bias=w[name + "_b"][:, 0:1]), t, dst_free, chain=False)
        banks.read_by(slot, t)
        qk_ready.append(t)
    v = A.v[b % 2]
    yield
    yield from banks.waited()
    bank, free, slot = banks.take()
    for c in range(CH):
        t_xv = st.pe(lambda e: e.matmul(bank[:, c * P:(c + 1) * P], x_chan[:, c * P:(c + 1) * P], w["v_w"][:, :], start=True, stop=True), free)
    for c in range(CH):
        t_v = st.dve(lambda e: e.tensor_tensor(v[:, c, :, 0:HD], bank[:, c * P:(c + 1) * P].rearrange("p (h d) -> p h d", h=NH1),
                                               w["v_b"][:, :].rearrange("p (h d) -> p h d", h=NH1), ALU.add), t_xv, A.ones_set,
                     A.v_free[b % 2], chain=False)
    banks.read_by(slot, t_v)
    A.projected[b] = (x_chan, x_slot, t_x, t_xv, k, k_slot, qk_ready, t_v)
    yield


def attention_heads(core, A, b, i, a, q_head, t_q, obank, ofree):
    st, banks = A.lines[a], A.banks
    k, v = A.projected[b][4], A.v[b % 2]
    qk_ready, t_v = A.projected[b][6:8]
    sc, p, pt, mx = A.scores[a], A.p[a], A.pt[a], A.mx[a]
    nk, rows = (i + 1) * P, slice(32 * a, 32 * a + 32)
    for g in range(4):
        h = 4 * g + a
        st.pe(lambda e: e.matmul(sc[:, 0:nk], q_head[:, h, :], k[:, 0:nk], start=True, stop=False, skip_group_check=True),
              t_q[g], qk_ready, A.scores_free[a])
        t = st.pe(lambda e: e.matmul(sc[:, i * P:nk], core.ident16[:, :], core.mask_neg[:, :], start=False, stop=True, skip_group_check=True))
        yield
        t = st.dve(lambda e: e.tensor_reduce(mx[:, :], sc[:, 0:nk], AX.X, ALU.max, negate=True), t, A.scores_free[a])
        yield
        t_p = st.act(lambda e: e.activation(p[:, 0:nk], sc[:, 0:nk], ACT.Exp, bias=mx[:, 0:1]), t, A.p_free[a], chain=False)
        A.scores_free[a] = t_p
        yield
        yield from banks.waited()
        bank, free, slot = banks.take()
        for kt in range(i + 1):
            t = st.pe(lambda e: e.transpose(bank[:, kt * P:(kt + 1) * P], p[:, kt * P:(kt + 1) * P], core.ident[:, :]), t_p, free)
        dst = pt[:, 0:i + 1, :].rearrange("p k q -> p (k q)")
        if g % 2:
            t_pt = st.dve(lambda e: e.tensor_copy(dst, bank[:, 0:nk]), t, A.pt_free[a], chain=False)
        else:
            t_pt = st.act(lambda e: e.activation(dst, bank[:, 0:nk], ACT.Copy), t, A.pt_free[a], chain=False)
        banks.read_by(slot, t_pt)
        A.p_free[a] = t
        yield
        for kt in range(i + 1):
            t_o = st.pe(lambda e: e.matmul(obank[rows, g * P:(g + 1) * P], v[:, kt, h, :], pt[:, kt, :], start=(kt == 0),
                                           stop=(kt == i), skip_group_check=True), t_pt, t_v, ofree)
        A.pt_free[a] = t_o
        yield
    A.o_ready[a] = t_o


def attention(core, A, nb):
    st, banks = A.st, A.banks
    t_raw_read = None

    def heads_of(i):
        q_head, q_free, q_slot = A.q_head.take()
        t_q = [st.pool(lambda e: e.tensor_tensor(q_head[:, 4 * g:4 * g + 4, :], A.q[:, i * P:(i + 1) * P].unsqueeze(1).to_broadcast([P, 4, P]),
                                                 core.head_of[:, 4 * g:4 * g + 4].unsqueeze(2).to_broadcast([P, 4, P]), ALU.mult),
                       A.projected[b][6], q_free, chain=False) for g in range(4)]
        if i == CH - 1:
            A.q_free = t_q[3]
        return q_head, t_q, q_slot
    b = 0
    yield from attention_inputs(core, A, b)
    coming = heads_of(0)
    for b in range(nb):
        o_chan, o_free, o_slot = A.o_chan.take()
        for i in range(CH):
            yield from banks.waited()
            obank, ofree, oslot = banks.take()
            q_head, t_q, q_slot = coming
            lines = [attention_heads(core, A, b, i, a, q_head, t_q, obank, ofree) for a in range(4)]
            if i < CH - 1:
                coming = heads_of(i + 1)
            while lines:
                for line in list(lines):
                    if next(line, "end") == "end":
                        lines.remove(line)
                    else:
                        yield
            A.q_head.read_by(q_slot, A.o_ready)
            t = st.act(lambda e: e.activation(A.o_raw[:, :], obank[:, :], ACT.Copy), A.o_ready, t_raw_read)
            yield
            for g in range(4):
                t_raw_read = st.pe(lambda e: e.transpose(obank[:, g * P:(g + 1) * P], A.o_raw[:, g * P:(g + 1) * P], core.ident[:, :]), t)
            yield
            ov = obank[:, :].rearrange("p (h d) -> p h d", h=NH1)
            t = st.dve(lambda e: e.reciprocal(A.rden[:, :], ov[:, :, HD]), t_raw_read)
            t = st.dve(lambda e: e.tensor_tensor(A.o[:, :, :], ov[:, :, 0:HD], A.rden[:, :].unsqueeze(2).to_broadcast([P, NH1, HD]), ALU.mult))
            yield
            t = st.pe(lambda e: e.transpose(obank[:, 0:P], A.o[:, :, :].rearrange("p h d -> p (h d)"), core.ident[:, :]), t)
            t = st.act(lambda e: e.activation(o_chan[:, i * P:(i + 1) * P], obank[:, 0:P], ACT.Copy), t, o_free)
            banks.read_by(oslot, t)
            yield
        A.v_free[b % 2] = list(A.o_ready)
        A.k.read_by(A.projected[b][5], *A.o_ready)
        A.finished[b] = (o_chan, o_slot, t)
        if b + 1 < nb:
            b += 1
            yield from attention_inputs(core, A, b)
            coming = heads_of(0)


class StateSpace:
    def __init__(self, sb, core, banks):
        self.st, self.banks = Stream(core, "ssm"), banks
        self.raw = Ring([sb([P, S + 3]) for _ in range(2)])
        for buf in self.raw.items:
            self.zeroed = self.st.pool(lambda e: e.memset(buf[:, 0:3], 0.0))
        self.xc = sb([P, DB, S])
        self.sz = sb([P, DB, S])
        self.dt_in = sb([DTR, S])
        self.bc = sb([6 * DS, S])
        self.bc3 = sb([6 * DS, S], BF16)
        self.dt = sb([P, DB, S])
        self.tmp = sb([P, DB, S])
        self.dtx = sb([P, DB, S])
        self.da = Ring([sb([P, S]) for _ in range(4)])
        self.h = Ring([sb([P, S]) for _ in range(4)])
        self.y = sb([P, DB, S])
        self.y_free = None
        self.finished = {}


def state_space(core, A, Z, b):
    st, w, banks = Z.st, core.w, Z.banks
    while b not in A.projected:
        yield
    x_chan, x_slot, t_x, t_xv = A.projected[b][0:4]
    for m in range(2 * DB):
        yield from banks.waited()
        bank, free, slot = banks.take()
        t = st.pe(lambda e: e.matmul(bank[:, :], w["in_proj_w"][:, m * P:(m + 1) * P], x_chan[:, :], start=True, stop=True), t_x, free)
        if m == 2 * DB - 1:
            A.x_chan.read_by(x_slot, t, t_xv)
        if m >= DB:
            t = st.act(lambda e: e.activation(Z.sz[:, m - DB, :], bank[:, :], ACT.Silu), t, chain=False)
            banks.read_by(slot, t)
            continue
        raw, raw_free, raw_slot = Z.raw.take()
        t = st.act(lambda e: e.activation(raw[:, 3:], bank[:, :], ACT.Copy), t, raw_free, Z.zeroed)
        banks.read_by(slot, t)
        cw, xc = w["conv1"], Z.xc[:, m, :]
        t = st.dve(lambda e: e.tensor_scalar(xc, raw[:, 3:3 + S], cw[:, m, 3:4], w["conv1_b"][:, m:m + 1], ALU.mult, ALU.add), t)
        yield
        for j in (2, 1, 0):
            t = st.dve(lambda e: e.scalar_tensor_tensor(out=xc, in0=raw[:, j:j + S], scalar=cw[:, m, j:j + 1], in1=xc, op0=ALU.mult, op1=ALU.add))
        Z.raw.read_by(raw_slot, t)
        t_c = st.act(lambda e: e.activation(xc, xc, ACT.Silu), t)
        yield
    yield from banks.waited()
    bank, free, slot = banks.take()
    for k in range(DB):
        t = st.pe(lambda e: e.matmul(bank[0:DTR, :], w["dt_in_w"][:, k, :], Z.xc[:, k, :], start=(k == 0), stop=(k == DB - 1)), t_c, free)
    t_di = st.act(lambda e: e.activation(Z.dt_in[:, :], bank[0:DTR, :], ACT.Copy), t)
    banks.read_by(slot, t_di)
    bank, free, slot = banks.take()
    for k in range(DB):
        t = st.pe(lambda e: e.matmul(bank[0:6 * DS, :], w["bc3_w"][:, k, :], Z.xc[:, k, :], start=(k == 0), stop=(k == DB - 1)), free)
    t = st.act(lambda e: e.activation(Z.bc[:, :], bank[0:6 * DS, :], ACT.Copy), t)
    banks.read_by(slot, t)
    yield
    t = st.dve(lambda e: e.tensor_copy(Z.bc3[:, :], Z.bc[:, :]), t)
    for k in (1, 2):
        for r in range(32 * k, 96, 32):
            rows = slice(r, r + 32)
            t = st.dve(lambda e: e.tensor_tensor(Z.bc[rows, :], Z.bc[rows, :], Z.bc3[rows, :], ALU.subtract))
        for r in range(32 * k, 96, 32):
            rows = slice(r, r + 32)
            t_bc = st.dve(lambda e: e.tensor_copy(Z.bc3[rows, :], Z.bc[rows, :]))
    yield
    for m in range(DB):
        yield from banks.waited()
        bank, free, slot = banks.take()
        t = st.pe(lambda e: e.matmul(bank[:, :], w["dt_w"][:, m * P:(m + 1) * P], Z.dt_in[:, :], start=True, stop=True), t_di, free)
        t = st.act(lambda e: e.activation(Z.dt[:, m, :], bank[:, :], ACT.Identity, bias=w["dt_b"][:, m:m + 1]), t)
        banks.read_by(slot, t)
        t = softplus_parts(st, Z.dt[:, m, :], Z.tmp[:, m, :], Z.tmp[:, m, :], t)
        t_dt = st.dve(lambda e: e.scalar_tensor_tensor(out=Z.dt[:, m, :], in0=Z.dt[:, m, :], scalar=0.0, in1=Z.tmp[:, m, :], op0=ALU.max, op1=ALU.add), t)
        t_dtx = st.dve(lambda e: e.tensor_tensor(Z.dtx[:, m, :], Z.dt[:, m, :], Z.xc[:, m, :], ALU.mult))
        yield
    t_y = []
    for m in range(DB):
        t_y.append(st.pool(lambda e: e.tensor_scalar(Z.y[:, m, :], Z.xc[:, m, :], w["d_param"][:, m:m + 1], None, ALU.mult), Z.y_free, t_c))

    def row(r):
        bank, free, slot = banks.take()
        t = st.pe(lambda e: e.matmul(bank[:, :], core.pick3[:, r:r + 1].to_broadcast([6 * DS, P]), Z.bc3[:, :], start=True, stop=True),
                  t_bc, free)
        return bank, slot, t

    def decays(n):
        out = []
        for m in range(DB):
            da, da_free, da_slot = Z.da.take()
            t = st.act(lambda e: e.activation(da[:, :], Z.dt[:, m, :], ACT.Exp, scale=core.neg_a1[:, m, n:n + 1]), t_dt, da_free, chain=False)
            out.append((da, da_slot, t))
        return out

    def drives(bank, slot, t_b):
        out = []
        for m in range(DB):
            h, h_free, h_slot = Z.h.take()
            t = st.dve(lambda e: e.tensor_tensor(h[:, :], bank[:, :], Z.dtx[:, m, :], ALU.mult), t_b, h_free, t_dtx, chain=False)
            out.append((h, h_slot, t))
        banks.read_by(slot, t)
        return out
    yield from banks.waited()
    b_row, da = row(0), decays(0)
    yield
    drive = drives(*b_row)
    for n in range(DS):
        yield from banks.waited()
        c_bank, c_slot, t_c = row(DS + n)
        t_h = []
        for m in range(DB):
            (a, a_slot, t_a), (h, h_slot, t) = da[m], drive[m]
            t_h.append(st.dve(lambda e: e.tensor_tensor_scan(h[:, :], a[:, :], h[:, :], 0.0, ALU.mult, ALU.add), t_a, t, chain=False))
            Z.da.read_by(a_slot, t_h[m])
        states = drive
        yield
        if n + 1 < DS:
            yield from banks.waited()
            b_row, da = row(n + 1), decays(n + 1)
        for m in range(DB):
            h, h_slot, _ = states[m]
            t_m = st.dve(lambda e: e.tensor_tensor(h[:, :], c_bank[:, :], h[:, :], ALU.mult), t_c, t_h[m], chain=False)
            t_y[m] = st.pool(lambda e: e.tensor_tensor(Z.y[:, m, :], Z.y[:, m, :], h[:, :], ALU.add), t_m, t_y[m], chain=False)
            Z.h.read_by(h_slot, t_y[m])
        banks.read_by(c_slot, t_m)
        yield
        if n + 1 < DS:
            drive = drives(*b_row)
    t = t_y
    for m in range(DB):
        t = st.dve(lambda e: e.tensor_tensor(Z.y[:, m, :], Z.y[:, m, :], Z.sz[:, m, :], ALU.mult), t)
    Z.finished[b] = t


class Tail:

    def __init__(self, sb, core, banks):
        self.st, self.banks = Stream(core, "tail"), banks
        self.x2 = sb([P, CH, H])
        self.n_tok = sb([P, CH, H])
        self.n_chan = sb([P, S])
        self.hid = sb([P, FB, S])
        self.work = (sb([P, CH, 6]), sb([P, CH, 2]), sb([P, CH]))


def tail(core, A, Z, T, b):
    st, w, banks = T.st, core.w, T.banks
    while b not in A.finished or b not in Z.finished:
        yield
    o_chan, o_slot, t_a = A.finished[b]
    yield from banks.waited()
    bank, free, slot = banks.take()
    for c in range(CH):
        tok = slice(c * P, (c + 1) * P)
        t_o = st.pe(lambda e: e.matmul(bank[:, tok], o_chan[:, tok], w["o_w"][:, :], start=True, stop=False), t_a, free)
        for k in range(DB):
            t = st.pe(lambda e: e.matmul(bank[:, tok], Z.y[:, k, tok], w["ssm_out_w"][:, k, :], start=False, stop=(k == DB - 1)), Z.finished[b])
    A.o_chan.read_by(o_slot, t_o)
    Z.y_free = t
    xb = core.xn1[:, b * CH:(b + 1) * CH, :]

    def bias(name):
        return w[name][:, :].unsqueeze(1).to_broadcast([P, CH, H])
    bview = bank[:, :].rearrange("p (c h) -> p c h", c=CH)
    yield
    t = st.dve(lambda e: e.tensor_tensor(T.x2[:, :, :], bview, xb, ALU.add), t)
    banks.read_by(slot, t)
    t = st.dve(lambda e: e.tensor_tensor(T.x2[:, :, :], T.x2[:, :, :], bias("o_b"), ALU.add))
    yield
    t = layer_norm_tok(st, T.x2, T.n_tok, T.work)
    yield
    yield from banks.waited()
    t_n = transpose_tiles(st, banks, T.n_tok, T.n_chan, w["mid_w"][:, 0:1], w["mid_b"][:, 0:1], t)
    yield
    for m in range(FB):
        yield from banks.waited()
        bank, free, slot = banks.take()
        t = st.pe(lambda e: e.matmul(bank[:, :], w["ffn_w1"][:, m * P:(m + 1) * P], T.n_chan[:, :], start=True, stop=True), t_n, free)
        t_h = st.act(lambda e: e.activation(T.hid[:, m, :], bank[:, :], ACT.Gelu, bias=w["ffn_b1"][:, m:m + 1]), t, chain=False)
        banks.read_by(slot, t_h)
        yield
    st.dve(lambda e: e.tensor_tensor(T.x2[:, :, :], T.x2[:, :, :], bias("ffn_b2"), ALU.add))
    yield from banks.waited()
    bank, free, slot = banks.take()
    for c in range(CH):
        tok = slice(c * P, (c + 1) * P)
        for m in range(FB):
            t = st.pe(lambda e: e.matmul(bank[:, tok], T.hid[:, m, tok], w["ffn_w2"][:, m, :], start=(m == 0), stop=(m == FB - 1)), t_h, free)
    bview2 = bank[:, :].rearrange("p (c h) -> p c h", c=CH)
    yield
    t = st.dve(lambda e: e.tensor_tensor(core.s1[:, b * CH:(b + 1) * CH, :], bview2, T.x2[:, :, :], ALU.add), t,
               A.projected[b][2])
    banks.read_by(slot, t)
    yield



class Selection:
    def __init__(self, sb, core, nt, banks):
        self.st, self.banks, self.nt = Stream(core, "sel"), banks, nt
        self.avail = sb([P, nt])
        self.masked = sb([P, nt])
        self.above = sb([P, WAYS - 1, nt], BF16)
        self.count = sb([P, WAYS - 1])
        self.range = sb([P, 2])
        self.step = sb([P, ROUNDS + 1])
        self.low = sb([P, 1])
        self.high = sb([P, 1])
        self.th = sb([P, WAYS - 1])
        self.kinds = sb([P, 2, nt])
        self.rank = sb([P, 2, nt])
        self.total = sb([P, 1])
        self.picks = sb([P, E, nt])
        self.excl = sb([P, E, nt + 1])
        self.pos = sb([P, E, nt])
        self.slot_f = sb([P, nt])


def prefix_ranks(core, G, src, n, out, total, *waits):
    st, nt = G.st, G.nt
    bank, free, slot = G.banks.take()
    cols = src.rearrange("p n t -> p (n t)")
    t = st.pe(lambda e: e.matmul(bank[:, 0:n * nt], core.ones[:, :], cols, start=True, stop=True), *waits, free)
    for k in range(n):
        t = st.dve(lambda e: e.tensor_tensor_scan(G.excl[:, k, 1:nt + 1], core.ones[:, 0:nt], bank[:, k * nt:(k + 1) * nt], 0.0, ALU.mult, ALU.add), t)
    if total is not None:
        st.dve(lambda e: e.tensor_copy(total, G.excl[:, 0, nt:nt + 1]))
    t = st.pe(lambda e: e.matmul(bank[:, 0:n * nt], core.mask_strict[:, :], cols, start=True, stop=True), t)
    t = st.dve(lambda e: e.tensor_tensor(out, bank[:, 0:n * nt].rearrange("p (n t) -> p n t", n=n), G.excl[:, 0:n, 0:nt], ALU.add), t)
    G.banks.read_by(slot, t)
    return t


def selection(core, G, scores, cap):
    st, nt, banks = G.st, G.nt, G.banks
    st.dve(lambda e: e.memset(G.avail[:, :], 1.0))
    st.dve(lambda e: e.memset(G.excl[:, :, :], 0.0))
    flat_scores = scores[:, :, :].rearrange("p e t -> p (e t)")
    st.dve(lambda e: e.tensor_reduce(G.range[:, 0:1], flat_scores, AX.X, ALU.max), core.xhat_ready)
    st.dve(lambda e: e.tensor_reduce(G.range[:, 1:2], flat_scores, AX.X, ALU.min, negate=True))
    t = st.dve(lambda e: e.tensor_reduce(G.low[:, :], G.range[:, :], AX.X, ALU.max))
    t = st.pool(lambda e: e.partition_all_reduce(G.high[:, :], G.low[:, :], P, bass.bass_isa.ReduceOp.max), t)
    t = st.dve(lambda e: e.tensor_scalar(G.range[:, 1:2], G.high[:, :], 1.001, 1e-30, ALU.mult, ALU.add), t)
    for r in range(ROUNDS):
        st.dve(lambda e: e.tensor_scalar(G.step[:, r:r + 1], G.range[:, 1:2], 2.0 / WAYS ** (r + 1), None, ALU.mult), chain=(r == 0))
    yield
    for x in range(E - 1):
        st.dve(lambda e: e.tensor_scalar(G.kinds[:, 0, :], G.avail[:, :], 1.0, SCORE_BIG, ALU.subtract, ALU.mult))
        st.dve(lambda e: e.tensor_tensor(G.masked[:, :], scores[:, x, :], G.avail[:, :], ALU.mult))
        t_s = st.dve(lambda e: e.tensor_tensor(G.masked[:, :], G.masked[:, :], G.kinds[:, 0, :], ALU.add))
        t_l = st.dve(lambda e: e.tensor_scalar(G.low[:, :], G.range[:, 1:2], -1.0, None, ALU.mult))
        for r in range(ROUNDS):
            step = G.step[:, r:r + 1]
            t = st.dve(lambda e: e.tensor_scalar(G.th[:, :], core.iota[:, 1:WAYS], step, G.low[:, 0:1], ALU.mult, ALU.add))
            t = st.dve(lambda e: e.tensor_tensor(G.above[:, :, :], G.masked[:, :].unsqueeze(1).to_broadcast([P, WAYS - 1, nt]),
                                                  G.th[:, :].unsqueeze(2).to_broadcast([P, WAYS - 1, nt]), ALU.is_ge))
            yield
            yield from banks.waited()
            bank, free, slot = banks.take()
            n = (WAYS - 1) * nt
            t = st.pe(lambda e: e.matmul(bank[:, 0:n], core.ones16[:, :], G.above[:, :, :].rearrange("p w t -> p (w t)"), start=True, stop=True), t, free)
            yield
            t = st.dve(lambda e: e.tensor_reduce(G.count[:, :], bank[:, 0:n].rearrange("p (w t) -> p w t", w=WAYS - 1), AX.X, ALU.add), t)
            banks.read_by(slot, t)
            yield
            st.dve(lambda e: e.tensor_scalar(G.count[:, :], G.count[:, :], float(cap), None, ALU.is_ge))
            st.dve(lambda e: e.tensor_reduce(G.total[:, :], G.count[:, :], AX.X, ALU.add))
            t_l = st.dve(lambda e: e.tensor_scalar(G.low[:, :], G.total[:, :], step, G.low[:, 0:1], ALU.mult, ALU.add))
            yield
        st.dve(lambda e: e.tensor_tensor(G.high[:, :], G.low[:, :], G.step[:, ROUNDS - 1:ROUNDS], ALU.add))
        st.dve(lambda e: e.tensor_scalar(G.kinds[:, 1, :], G.masked[:, :], G.low[:, 0:1], None, ALU.is_gt))
        st.dve(lambda e: e.scalar_tensor_tensor(out=G.kinds[:, 0, :], in0=G.masked[:, :], scalar=G.high[:, 0:1], in1=G.kinds[:, 1, :],
                                                op0=ALU.is_ge, op1=ALU.mult))
        t = st.dve(lambda e: e.scalar_tensor_tensor(out=G.kinds[:, 1, :], in0=G.masked[:, :], scalar=G.low[:, 0:1], in1=G.kinds[:, 0, :],
                                                    op0=ALU.is_ge, op1=ALU.subtract))
        yield
        yield from banks.waited()
        prefix_ranks(core, G, G.kinds[:, :, :], 2, G.rank[:, :, :], G.total[:, :], t)
        st.dve(lambda e: e.tensor_scalar(G.rank[:, 1, :], G.rank[:, 1, :], G.total[:, 0:1], None, ALU.add))
        st.dve(lambda e: e.scalar_tensor_tensor(out=G.rank[:, :, :], in0=G.rank[:, :, :], scalar=float(cap), in1=G.kinds[:, :, :],
                                                op0=ALU.is_lt, op1=ALU.mult))
        st.dve(lambda e: e.tensor_tensor(G.picks[:, x, :], G.rank[:, 0, :], G.rank[:, 1, :], ALU.add))
        st.dve(lambda e: e.tensor_tensor(G.avail[:, :], G.avail[:, :], G.picks[:, x, :], ALU.subtract))
        yield
    t = st.dve(lambda e: e.tensor_copy(G.picks[:, E - 1, :], G.avail[:, :]))
    yield from banks.waited()
    prefix_ranks(core, G, G.picks[:, :, :], E, G.pos[:, :, :], None, t)
    for x in range(E):
        st.dve(lambda e: e.tensor_scalar(G.pos[:, x, :], G.pos[:, x, :], float(x * cap), None, ALU.add), chain=(x == 0))
    st.dve(lambda e: e.tensor_tensor(G.pos[:, :, :], G.pos[:, :, :], G.picks[:, :, :], ALU.mult))
    st.dve(lambda e: e.tensor_reduce(G.slot_f[:, :], G.pos[:, :, :].rearrange("p e t -> p t e"), AX.X, ALU.add))
    G.done = st.dve(lambda e: e.tensor_copy(core.slot_i[:, :], G.slot_f[:, :]))


class Expert1:
    def __init__(self, sb, core, n, ct, banks):
        self.st, self.banks = Stream(core, f"bx{n}"), banks
        self.tok = sb([P, ct, H])
        self.n_tok = sb([P, ct, H])
        self.n_chan = sb([P, ct * P])
        self.hid = sb([P, FB, ct * P])
        self.out = sb([P, ct, H])
        self.work = (sb([P, ct, 6]), sb([P, ct, 2]), sb([P, ct]))
        self.load, self.store = Dma(core, f"bx{n}_load"), Dma(core, f"bx{n}_store")
        self.tok_free = self.stored = None


def expert1(core, X, routed, answered, x, ct, scattered):
    st, w, banks = X.st, core.w, X.banks
    rows = routed[x * ct * P:(x + 1) * ct * P, :].rearrange("(c p) h -> p c h", p=P)
    t = X.load.start(X.tok[:, :, :], rows, scattered, X.tok_free)
    t = layer_norm_tok(st, X.tok, X.n_tok, X.work, t, n=ct)
    X.tok_free = t
    t_n = transpose_tiles(st, banks, X.n_tok, X.n_chan, w["m_ln_g"][:, 0:1], w["m_ln_b"][:, 0:1], t, n=ct)
    yield
    for m in range(FB):
        bank, free, slot = banks.take()
        t = st.pe(lambda e: e.matmul(bank[:, 0:ct * P], w["m_w1"][:, x, m * P:(m + 1) * P], X.n_chan[:, :], start=True, stop=True), t_n, free)
        t_h = st.act(lambda e: e.activation(X.hid[:, m, :], bank[:, 0:ct * P], ACT.Gelu_apprx_tanh, bias=w["m_b1"][:, x, m:m + 1]), t,
                     chain=(m == 0))
        banks.read_by(slot, t_h)
    yield
    bank, free, slot = banks.take()
    for c in range(ct):
        for m in range(FB):
            t = st.pe(lambda e: e.matmul(bank[:, c * P:(c + 1) * P], X.hid[:, m, c * P:(c + 1) * P], w["m_w2"][:, x, m, :],
                                         start=(m == 0), stop=(m == FB - 1)), t_h, free)
    t = st.dve(lambda e: e.tensor_tensor(X.out[:, :, :], bank[:, 0:ct * P].rearrange("p (c h) -> p c h", c=ct),
                                         w["m_b2"][:, x, :].unsqueeze(1).to_broadcast([P, ct, H]), ALU.add), t, X.stored)
    banks.read_by(slot, t)
    rows_out = answered[x * ct * P:(x + 1) * ct * P, :].rearrange("(c p) h -> p c h", p=P)
    X.stored = X.store.start(rows_out, X.out[:, :, :], t)
    yield



def layer1_weights(core, ins, dma):
    w, nc = core.w, core.nc

    def weight(name, shape):
        w[name] = core.sb(name, shape)
        dma.start(w[name][tuple(slice(None) for _ in shape)], ins[name])

    def row(name, n):
        w[name] = core.sb(name, [P, n])
        dma.start(w[name][:, :], ins[name].partition_broadcast(P))
    for name in ("pre_w", "pre_b", "mid_w", "mid_b", "m_ln_g", "m_ln_b"):
        weight(name, [P, 1])
    weight("centroids", [P, E])
    weight("q_w", [P, H])
    weight("q_b", [P, 1])
    weight("k_w", [P, H])
    weight("k_b", [P, 1])
    weight("v_w", [P, H])
    row("v_b", H)
    weight("o_w", [P, H])
    row("o_b", H)
    row("mix", H)
    weight("ssm_out_w", [P, DB, H])
    weight("in_proj_w", [P, 2 * DI])
    weight("conv1", [P, DB, 4])
    weight("conv1_b", [P, DB])
    weight("dt_in_w", [P, DB, DTR])
    weight("bc3_w", [P, DB, 6 * DS])
    weight("dt_w", [DTR, DI])
    weight("dt_b", [P, DB])
    weight("a_log1", [P, DB, DS])
    weight("d_param", [P, DB])
    weight("ffn_w1", [P, FF])
    weight("ffn_b1", [P, FB])
    weight("ffn_w2", [P, FB, H])
    row("ffn_b2", H)
    loaded = (dma.sem, dma.count)
    st = Stream(core, "prep1")
    core.neg_a1 = core.sb("neg_a1", [P, DB, DS])
    t = st.act(lambda e: e.activation(core.neg_a1[:, :, :], w["a_log1"][:, :, :], ACT.Exp), loaded)
    st.dve(lambda e: e.tensor_scalar(core.neg_a1[:, :, :], core.neg_a1[:, :, :], -1.0, None, ALU.mult), t)
    t = st.act(lambda e: e.activation(w["mix"][:, :], w["mix"][:, :], ACT.Exp, scale=-1.0), chain=False)
    st.dve(lambda e: e.tensor_scalar(w["mix"][:, :], w["mix"][:, :], 1.0, None, ALU.add), t)
    st.dve(lambda e: e.reciprocal(w["mix"][:, :], w["mix"][:, :]))
    st.dve(lambda e: e.tensor_tensor(w["o_w"][:, :], w["o_w"][:, :], w["mix"][:, :], ALU.mult))
    st.dve(lambda e: e.tensor_tensor(w["o_b"][:, :], w["o_b"][:, :], w["mix"][:, :], ALU.mult))
    st.dve(lambda e: e.tensor_scalar(w["mix"][:, :], w["mix"][:, :], -1.0, 1.0, ALU.mult, ALU.add))
    st.dve(lambda e: e.tensor_tensor(w["ssm_out_w"][:, :, :], w["ssm_out_w"][:, :, :],
                                     w["mix"][:, :].unsqueeze(1).to_broadcast([P, DB, H]), ALU.mult))
    return loaded


def layer1_norms(core, T, x_tok, nb, scores, banks):
    w, st = core.w, T
    core.xhat_ready = []
    for b in range(nb):
        rows = slice(b * CH, (b + 1) * CH)
        xhat = core.xhat_chan[:, b * S:(b + 1) * S]
        t = layer_norm_tok(st, x_tok[:, rows, :], core.xn1[:, rows, :], core.ln_work1)
        t = layer_norm_tok(st, core.xn1[:, rows, :], core.n_tok1, core.ln_work1)
        t = transpose_tiles(st, banks, core.n_tok1, xhat, None, None, t)
        core.xhat_ready.append(t)
        t = st.dve(lambda e: e.tensor_scalar(core.n_chan1[:, :], xhat, w["m_ln_g"][:, 0:1], w["m_ln_b"][:, 0:1], ALU.mult, ALU.add), t)
        bank, free, slot = banks.take()
        for c in range(CH):
            t = st.pe(lambda e: e.matmul(bank[:, c * E:(c + 1) * E], core.n_chan1[:, c * P:(c + 1) * P], w["centroids"][:, :],
                                         start=True, stop=True), t, free)
        t = st.dve(lambda e: e.tensor_copy(scores[:, :, rows], bank[:, 0:CH * E].rearrange("p (c e) -> p e c", c=CH)), t)
        banks.read_by(slot, t)


def layer1(core, ctx, ins, outs, x_tok, psum, bank, dram, nb, dbg):
    nc, w, nt = core.nc, core.w, nb * CH
    names = iter(range(1000))

    def sb(shape, dtype=F32):
        return core.sb(f"l1_{next(names)}", shape, dtype)
    core.xn1 = sb([P, nt, H])
    core.s1 = sb([P, nt, H])
    core.xhat_chan = core.s1[:, :, :].rearrange("p n h -> p (n h)")
    core.slot_i = core.sb("slot_i", [P, nt], I32)
    scores = sb([P, E, nt])
    with ExitStack() as inner:
        core.ctx = inner
        dma = Dma(core, "weights1")
        layer1_weights(core, ins, dma)
        core.ln_work1 = (sb([P, CH, 6]), sb([P, CH, 2]), sb([P, CH]))
        ring = Ring(bank[4:8])
        A = Attention(sb, core, bank[0:4], ring)
        Z = StateSpace(sb, core, ring)
        T = Tail(sb, core, ring)
        core.n_tok1, core.n_chan1 = T.n_tok, T.n_chan
        G = Selection(sb, core, nt, ring)
        core.fence()
        layer1_norms(core, Stream(core, "norm1"), x_tok, nb, scores, Ring(bank[0:4]))
        core.fence()

        def every(line):
            for b in range(nb):
                yield from line(b)
        interleave([paced(attention(core, A, nb), ATTENTION_STEPS), every(lambda b: state_space(core, A, Z, b)), every(lambda b: tail(core, A, Z, T, b)),
                    selection(core, G, scores, nb * S // E)])
        core.fence()
    with ExitStack() as inner:
        core.ctx = inner
        ct = nt // E
        dma = Dma(core, "weights2")

        def weight(name, shape):
            w[name] = core.sb(name, shape)
            return dma.start(w[name][tuple(slice(None) for _ in shape)], ins[name])
        weight("m_w1", [P, E, F])
        weight("m_b1", [P, E, FB])
        weight("m_w2", [P, E, FB, H])
        w["m_b2"] = core.sb("m_b2", [P, E, H])
        t_w = dma.start(w["m_b2"][:, :, :], ins["m_b2"].partition_broadcast(P))
        weight("m_g", [P, 1])
        t_w = weight("m_b", [P, 1])
        w["m_ln_g"], w["m_ln_b"] = w["m_g"], w["m_b"]
        hg = sb([P, nt, H])
        X = [Expert1(sb, core, n, ct, Ring(bank[4 * n:4 * n + 4])) for n in range(2)]
        move = Dma(core, "route")
        for n in range(nt):
            nc.gpsimd.indirect_dma_start(out=dram["routed"], out_offset=bass.IndirectOffsetOnAxis(ap=core.slot_i[:, n:n + 1], axis=0),
                                         in_=core.xn1[:, n, :], in_offset=None).then_inc(move.sem, 16)
            move.count += 16
        scattered = (move.sem, move.count)

        def line(n):
            for x in range(n, E, 2):
                yield from expert1(core, X[n], dram["routed"], dram["answered"], x, ct, [scattered, t_w])
        interleave([line(0), line(1)])
        core.wait("pool", nc.gpsimd, [X[0].stored, X[1].stored])
        for n in range(nt):
            nc.gpsimd.indirect_dma_start(out=hg[:, n, :], out_offset=None, in_=dram["answered"],
                                         in_offset=bass.IndirectOffsetOnAxis(ap=core.slot_i[:, n:n + 1], axis=0)).then_inc(move.sem, 16)
            move.count += 16
        st = Stream(core, "final")
        store = Dma(core, "store_out")
        for b in range(nb):
            rows = slice(b * CH, (b + 1) * CH)

            def n2(a):
                return a[:, rows, :].rearrange("p c h -> p (c h)")
            t = st.dve(lambda e: e.tensor_tensor(n2(hg), n2(hg), n2(core.xn1), ALU.add), (move.sem, move.count), chain=False)
            t = st.act(lambda e: e.activation(n2(hg), n2(hg), ACT.Silu), t, chain=False)
            t = st.dve(lambda e: e.tensor_tensor(n2(core.s1), n2(core.s1), n2(hg), ALU.mult), t, chain=False) if dbg not in ("s1", "g1") else t
            t = st.dve(lambda e: e.tensor_tensor(n2(x_tok), n2(x_tok), n2(core.s1), ALU.add), t)
            src = {"s1": core.s1, "g1": hg}.get(dbg, x_tok)
            t = store.start(outs["out"][b].rearrange("(c p) h -> p c h", p=P), src[:, rows, :], t)
        core.fence()


def every_weight(core, ins, names_shapes, dma):
    for name, shape in names_shapes:
        core.w[name] = core.sb(name, shape)
        t = dma.start(core.w[name][tuple(slice(None) for _ in shape)], ins[name])
    return t


def layer0_delta(core, ins, x_tok, x_ready, gate_dram, bank, nb, const_done):
    w = core.w
    names = iter(range(1000))

    def sb(shape, dtype=F32):
        return core.sb(f"d_{next(names)}", shape, dtype)
    t_w = every_weight(core, ins, [("w_qkv", [P, 4 * NKH * DK]), ("w_z", [P, NVH * DK]), ("w_a", [P, NVH]), ("w_b", [P, NVH]),
                                   ("dt_bias", [NVH, 1]), ("a_log", [NVH, 1]), ("conv0", [P, 16, 4]), ("w_out", [P, 2 * NG, H]),
                                   ("norm_w", [P, 1])], Dma(core, "weights0"))
    prep = Stream(core, "prep")
    core.neg_exp_a0 = core.sb("neg_exp_a0", [NVH, 1])
    t = prep.act(lambda e: e.activation(core.neg_exp_a0[:, :], w["a_log"][:, :], ACT.Exp), t_w, const_done)
    prep.dve(lambda e: e.tensor_scalar(core.neg_exp_a0[:, :], core.neg_exp_a0[:, :], -1.0, None, ALU.mult), t)
    core.prep_done = prep.dve(lambda e: e.tensor_scalar(w["w_out"][:, :, :], w["w_out"][:, :, :], w["norm_w"][:, 0:1], None, ALU.mult))
    ring = Ring(bank)
    L = Layer0(sb, core, gate_dram, ring, nb)
    D = [DeltaLine(sb, core, n, ring) for n in range(DELTA_LINES)]
    core.fence()
    units = [(b, g) for b in range(nb) for g in range(NG)]

    def prologues():
        for b in range(nb):
            yield from layer0_prologue(core, L, b, x_tok[:, b * CH:(b + 1) * CH, :], x_ready[b])

    def line(n):
        for _ in range(n * 14):
            yield
        while units:
            b, g = units.pop(0)
            yield from delta_group(core, L, D[n], b, g)
    interleave([prologues(), *[line(n) for n in range(DELTA_LINES)]])


def layer0_mixture(core, ins, x_tok, bank, nb):
    w = core.w
    names = iter(range(1000))

    def sb(shape, dtype=F32):
        return core.sb(f"m_{next(names)}", shape, dtype)
    core.small_ready = every_weight(core, ins, [("router_w", [P, E]), ("f_ln_g", [P, 1]), ("f_ln_b", [P, 1]), ("down_b", [E, H]),
                                                ("up_b", [P, E, FB]), ("spec1a_b", [P, 2, FB // 2]),
                                                *[(name, [P, 2, FB]) for name in ("spec0_b", "ln0_g", "ln0_b", "spec1b_b", "ln1_g", "ln1_b", "spec2_b")]],
                                    Dma(core, "small_weights"))
    core.up_ready = every_weight(core, ins, [("up_w", [P, E, F])], Dma(core, "up_w_load"))
    spec0 = every_weight(core, ins, [("spec0_w", [P, 2, FB, F])], Dma(core, "spec0_w_load"))
    core.spec1a_ready = every_weight(core, ins, [("spec1a_w", [P, 2, FB, F // 2])], Dma(core, "spec1a_w_load"))
    spec1b = every_weight(core, ins, [("spec1b_w", [P, 2, FB // 2, F])], Dma(core, "spec1b_w_load"))
    core.down_ready = every_weight(core, ins, [("down_w", [P, E, FB, H])], Dma(core, "down_w_load"))
    core.spec2_ready = every_weight(core, ins, [("spec2_w", [P, 2, FB, F])], Dma(core, "spec2_w_load"))
    ring = Ring(bank)
    prep = Stream(core, "prep0")
    sums = sb([P, 2 * FB])
    core.spec0_ready = center_weights(core, prep, w["spec0_w"], w["spec0_b"], FB, sums, bank[0], spec0, core.small_ready)
    core.spec1b_ready = center_weights(core, prep, w["spec1b_w"], w["spec1b_b"], 2, sums, bank[0], spec1b)
    for readers in ring.readers:
        readers.append(core.spec1b_ready)
    M = [Mixture0(sb, core, n, ring) for n in range(2)]
    X = [ExpertLine(sb, core, n, ring) for n in range(2)]
    units = [(b, e) for b in range(nb) for e in range(E)]

    def sequences(n):
        for b in range(n, nb, 2):
            x_tile = x_tok[:, b * CH:(b + 1) * CH, :]
            yield from mixture0_start(core, M[n], b, x_tile)
            yield from mixture0_end(core, M[n], b, x_tile)

    def line(n):
        while units:
            b, e = units.pop(0)
            while M[b % 2].started < b:
                yield
            yield from expert0(core, X[n], M[b % 2], e)
    interleave([sequences(0), sequences(1), line(0), line(1)])


def build(nc, ins, outs, nb, dbg=None):
    with ExitStack() as ctx:
        core = Core(nc, ctx)
        const_done = build_constants(core)
        nt = nb * CH
        core.w = {}
        x_tok = core.sb("x_tok", [P, nt, H])
        psum = ctx.enter_context(nc.psum_tensor("psum", [P, 8, 512], F32))
        bank = [psum[:, i, :] for i in range(8)]
        x_dma = [Dma(core, f"x{b}") for b in range(nb)]
        x_ready = [x_dma[b].start(x_tok[:, b * CH:(b + 1) * CH, :], ins["x"][b].rearrange("(c p) h -> p c h", p=P)) for b in range(nb)]
        gate_dram = nc.dram_tensor("gate_scratch", [nb, NVH, S], F32).ap()
        dram = {"routed": nc.dram_tensor("routed", [nt * P, H], F32).ap(),
                "answered": nc.dram_tensor("answered", [nt * P, H], F32).ap()}
        with ExitStack() as layer0_ctx:
            core.ctx = layer0_ctx
            core.s0 = core.sb("s0", [P, nt, H])
            for part in (lambda: layer0_delta(core, ins, x_tok, x_ready, gate_dram, bank, nb, const_done),
                         lambda: layer0_mixture(core, ins, x_tok, bank, nb)):
                with ExitStack() as inner:
                    core.ctx = inner
                    part()
                    core.fence()
                if dbg == "s":
                    x_tok = core.s0
                    break
        if dbg in ("x1", "g0", "s"):
            core.fence()
            d = Dma(core, "dbg")
            for b in range(nb):
                t2 = d.start(outs["out"][b].rearrange("(c p) h -> p c h", p=P), x_tok[:, b * CH:(b + 1) * CH, :])
            core.wait("sp", nc.sync, [t2])
            return
        with ExitStack() as layer1_ctx:
            core.ctx = layer1_ctx
            layer1(core, layer1_ctx, ins, outs, x_tok, psum, bank, dram, nb, dbg)


def host_layout(x):
    a = {}
    heads = np.array(SLOT_HEADS)
    a["x"] = x["L0_attn_hidden_states"]
    a["w_qkv"] = x["L0_attn_W_qkv"].T
    a["w_z"] = x["L0_attn_W_z"].reshape(NVH, DK, H)[heads].reshape(NVH * DK, H).T
    a["w_a"] = x["L0_attn_W_a"][heads].T
    a["w_b"] = x["L0_attn_W_b"][heads].T
    a["dt_bias"] = x["L0_attn_dt_bias"][heads].reshape(NVH, 1)
    a["a_log"] = x["L0_attn_A_log"][heads].reshape(NVH, 1)
    a["conv0"] = x["L0_attn_conv_w"].reshape(16, P, 4).transpose(1, 0, 2)
    a["w_out"] = x["L0_attn_W_out"].reshape(H, NVH, DK)[:, heads].reshape(H, 2 * NG, P).transpose(2, 1, 0)
    a["norm_w"] = np.concatenate([x["L0_attn_norm_weight"]] * 2).reshape(P, 1)
    f = {k[7:]: v for k, v in x.items() if k.startswith("L0_ffn_")}
    a["up_w"] = f["up_W"].transpose(1, 0, 2)
    a["up_b"] = f["up_b"].reshape(E, FB, P).transpose(2, 0, 1)
    a["down_w"] = f["down_W"].reshape(E, FB, P, H).transpose(2, 0, 1, 3)
    a["down_b"] = f["down_b"]
    a["router_w"] = f["router_w"]
    a["f_ln_g"] = f["ln_g"].reshape(P, 1)
    a["f_ln_b"] = f["ln_b"].reshape(P, 1)
    for name in ("spec0_W", "spec1a_W", "spec1b_W", "spec2_W"):
        s, k, n = f[name].shape
        a[name.replace("W", "w")] = f[name].reshape(s, k // P, P, n).transpose(2, 0, 1, 3)
    for name in ("spec0_b", "ln0_g", "ln0_b", "spec1a_b", "spec1b_b", "ln1_g", "ln1_b", "spec2_b"):
        a[name] = f[name].reshape(2, -1, P).transpose(2, 0, 1)
    f = {k[8:]: v for k, v in x.items() if k.startswith("L1_attn_")}
    for name, source in (("pre_w", "ln1_w"), ("pre_b", "ln1_b"), ("mid_w", "ln2_w"), ("mid_b", "ln2_b")):
        a[name] = f[source].reshape(P, 1)
    for name in ("q_b", "k_b"):
        a[name] = f[name].reshape(P, 1)
    for name in ("q_w", "k_w", "v_w", "v_b", "o_w", "o_b", "in_proj_w", "dt_w", "ffn_w1", "ffn_b2"):
        a[name] = f[name]
    a["mix"] = f["mix_weight"]
    a["ssm_out_w"] = f["ssm_out_w"].reshape(DB, P, H).transpose(1, 0, 2)
    a["conv1"] = f["conv_w"].reshape(DB, P, 4).transpose(1, 0, 2)
    a["conv1_b"] = f["conv_b"].reshape(DB, P).T
    xp = f["x_proj_w"].reshape(DB, P, DTR + 2 * DS).transpose(1, 0, 2)
    a["dt_in_w"] = xp[:, :, :DTR]
    a["bc3_w"] = np.concatenate([xp[:, :, DTR:]] * 3, axis=2)
    a["dt_b"] = f["dt_b"].reshape(DB, P).T
    a["a_log1"] = f["A_log"].reshape(DB, P, DS).transpose(1, 0, 2)
    a["d_param"] = f["D_param"].reshape(DB, P).T
    a["ffn_b1"] = f["ffn_b1"].reshape(FB, P).T
    a["ffn_w2"] = f["ffn_w2"].reshape(FB, P, H).transpose(1, 0, 2)
    f = {k[7:]: v for k, v in x.items() if k.startswith("L1_ffn_")}
    a["centroids"] = f["centroids"].T
    a["m_ln_g"] = a["m_g"] = f["ln_g"].reshape(P, 1)
    a["m_ln_b"] = a["m_b"] = f["ln_b"].reshape(P, 1)
    a["m_w1"] = f["w1"].transpose(1, 0, 2)
    a["m_b1"] = f["b1"].reshape(E, FB, P).transpose(2, 0, 1)
    a["m_w2"] = f["w2"].reshape(E, FB, P, H).transpose(2, 0, 1, 3)
    a["m_b2"] = f["b2"]
    return {k: np.ascontiguousarray(v) for k, v in a.items()}


def kernel(**inputs):
    import concourse.bacc as bacc
    from concourse.bass_utils import run_bass_kernel_spmd

    arrays = {f"in_{k}": v for k, v in host_layout({k: np.asarray(v) for k, v in inputs.items()}).items()}
    nb = arrays["in_x"].shape[0]
    nc = bacc.Bacc("TRN2", target_bir_lowering=False, num_devices=1)
    ins = {k[3:]: nc.dram_tensor(k, v.shape, F32, kind="ExternalInput").ap() for k, v in arrays.items()}
    outs = {"out": nc.dram_tensor("out", [nb, S, H], F32, kind="ExternalOutput").ap()}
    build(nc, ins, outs, nb)
    return run_bass_kernel_spmd(nc, [arrays], core_ids=[0]).results[0]["out"]
```
